# Optimizing a Trainium2 kernel written in Bass

```python
import numpy as np
import jax
import jax.numpy as jnp

def _softmax(x, axis=-1):
    return jax.nn.softmax(x, axis=axis)

def _gelu(x):
    return jax.nn.gelu(x, approximate=True)

def _silu(x):
    return jax.nn.silu(x)

def _sigmoid(x):
    return jax.nn.sigmoid(x)

def _layernorm(x, axis=-1, eps=1e-05):
    m = jnp.mean(x, axis=axis, keepdims=True)
    v = jnp.var(x, axis=axis, keepdims=True)
    return (x - m) / jnp.sqrt(v + eps)

def _scatter_add(tgt, idx, src, axis=0):
    return tgt.at[idx].add(src)

def _segment_sum(src, seg, n):
    return jax.ops.segment_sum(src, seg, n)
kernel_name = 'mk_gnn_ffn_d1_gnn_r32_936020'

def setup_inputs(seed: int=0):
    np.random.seed(seed)
    _w = jnp.asarray

    def _rec_inputs():
        import jax
        import jax.numpy as jnp
        _gk = jax.random.key(seed)
        x = -0.0002117 + 1 * jax.random.normal(jax.random.fold_in(_gk, 1), (3125, 256), jnp.float32)
        _s = jax.random.randint(jax.random.fold_in(_gk, 2), (25000,), 0, 3125, jnp.int32)
        _d = jax.random.randint(jax.random.fold_in(_gk, 3), (25000,), 0, 3125, jnp.int32)
        _loop = jnp.arange(3125, dtype=jnp.int32)
        src = jnp.concatenate([_s, _d, _loop])
        dst = jnp.concatenate([_d, _s, _loop])
        _o = jnp.argsort(dst, stable=True)
        src = src[_o]
        dst = dst[_o]
        edge_weight = jax.random.uniform(jax.random.fold_in(_gk, 12), (53125,), jnp.float32, 0.0, 1)
        return (x, src, dst, edge_weight)
    x, src, dst, edge_weight = _rec_inputs()

    def _L0_gnn_setup():
        import jax, jax.numpy as jnp
        import numpy as np
        N_NODES = 3125
        N_EDGES = 100000
        IN_C = 256
        OUT_C = 256
        key = jax.random.key(seed)
        k1, k2, k3, k4, k5 = jax.random.split(key, 5)
        limit = float(np.sqrt(6.0 / (IN_C + OUT_C)))
        W = jax.random.uniform(k2, (IN_C, OUT_C), jnp.float32, -limit, limit)
        return {'x': jax.random.normal(k1, (N_NODES, IN_C), jnp.float32), 'W': W, 'bias': jnp.zeros((OUT_C,), jnp.float32), 'edge_row': jax.random.randint(k3, (N_EDGES,), 0, N_NODES, jnp.int32), 'edge_col': jax.random.randint(k4, (N_EDGES,), 0, N_NODES, jnp.int32), 'edge_val': jax.random.uniform(k5, (N_EDGES,), jnp.float32)}
    _L0_gnn_all = _L0_gnn_setup()
    _L0_gnn_in = {k: v for k, v in _L0_gnn_all.items() if k in ('W', 'bias')}
    del _L0_gnn_all

    def _L0_ffn_setup():
        import jax, jax.numpy as jnp
        import numpy as np
        B, N, D = (16, 128, 256)
        NUM_EXPERTS, TOP_K, HEADS = (4, 2, 4)
        N_EDGES = 32768
        LN_EPS = 1e-05

        def _layernorm(x, g, b):
            mu = x.mean(-1, keepdims=True)
            var = ((x - mu) ** 2).mean(-1, keepdims=True)
            return (x - mu) * jax.lax.rsqrt(var + LN_EPS) * g + b

        def _forward(x, edge_index, W_gat, att_src, att_dst, b_gat, ln_gamma, ln_beta, W1, b1, W2, b2):
            Bc, Nc, Dc = x.shape
            M = Bc * Nc
            x_flat = x.reshape(M, Dc)
            h = (x_flat @ W_gat).reshape(M, HEADS, NUM_EXPERTS)
            loops = jnp.arange(M, dtype=edge_index.dtype)
            src = jnp.concatenate([edge_index[0], loops])
            dst = jnp.concatenate([edge_index[1], loops])
            a_src = (h * att_src).sum(-1)
            a_dst = (h * att_dst).sum(-1)
            e = jax.nn.leaky_relu(a_src[src] + a_dst[dst], negative_slope=0.2)
            e_max = jax.ops.segment_max(e, dst, num_segments=M)
            ee = jnp.exp(e - e_max[dst])
            denom = jax.ops.segment_sum(ee, dst, num_segments=M)
            alpha = ee / (denom[dst] + 1e-16)
            msg = h[src] * alpha[:, :, None]
            agg = jax.ops.segment_sum(msg, dst, num_segments=M).reshape(M, HEADS * NUM_EXPERTS) + b_gat
            scores = _layernorm(agg, ln_gamma, ln_beta).reshape(M, HEADS, NUM_EXPERTS).mean(1)
            scores = scores.reshape(Bc, Nc, NUM_EXPERTS)
            topk_s, topk_i = jax.lax.top_k(scores, TOP_K)
            w = jax.nn.softmax(topk_s, axis=-1)
            out = jnp.zeros_like(x)
            for ei in range(NUM_EXPERTS):
                g = jnp.where(topk_i == ei, w, 0.0).sum(-1)
                hh = jax.nn.gelu(x @ W1[ei] + b1[ei], approximate=False)
                out = out + g[..., None] * (hh @ W2[ei] + b2[ei])
            return out
        key = jax.random.key(seed)
        ks = jax.random.split(key, 8)
        s = 0.05
        return {'x': jax.random.normal(ks[0], (B, N, D), jnp.float32), 'W_gat': jax.random.normal(ks[1], (D, HEADS * NUM_EXPERTS), jnp.float32) * s, 'att_src': jax.random.normal(ks[2], (HEADS, NUM_EXPERTS), jnp.float32) * s, 'att_dst': jax.random.normal(ks[3], (HEADS, NUM_EXPERTS), jnp.float32) * s, 'b_gat': jnp.zeros((HEADS * NUM_EXPERTS,), jnp.float32), 'ln_gamma': jnp.ones((HEADS * NUM_EXPERTS,), jnp.float32), 'ln_beta': jnp.zeros((HEADS * NUM_EXPERTS,), jnp.float32), 'W1': jax.random.normal(ks[4], (NUM_EXPERTS, D, 2 * D), jnp.float32) * s, 'b1': jnp.zeros((NUM_EXPERTS, 2 * D), jnp.float32), 'W2': jax.random.normal(ks[5], (NUM_EXPERTS, 2 * D, D), jnp.float32) * s, 'b2': jnp.zeros((NUM_EXPERTS, D), jnp.float32), 'edge_index': jax.random.randint(ks[6], (2, N_EDGES), 0, B * N, jnp.int32)}
    _L0_ffn_all = _L0_ffn_setup()
    _L0_ffn_in = {k: v for k, v in _L0_ffn_all.items() if k in ('W_gat', 'att_src', 'att_dst', 'b_gat', 'ln_gamma', 'ln_beta', 'W1', 'b1', 'W2', 'b2', 'edge_index')}
    del _L0_ffn_all
    return {'x': x, 'src': src, 'dst': dst, 'edge_weight': edge_weight, 'L0_gnn_W': _L0_gnn_in['W'], 'L0_gnn_bias': _L0_gnn_in['bias'], 'L0_ffn_W_gat': _L0_ffn_in['W_gat'], 'L0_ffn_att_src': _L0_ffn_in['att_src'], 'L0_ffn_att_dst': _L0_ffn_in['att_dst'], 'L0_ffn_b_gat': _L0_ffn_in['b_gat'], 'L0_ffn_ln_gamma': _L0_ffn_in['ln_gamma'], 'L0_ffn_ln_beta': _L0_ffn_in['ln_beta'], 'L0_ffn_W1': _L0_ffn_in['W1'], 'L0_ffn_b1': _L0_ffn_in['b1'], 'L0_ffn_W2': _L0_ffn_in['W2'], 'L0_ffn_b2': _L0_ffn_in['b2'], 'L0_ffn_edge_index': _L0_ffn_in['edge_index']}

def reference(x, src, dst, edge_weight, L0_gnn_W, L0_gnn_bias, L0_ffn_W_gat, L0_ffn_att_src, L0_ffn_att_dst, L0_ffn_b_gat, L0_ffn_ln_gamma, L0_ffn_ln_beta, L0_ffn_W1, L0_ffn_b1, L0_ffn_W2, L0_ffn_b2, L0_ffn_edge_index):
    import jax
    import jax.numpy as jnp

    def _L0_gnn_ref(x, W, bias, edge_row, edge_col, edge_val):
        import jax, jax.numpy as jnp
        import numpy as np
        N_NODES = 3125
        N_EDGES = 100000
        IN_C = 256
        OUT_C = 256
        h = x @ W
        msgs = h[edge_col] * edge_val[:, None]
        agg = jax.ops.segment_sum(msgs, edge_row, num_segments=N_NODES)
        return agg + bias

    def _L0_ffn_ref(x, W_gat, att_src, att_dst, b_gat, ln_gamma, ln_beta, W1, b1, W2, b2, edge_index):
        import jax, jax.numpy as jnp
        import numpy as np
        B, N, D = (16, 128, 256)
        NUM_EXPERTS, TOP_K, HEADS = (4, 2, 4)
        N_EDGES = 32768
        LN_EPS = 1e-05

        def _layernorm(x, g, b):
            mu = x.mean(-1, keepdims=True)
            var = ((x - mu) ** 2).mean(-1, keepdims=True)
            return (x - mu) * jax.lax.rsqrt(var + LN_EPS) * g + b

        def _forward(x, edge_index, W_gat, att_src, att_dst, b_gat, ln_gamma, ln_beta, W1, b1, W2, b2):
            Bc, Nc, Dc = x.shape
            M = Bc * Nc
            x_flat = x.reshape(M, Dc)
            h = (x_flat @ W_gat).reshape(M, HEADS, NUM_EXPERTS)
            loops = jnp.arange(M, dtype=edge_index.dtype)
            src = jnp.concatenate([edge_index[0], loops])
            dst = jnp.concatenate([edge_index[1], loops])
            a_src = (h * att_src).sum(-1)
            a_dst = (h * att_dst).sum(-1)
            e = jax.nn.leaky_relu(a_src[src] + a_dst[dst], negative_slope=0.2)
            e_max = jax.ops.segment_max(e, dst, num_segments=M)
            ee = jnp.exp(e - e_max[dst])
            denom = jax.ops.segment_sum(ee, dst, num_segments=M)
            alpha = ee / (denom[dst] + 1e-16)
            msg = h[src] * alpha[:, :, None]
            agg = jax.ops.segment_sum(msg, dst, num_segments=M).reshape(M, HEADS * NUM_EXPERTS) + b_gat
            scores = _layernorm(agg, ln_gamma, ln_beta).reshape(M, HEADS, NUM_EXPERTS).mean(1)
            scores = scores.reshape(Bc, Nc, NUM_EXPERTS)
            topk_s, topk_i = jax.lax.top_k(scores, TOP_K)
            w = jax.nn.softmax(topk_s, axis=-1)
            out = jnp.zeros_like(x)
            for ei in range(NUM_EXPERTS):
                g = jnp.where(topk_i == ei, w, 0.0).sum(-1)
                hh = jax.nn.gelu(x @ W1[ei] + b1[ei], approximate=False)
                out = out + g[..., None] * (hh @ W2[ei] + b2[ei])
            return out
        return _forward(x, edge_index, W_gat, att_src, att_dst, b_gat, ln_gamma, ln_beta, W1, b1, W2, b2)
    x = x + _L0_gnn_ref(_layernorm(x, axis=-1), L0_gnn_W, L0_gnn_bias, src, dst, edge_weight)
    x = x + _L0_ffn_ref(_layernorm(x, axis=-1)[None], L0_ffn_W_gat, L0_ffn_att_src, L0_ffn_att_dst, L0_ffn_b_gat, L0_ffn_ln_gamma, L0_ffn_ln_beta, L0_ffn_W1, L0_ffn_b1, L0_ffn_W2, L0_ffn_b2, L0_ffn_edge_index)[0]
    return x

_drawn_inputs = setup_inputs


def setup_inputs(seed=0):
    import zlib

    import numpy as np

    out = dict(_drawn_inputs(seed))
    spreads = {'L0_gnn_bias': (0.0, 0.1),
     'L0_ffn_b_gat': (0.0, 0.1),
     'L0_ffn_ln_gamma': (1.0, 0.2),
     'L0_ffn_ln_beta': (0.0, 0.1),
     'L0_ffn_b1': (0.0, 0.388),
     'L0_ffn_b2': (0.0, 0.294)}
    factors = {'L0_ffn_att_src': 3.552, 'L0_ffn_att_dst': 4.674}
    for name, (base, spread) in spreads.items():
        noise = np.random.default_rng([zlib.crc32(name.encode()), seed]).standard_normal(out[name].shape)
        drawn = base * np.exp(spread * noise) if base else spread * noise
        out[name] = jnp.asarray(drawn.astype(out[name].dtype))
    for name, factor in factors.items():
        out[name] = (out[name] * factor).astype(out[name].dtype)
    return out
```

```python
import concourse.bass as bass
from concourse import mybir
from contextlib import ExitStack

P = 128


class Steps:

    def __init__(self, engine, sem):
        self.engine, self.sem, self.value, self.offset = engine, sem, 0, 0

    def mark(self, instruction):
        self.value += 1
        instruction.then_inc(self.sem, 1)

    def wait(self):
        self.engine.wait_ge(self.sem, self.value + self.offset)

    def done(self, instruction):
        self.mark(instruction)
        self.wait()

    def enter(self, index, per_turn):
        self.begun, self.per_turn, self.offset = self.value, per_turn, index * per_turn

    def leave(self, turns):
        assert self.value == self.begun + self.per_turn, self.value - self.begun
        self.value, self.offset = self.begun + turns * self.per_turn, 0


def gnn_moe_kernel(nc, x, src, dst, edge_weight, W, bias, W_gat, att_src, att_dst, b_gat,
                   ln_gamma, ln_beta, W1, b1, W2, b2, edge_index, out):
    F32, I32, F16, BF16 = mybir.dt.float32, mybir.dt.int32, mybir.dt.float16, mybir.dt.bfloat16
    ALU, ACT, AX = mybir.AluOpType, mybir.ActivationFunctionType, mybir.AxisListType.X
    ds = bass.ds

    N, D = x.shape
    KD = D // P
    NT = -(-N // P)
    N_LAST = N - (NT - 1) * P
    NP_ = NT * P
    E1 = src.shape[0]
    HALF = 13
    G = 2 * HALF
    NG = -(-E1 // (P * G))
    C1 = NG * G
    E1_LAST = E1 - (P - 1) * C1
    U = 8
    K1 = -(-((P * C1 + (P - 1) * NT) // P) // U) * U
    L = -(-(P * G + 2 * (P - 1) * NT) // P // 2) * 2
    EX, _, HID = W1.shape
    KH = HID // P
    HEADS = att_src.shape[0]
    CH = HEADS * EX
    ROW = CH + 2 * HEADS
    E2 = edge_index.shape[1]
    C2E = E2 // P
    C2 = NT + C2E
    U2 = 12
    T2 = -(-C2 // U2)
    C2T = T2 * U2
    CG = -(-C2T // NG)
    SUB = 4
    SUBS = U2 // SUB
    LOOPS = -(-NT // U2)
    COUNT_TURNS = 3
    RANK_0 = COUNT_TURNS
    PLACE_TURN = RANK_0 + T2
    MOVE_0 = PLACE_TURN + 1
    MARK_0 = MOVE_0 + T2
    SLOTS = 6
    C2G = -(-C2 // SLOTS) * SLOTS
    NS = CH + HEADS
    T5 = 5
    assert T2 % 2 == 0 and C2T % 3 == 0 and CG * NG == C2T and K1 // U == MARK_0 + LOOPS and U2 % SUB == 0 and CG * NT <= 512
    assert NT % T5 == 0 and P * C2E == E2 and HID % P == 0 and L <= P and 0 < E1_LAST <= C1
    LN_EPS = 1e-5
    BIG = 1e30
    MIDDLE = float(NP_ // 2)
    NO_CHUNK = 4096.0
    BLK = 512
    TB = BLK // P
    NBLK = NT // TB
    assert NT == NBLK * TB + 1 and NP_ // 2 <= 2048

    ctx = ExitStack()
    with ctx:
        def sb(name, shape, dt=F32):
            return ctx.enter_context(nc.sbuf_tensor(name, shape, dt))

        def sem(name):
            return ctx.enter_context(nc.semaphore(name))

        h_dram = nc.dram_tensor("h_rows", [NP_, D], F32, kind="Internal").ap()
        gat_dram = nc.dram_tensor("gat_rows", [NP_, ROW], F32, kind="Internal").ap()
        sums_dram = nc.dram_tensor("gat_sums", [P * C2, NS], F32, kind="Internal").ap()
        rows_dram = nc.dram_tensor("gat_key_rows", [C2T, 2, P], F16, kind="Internal").ap()
        y_dram = nc.dram_tensor("expert_rows", [NP_, EX, D], F32, kind="Internal").ap()

        xs = sb("xs", [P, NT, D])
        big_t = sb("big_t", [P, KD * NP_])
        big_w = sb("big_w", [P, 2 * EX * KD * HID])
        big_h = sb("big_h", [P, 2 * KH * BLK])
        big_g = sb("big_g", [P, max(C2G * ROW, (C2T + 1) * NT)])
        big_y = sb("big_y", [P, 2 * TB * D])
        REGION = max(4 * K1 + 9 * C1, (4 * HEADS + 3) * C2)
        region = sb("region", [P, REGION])

        def part(place, start, shape, dt=F32):
            n = 1
            for s in shape:
                n *= s
            words = n if dt in (F32, I32) else -(-n // 2)
            assert start + words <= place.shape[1], (place.shape, start, shape)
            v = place[:, start:start + words]
            if dt is not F32:
                v = v.bitcast(dt)
            if len(shape) == 2:
                v = v.rearrange("p (a b) -> p a b", b=shape[1])
            elif len(shape) == 3:
                v = v.rearrange("p (a b c) -> p a b c", b=shape[1], c=shape[2])
            return v, start + words

        xT, _ = part(big_t, 0, [KD, NP_])
        ind5, n_ = part(big_t, 0, [T5, C1])
        at5, n_ = part(big_t, n_, [T5, C1])
        in5, n_ = part(big_t, n_, [T5, C1])
        rows2, n_ = part(big_t, 0, [2, U2, 2 * P], F16)
        rows2 = rows2.rearrange("p s u (v e) -> p s u v e", v=2)
        olT0, n_ = part(big_t, n_, [U2, P])
        rsel, n_ = part(big_t, n_, [U2, NT])
        same, n_ = part(big_t, n_, [U2, P], F16)
        ocol, n_ = part(big_t, 0, [U2, C2], F16)
        olane2, n_ = part(big_t, n_, [U2, P], F16)
        oval2, n_ = part(big_t, n_, [U2, P], F16)
        V20, _ = part(big_t, 0, [NS, C2])
        W1_sb, n_ = part(big_w, 0, [KD, EX, HID])
        W2_sb, _ = part(big_w, n_, [EX, KH, D])
        cum1, _ = part(big_w, 0, [NT, C1], F16)
        OH, n_ = part(big_w, 0, [C2T, NT], BF16)
        CT, n_ = part(big_w, n_, [C2T, NT], BF16)
        TK = C2T // 3
        key_rows, _ = part(big_w, n_, [3, 2 * P], F16)
        key_rows = key_rows.rearrange("p b (v e) -> p b v e", v=2)[0:TK, :, :, :]
        VS, _ = part(big_w, 0, [C2, NS])
        h_ff, _ = part(big_h, 0, [2, KH, BLK])
        olane1, _ = part(big_h, 0, [2, HALF, P])
        GT, _ = part(big_g, 0, [C2G, ROW])
        ochunk, n_ = part(big_g, 0, [2, HALF, L])
        pay_oh, n_ = part(big_g, n_, [2, HALF, 2 * L])
        PT, _ = part(big_g, 0, [C2T + 1, NT])
        y_sb, _ = part(big_y, 0, [2, TB * D])
        y_sb = y_sb.rearrange("p s (t d) -> p s t d", d=D)
        h_out, _ = part(big_y, 0, [T5, D])
        olT = (olT0, part(big_y, 0, [U2, P])[0])

        idx_s, n_ = part(region, 0, [K1], I32)
        w_s, n_ = part(region, n_, [K1])
        loc_s, n_ = part(region, n_, [K1])
        pack_i, n_ = part(region, n_, [K1], I32)
        n_sorting = n_
        lane1, n_ = part(region, n_, [C1])
        chunk1, n_ = part(region, n_, [C1])
        payload, n_ = part(region, n_, [2, C1])
        n_ranked = n_
        src1, n_ = part(region, n_, [C1], I32)
        dst1, n_ = part(region, n_, [C1], I32)
        tile1, n_ = part(region, n_, [C1])
        place1, n_ = part(region, n_, [C1])
        tmp1, n_ = part(region, n_, [C1], I32)
        ol1, n_ = part(region, n_ranked, [CG, P], BF16)
        lo2, n_ = part(region, n_, [C2T])
        hi2, n_ = part(region, n_, [C2T])
        val2, n_ = part(region, n_, [C2T + LOOPS * U2])
        pos2, n_ = part(region, n_sorting, [C2T])
        lane2, n_ = part(region, n_, [C2T + LOOPS * U2])
        col2, n_ = part(region, n_, [C2T + LOOPS * U2])
        tmp2, n_ = part(region, n_, [C2T])
        tmp2i, n_ = part(region, n_, [C2T], I32)
        ad_e, n_ = part(region, 0, [HEADS, C2])
        e_e, n_ = part(region, n_, [HEADS, C2])
        f_e, n_ = part(region, n_, [HEADS, C2])
        s_e, n_ = part(region, n_, [HEADS, C2])
        keep, n_ = part(region, n_, [C2])
        drop_f, n_ = part(region, n_, [C2])
        drop_r, n_ = part(region, n_, [C2])

        ident = sb("ident", [P, P])
        tri = sb("tri", [P, P])
        ones = sb("ones", [P, P])
        iota16 = sb("iota16", [P, 512], F16)
        iota_k = sb("iota_k", [P, K1])
        iota_p = sb("iota_p", [P, 1])
        first_g, _ = part(big_h, 0, [NT, NG])
        bias_b = sb("bias_b", [P, D])
        w_sb = sb("w_sb", [P, KD, D])
        wgat_sb = sb("wgat_sb", [P, KD, CH])
        att_b = sb("att_b", [P, 2, CH])
        gam_b = sb("gam_b", [P, 3, CH])
        b1_sb = sb("b1_sb", [P, EX, KH])
        b2_sb = sb("b2_sb", [EX, D])
        stats = sb("stats", [P, 2 * T5, 6])
        mv = sb("mv", [P, NT, 2])
        rstd = sb("rstd", [P, 4, NT])
        eps_c = sb("eps_c", [P, 1])
        xn = sb("xn", [P, T5, D])
        xnT = sb("xnT", [P, T5, KD, P])
        bucket = sb("bucket", [P, 6, NT])
        bucket_i = sb("bucket_i", [P, NT], I32)
        global_chunk = sb("global_chunk", [P, 3, NG])
        ogc = sb("ogc", [L, K1])
        keyc2 = sb("keyc2", [P, C2T])
        rank2 = sb("rank2", [P, C2T])
        tri16 = sb("tri16", [P, P], F16)
        lane_now = sb("lane_now", [P, HALF])
        group_sb = sb("group_sb", [P, 2, L])
        group_T = sb("group_T", [L, 2, P])
        zero_row = sb("zero_row", [1, K1])
        end_col = sb("end_col", [NT, 1])
        geq = ogc[0:NT, :]
        tile_of_chunk = sb("tile_of_chunk", [1, K1], I32)
        idx_turn = sb("idx_turn", [P, 2, U], I32)
        big_m = sb("big_m", [P, U * (D + P)])
        msgs, n_ = part(big_m, 0, [U, D])
        S1, _ = part(big_m, n_, [U, P])
        cnt = [part(big_m, i * NT * NG, [NT, NG])[0] for i in range(6)]
        cnt_i, _ = part(big_m, 6 * NT * NG, [NT, NG], I32)
        by_g = [part(big_y, i * NT * NG, [NG, NT])[0] for i in range(3)]
        key2 = sb("key2", [P, C2], I32)
        src2 = sb("src2", [P, C2], I32)
        endpos = sb("endpos", [P, NT], I32)
        starts = sb("starts", [P, C2])
        src_sorted = sb("src_sorted", [P, C2G], I32)
        gat_slot = sb("gat_slot", [P, SLOTS, ROW])
        edge_cols = sb("edge_cols", [P, 2, NS])
        across = sb("across", [NS, 3, P + 1])
        carry = sb("carry", [P, 2, NS])
        flag_any = sb("flag_any", [P, 4])
        key_tile, _ = part(starts, 0, [C2], I32)
        node_sums, n_ = part(big_m, 0, [NT, NS])
        agg, n_ = part(big_m, n_, [NT, CH])
        agg2, n_gT = part(big_m, n_, [NT, CH])
        sc4 = sb("sc4", [P, EX, NT])
        gate = sb("gate", [P, EX, NT])
        rank4 = sb("rank4", [P, EX, NT])
        pair = sb("pair", [P, 6, NT])
        gT = part(big_m, n_gT, [2, P])[0][0:EX, :, :]
        y_in = part(big_h, 0, [3, EX * D])[0].rearrange("p s (e d) -> p s e d", d=D)

        bank = [ctx.enter_context(nc.psum_tensor(f"bank{i}", [P, 512], F32)) for i in range(8)]

        AGG = 4

        def agg_bank(u):
            return bank[(0, 1, 4, 5)[u % AGG]][:, 0:D]

        names = """ld_src ld_dst ld_wt ld_x ld_w ld_keys ld_ffw pads_set consts dve_step pool_step
            counts_ready counts_mm ends_ready ends_mm geq_ready geq_mm
            var_a std_a xn_ready_a xn_T_a xnT_copied_a proj_mm_a proj_taken_a
            var_b std_b xn_ready_b xn_T_b xnT_copied_b proj_mm_b proj_taken_b xT_done
            hots_ready hots_used group_copied group_T_mm group_T_copied ogc_ready moved_mm
            moved_all edges_ready onehot_ready slots_free idx_copied idx_read agg_free
            ranks_done lane_hots_ready keys_ready tile_hots_ready squares_ready ol_ready cnt_mm cnt_copied tot2_ready base2_mm places_ready
            keys_T keys_T_copied key_rows_sent olT_squares olT_ready ranked r_mm r_used
            perm_ready perm_scaled perm_used perm_mm perm_taken
            table_ready table_sent gat_free gat_idx_copied gat_idx_read
            up_mm up_free down_mm down_taken y_ready
            cols_ready cols_T across_ready across_T exp_in exp_out
            sums_ready sums_sent var_c std_c wexp_in wexp_out
            gate_ready gate_T gate_T_copied gb_mm gb_used y_used out_ready out_sent""".split()
        S = {n: sem(n) for n in names}
        h_sent = [sem(f"h_sent{u}") for u in range(T5)]
        gathered = [sem(f"gathered{u}") for u in range(U)]
        gat_in = [sem(f"gat_in{u}") for u in range(SLOTS)]
        y_stored = [sem(f"y_stored{s}") for s in range(2)]
        rows_landed = [sem(f"rows_landed{s}") for s in range(2)]
        y_loaded = [sem(f"y_loaded{s}") for s in range(3)]
        sums_in = sem("sums_in")

        block = ctx.enter_context(nc.Block())

        @block.sync
        def _(sp):
            sp.wait_ge(S["pads_set"], 1)
            for place, array, landed in ((src1, src, "ld_src"), (dst1, dst, "ld_dst"),
                                         (payload[:, 0, :], edge_weight, "ld_wt")):
                sp.dma_start(place[0:P - 1, :], array[0:(P - 1) * C1].rearrange("(p c) -> p c", c=C1)).then_inc(S[landed], 16)
                sp.dma_start(place[P - 1:P, 0:E1_LAST], array[(P - 1) * C1:E1].rearrange("(p c) -> p c", p=1)).then_inc(S[landed], 16)
            sp.dma_start(xs[:, 0:NT - 1, :], x[0:(NT - 1) * P, :].rearrange("(t p) d -> p t d", p=P)).then_inc(S["ld_x"], 16)
            sp.dma_start(xs[0:N_LAST, NT - 1, :], x[(NT - 1) * P:N, :]).then_inc(S["ld_x"], 16)
            sp.dma_start(w_sb[:, :, :], W.rearrange("(k p) n -> p k n", p=P)).then_inc(S["ld_w"], 16)
            sp.dma_start(wgat_sb[:, :, :], W_gat.rearrange("(k p) n -> p k n", p=P)).then_inc(S["ld_w"], 16)
            sp.dma_start(bias_b[:, :], bias.unsqueeze(0).to_broadcast([P, D])).then_inc(S["ld_w"], 16)
            for i, v in enumerate((att_src, att_dst)):
                sp.dma_start(att_b[:, i, :], v.rearrange("h e -> (h e)").unsqueeze(0).to_broadcast([P, CH])).then_inc(S["ld_w"], 16)
            for i, v in enumerate((ln_gamma, ln_beta, b_gat)):
                sp.dma_start(gam_b[:, i, :], v.unsqueeze(0).to_broadcast([P, CH])).then_inc(S["ld_w"], 16)
            with nc.allow_non_contiguous_dma(reason="2048 bias words, once"):
                for e in range(EX):
                    sp.dma_start(b1_sb[:, e, :], b1[e, :].rearrange("(j p) -> p j", p=P)).then_inc(S["ld_w"], 16)
            sp.dma_start(b2_sb[:, :], b2).then_inc(S["ld_w"], 16)
            sp.dma_start(key2[:, NT:C2], edge_index[1, :].rearrange("(p c) -> p c", c=C2E)).then_inc(S["ld_keys"], 16)
            sp.dma_start(src2[:, NT:C2], edge_index[0, :].rearrange("(p c) -> p c", c=C2E)).then_inc(S["ld_keys"], 16)
            with sp.Fori(0, NT // T5) as i:
                for u in range(T5):
                    sp.wait_ge(S["proj_taken_a"], 2 + i * T5 + (u + 1))
                    sp.dma_start(h_dram[ds((i * T5 + u) * P, P), :], h_out[:, u, :]).then_inc(h_sent[u], 16)
            sp.wait_ge(S["keys_T_copied"], 6)
            sp.dma_start(rows_dram.rearrange("(b c) v e -> c b v e", b=3), key_rows[:, :, :, :]).then_inc(S["key_rows_sent"], 16)
            sp.wait_ge(S["key_rows_sent"], 16)
            sp.wait_ge(S["moved_all"], 1)
            def load_rows(k, side):
                sp.dma_start(rows2[:, side, :, :, :], rows_dram[ds(k * U2, U2), :, :].unsqueeze(0).to_broadcast([P, U2, 2, P])
                             ).then_inc(rows_landed[side], 16)

            for side in range(2):
                load_rows(side, side)
            with sp.Fori(1, T2 // 2) as i:
                for side in range(2):
                    sp.wait_ge(S["ranked"], i * 2 + side - 1)
                    sp.wait_ge(S["olT_ready"], i * 2 + side - 1)
                    load_rows(i * 2 + side, side)
            sp.wait_ge(S["perm_taken"], 1)
            for e in range(EX):
                sp.dma_start(W1_sb[:, :, e, :], W1[e, :, :].rearrange("(k p) n -> p k n", p=P)).then_inc(S["ld_ffw"], 16)
                sp.dma_start(W2_sb[:, e, :, :], W2[e, :, :].rearrange("(k p) n -> p k n", p=P)).then_inc(S["ld_ffw"], 16)
            sp.wait_ge(S["table_ready"], 1)
            sp.dma_start(gat_dram.rearrange("(t p) r -> p t r", p=P), GT[:, 0:NT, :]).then_inc(S["table_sent"], 16)

            def store_y(tile0, tiles, e, nth):
                sp.wait_ge(S["y_ready"], nth)
                sp.dma_start(y_dram[ds(tile0 * P, tiles * P), e, :].rearrange("(t p) d -> p t d", p=P),
                             y_sb[:, e % 2, 0:tiles, :]).then_inc(y_stored[e % 2], 16)

            with sp.Fori(0, NBLK) as i:
                for e in range(EX):
                    store_y(i * TB, TB, e, i * EX + (e + 1))
            for e in range(EX):
                store_y(NBLK * TB, 1, e, NBLK * EX + e + 1)
            sp.wait_ge(S["sums_ready"], 1)
            sp.dma_start(sums_dram.rearrange("(p c) s -> p (c s)", p=P), VS.rearrange("p c s -> p (c s)")).then_inc(S["sums_sent"], 16)
            for s in range(2):
                sp.wait_ge(y_stored[s], 16 * (EX // 2) * (NBLK + 1))
            sp.wait_ge(S["down_mm"], 2 * TB + EX * (NBLK * TB + 1))
            for t in range(NT):
                if t >= 3:
                    sp.wait_ge(S["y_used"], t - 2)
                sp.dma_start(y_in[:, t % 3, :, :], y_dram[t * P:(t + 1) * P, :, :]).then_inc(y_loaded[t % 3], 16)
                if t >= 3:
                    sp.wait_ge(S["out_ready"], t - 2)
                    sp.dma_start(out[(t - 3) * P:(t - 2) * P, :], xs[:, t - 3, :]).then_inc(S["out_sent"], 16)
            for t in range(NT - 3, NT):
                sp.wait_ge(S["out_ready"], t + 1)
                rows = P if t < NT - 1 else N_LAST
                sp.dma_start(out[t * P:t * P + rows, :], xs[0:rows, t, :]).then_inc(S["out_sent"], 16)
            sp.wait_ge(S["out_sent"], 16 * NT)

        @block.gpsimd
        def _(pool):
            steps = Steps(pool, S["pool_step"])
            steps.mark(pool.memset(xs[:, NT - 1, :], 0.0))
            for v in (src1, dst1, payload[:, 0, :]):
                steps.mark(pool.memset(v, 0))
            steps.wait()
            pool.nop().then_inc(S["pads_set"], 1)
            steps.mark(pool.memset(ident[:, :], 0.0))
            steps.mark(pool.memset(ones[:, :], 1.0))
            steps.mark(pool.memset(tri[:, :], 1.0))
            steps.mark(pool.memset(first_g[:, :, :], 1.0))
            steps.mark(pool.memset(zero_row[:, :], 0.0))
            steps.mark(pool.memset(eps_c[:, :], LN_EPS))
            for v, pattern, cm in ((iota16[:, :], [[1, 512]], 0), (iota_k[:, :], [[1, K1]], 0), (iota_p[:, :], [[0, 1]], 1)):
                steps.mark(pool.iota(v, pattern=pattern, base=0, channel_multiplier=cm, allow_small_or_imprecise_dtypes=True))
            steps.wait()
            steps.mark(pool.memset(first_g[:, :, 0:1], 0.0))
            steps.mark(pool.affine_select(out=ident[:, :], in_=ident[:, :], compare_op=ALU.not_equal, fill=1.0, base=0,
                                          pattern=[[-1, P]], channel_multiplier=1))
            steps.mark(pool.affine_select(out=tri[:, :], in_=tri[:, :], compare_op=ALU.is_gt, fill=0.0, base=0,
                                          pattern=[[1, P]], channel_multiplier=-1))
            steps.mark(pool.iota(key2[:, 0:NT], pattern=[[P, NT]], base=0, channel_multiplier=1))
            steps.mark(pool.iota(src2[:, 0:NT], pattern=[[P, NT]], base=0, channel_multiplier=1))
            steps.wait()
            steps.done(pool.memset(tri16[:, :], 1.0))
            steps.done(pool.affine_select(out=tri16[:, :], in_=tri16[:, :], compare_op=ALU.is_gt, fill=0.0, base=0,
                                          pattern=[[-1, P]], channel_multiplier=1))
            pool.nop().then_inc(S["consts"], 1)

            pool.wait_ge(S["ranks_done"], 1)
            pool.wait_ge(S["ld_keys"], 32)
            steps.mark(pool.memset(lo2, -1.0))
            steps.mark(pool.memset(hi2, -1.0))
            steps.mark(pool.memset(val2, 0.0))
            steps.wait()
            steps.mark(pool.tensor_copy(lo2[:, 0:C2], key2[:, :]))
            steps.mark(pool.memset(keyc2[:, :], 0.0))
            steps.mark(pool.tensor_copy(hi2[:, 0:C2], key_tile))
            steps.mark(pool.tensor_scalar(val2[:, 0:C2], src2[:, :], MIDDLE, None, ALU.subtract))
            steps.wait()
            steps.done(pool.tensor_scalar(keyc2[:, 0:C2], hi2[:, 0:C2], float(P), MIDDLE, ALU.mult, ALU.subtract))
            steps.mark(pool.tensor_tensor(keyc2[:, 0:C2], keyc2[:, 0:C2], lo2[:, 0:C2], ALU.add))
            steps.mark(pool.memset(val2[:, C2T:C2T + NT], 1.0))
            steps.wait()
            pool.nop().then_inc(S["keys_ready"], 1)
            for t in range(NT):
                steps.mark(pool.tensor_scalar(OH[:, :, t], hi2, float(t), None, ALU.is_equal))
            steps.wait()
            pool.nop().then_inc(S["tile_hots_ready"], 1)
            with pool.Fori(0, NG) as g:
                pool.wait_ge(S["hots_used"], g * 2 + 1)
                steps.enter(g, 1)
                steps.done(pool.tensor_copy(lane_now[:, :], lane1[:, ds(g * G, HALF)]))
                steps.leave(NG)
                pool.nop(nofuse=True)
                for c in range(HALF):
                    last = pool.tensor_scalar(olane1[:, 0, c, :], iota_k[:, 0:P], lane_now[:, c:c + 1], None, ALU.is_equal)
                last.then_inc(S["lane_hots_ready"], 1)

            pool.wait_ge(S["edges_ready"], 1)
            for u in range(T5):
                pool.wait_ge(h_sent[u], 16 * (NT // T5))
            def gather_turn(turn, side, slots, rows, numbers, table, free, copied, landed):
                pool.tensor_copy(idx_turn[:, side, 0:slots], numbers[:, ds(turn * slots, slots)]).then_inc(copied, 1)
                pool.wait_ge(copied, turn + 1)
                for u in range(slots):
                    pool.wait_ge(free, turn * slots + (u + 1))
                    pool.nop(nofuse=True)
                    pool.indirect_dma_start(rows[:, u, :], None, table,
                                            bass.IndirectOffsetOnAxis(ap=idx_turn[:, side, u:u + 1], axis=0)).then_inc(landed[u], 16)

            def gather_all(turns, *how):
                with pool.Fori(0, turns // 2) as i:
                    gather_turn(i * 2, 0, *how)
                    gather_turn(i * 2 + 1, 1, *how)
                for turn in range(turns // 2 * 2, turns):
                    gather_turn(turn, 0, *how)

            gather_all(K1 // U, U, msgs, idx_s, h_dram, S["slots_free"], S["idx_copied"], gathered)

            pool.wait_ge(S["slots_free"], U + K1)
            pool.wait_ge(S["perm_taken"], 1)
            pool.wait_ge(S["table_sent"], 16)
            gather_all(C2G // SLOTS, SLOTS, gat_slot, src_sorted, gat_dram, S["gat_free"], S["gat_idx_copied"], gat_in)

            pool.wait_ge(S["sums_sent"], 16)
            for t in range(NT):
                pool.indirect_dma_start(node_sums[:, t, :], None, sums_dram,
                                        bass.IndirectOffsetOnAxis(ap=endpos[:, t:t + 1], axis=0)).then_inc(sums_in, 16)

        def ln_act(act, which):
            out_rows = (lambda i, u: h_out[:, u, :]) if which == "a" else (lambda i, u: GT[:, ds(i * T5 + u, 1), 0:CH])

            def copy(i, u):
                act.wait_ge(S[f"xn_T_{which}"], T5 + i * T5 + (u + 1))
                act.wait_ge(S[f"proj_mm_{which}"], i * T5 + (u + 1))
                view = bank[u][:, 0:D].rearrange("p (k n) -> p k n", k=KD)
                nc.scalar.activation(xnT[:, u, :, :], view, ACT.Copy).then_inc(S[f"xnT_copied_{which}"], 1)

            def copy_whole(i, u):
                act.wait_ge(S[f"xnT_copied_{which}"], T5 + i * T5 + (u + 1))
                nc.scalar.activation(xT[:, :, ds((i * T5 + u) * P, P)], xnT[:, u, :, :], ACT.Copy).then_inc(S["xT_done"], 1)

            def take(i, u, first):
                act.wait_ge(S[f"proj_mm_{which}"], T5 + i * T5 + (u + 1))
                if which == "a" and not first:
                    act.wait_ge(h_sent[u], i * 16)
                width = D if which == "a" else CH
                nc.scalar.activation(out_rows(i, u), bank[5 + u % 3][:, 0:width], ACT.Copy).then_inc(S[f"proj_taken_{which}"], 1)

            def turn(i, first=False):
                for u in range(T5 + 1):
                    if u < T5:
                        copy(i, u)
                        if which == "b":
                            copy_whole(i, u)
                    if u:
                        take(i, u - 1, first)

            turn(0, True)
            with act.Fori(1, NT // T5) as i:
                turn(i)

        @block.scalar
        def _(act):
            act.nop().then_inc(S["xnT_copied_a"], T5)
            act.nop().then_inc(S["xnT_copied_b"], T5)
            act.nop().then_inc(S["proj_taken_a"], 2)
            act.nop().then_inc(S["proj_taken_b"], 2)
            act.nop().then_inc(S["group_copied"], 1)
            act.nop().then_inc(S["cnt_copied"], 1)
            act.nop().then_inc(S["up_free"], KH)
            act.nop().then_inc(S["down_taken"], TB)
            act.wait_ge(S["var_a"], 1)
            nc.scalar.activation(rstd[:, 1, :], rstd[:, 0, :], ACT.Sqrt).then_inc(S["std_a"], 1)
            ln_act(act, "a")
            for n in range(6):
                act.wait_ge(S["keys_T"], n + 1)
                nc.scalar.activation(key_rows[:, n // 2, n % 2, :], bank[n][0:TK, 0:P], ACT.Copy).then_inc(S["keys_T_copied"], 1)
            act.wait_ge(S["keys_ready"], 1)
            with act.Fori(0, NG) as g:
                act.wait_ge(S["cnt_mm"], g + 1)
                for u in range(CG):
                    last = nc.scalar.activation(ol1[:, u, :], iota16[:, 0:P], ACT.Square, scale=-1.0, bias=lo2[:, ds(g * CG + u, 1)])
                last.then_inc(S["squares_ready"], 1)
                act.wait_ge(S["squares_ready"], g + 1)
                nc.scalar.activation(ol1, ol1, ACT.Relu, scale=-2.0, bias=ones[:, 0:1]).then_inc(S["ol_ready"], 1)
                act.wait_ge(S["cnt_mm"], g + 2)
                nc.scalar.activation(CT[:, ds(g * CG, CG), :], bank[0][:, 0:CG * NT].rearrange("p (u t) -> p u t", u=CG),
                                     ACT.Copy).then_inc(S["cnt_copied"], 1)
                act.wait_ge(S["hots_used"], 2 + (g + 1) * 2)
                nc.scalar.activation(group_sb[:, :, :], bank[4][:, 0:2 * L].rearrange("p (v l) -> p v l", v=2),
                                     ACT.Copy).then_inc(S["group_copied"], 1)
                act.wait_ge(S["group_T_mm"], g + 1)
                act.wait_ge(S["moved_mm"], g + 1)
                nc.scalar.activation(group_T[:, :, :], bank[5][0:L, 0:2 * P].rearrange("p (v l) -> p v l", v=2),
                                     ACT.Copy).then_inc(S["group_T_copied"], 1)
            def row_hots(i, side, first):
                k = i * 2 + side
                act.wait_ge(rows_landed[side], i * 16 + 16)
                if not first:
                    act.wait_ge(S["r_mm"], k - 1)
                nc.scalar.activation(olT[side], rows2[:, side, :, 0, :], ACT.Square, scale=-1.0, bias=iota_p[:, 0:1]).then_inc(S["olT_squares"], 1)
                act.wait_ge(S["olT_squares"], k + 1)
                nc.scalar.activation(olT[side], olT[side], ACT.Relu, scale=-2.0, bias=ones[:, 0:1]).then_inc(S["olT_ready"], 1)

            for u in range(T5):
                act.wait_ge(h_sent[u], 16 * (NT // T5))
            for side in range(2):
                row_hots(0, side, True)
            with act.Fori(1, T2 // 2) as i:
                for side in range(2):
                    row_hots(i, side, False)
            with act.Fori(0, T2 + LOOPS) as i:
                for q in range(SUBS):
                    act.wait_ge(S["perm_ready"], i * SUBS + (q + 1))
                    for u in range(q * SUB, (q + 1) * SUB):
                        last = nc.scalar.activation(oval2[:, u, :], olane2[:, u, :], ACT.Copy, scale=val2[:, ds(i * U2 + u, 1)])
                    last.then_inc(S["perm_scaled"], 1)
            act.wait_ge(S["var_b"], 1)
            nc.scalar.activation(rstd[:, 1, :], rstd[:, 0, :], ACT.Sqrt).then_inc(S["std_b"], 1)
            ln_act(act, "b")

            def hidden(tokens, e, up_before, down_before):
                act.wait_ge(S["down_mm"], 2 * TB + down_before)
                for j in range(KH):
                    act.wait_ge(S["up_mm"], up_before + (j + 1))
                    nc.scalar.activation(h_ff[:, e % 2, j, 0:tokens], bank[j][:, 0:tokens], ACT.Gelu,
                                         bias=b1_sb[:, e, j:j + 1]).then_inc(S["up_free"], 1)

            def rows(tiles, e, down_before, stored_before):
                if stored_before is not None:
                    act.wait_ge(y_stored[e % 2], stored_before)
                for t in range(tiles):
                    act.wait_ge(S["down_mm"], 2 * TB + down_before + (t + 1))
                    nc.scalar.activation(y_sb[:, e % 2, t, :], bank[4 + t][:, 0:D], ACT.Copy).then_inc(S["down_taken"], 1)
                act.wait_ge(S["down_taken"], TB + down_before + tiles)
                act.nop().then_inc(S["y_ready"], 1)

            def block_act(i, first):
                for e in range(EX + 1):
                    if e < EX:
                        hidden(BLK, e, (i * EX + e) * KH, (i * EX + (e - 1)) * TB)
                    if e:
                        stored = None if first and e - 1 < 2 else (i * (EX // 2) + (e - 1) // 2) * 16
                        rows(TB, e - 1, (i * EX + (e - 1)) * TB, stored)

            act.wait_ge(S["ld_w"], 16 * (8 + EX + 1))
            block_act(0, True)
            with act.Fori(1, NBLK) as i:
                block_act(i, False)
            all_before = NBLK * EX * TB
            for e in range(EX + 1):
                if e < EX:
                    hidden(P, e, (NBLK * EX + e) * KH, all_before - TB if e == 0 else all_before + e - 1)
                if e:
                    rows(1, e - 1, all_before + e - 1, (NBLK * (EX // 2) + (e - 1) // 2) * 16)
            act.wait_ge(S["exp_in"], 1)
            nc.scalar.activation(e_e[:, :, :], e_e[:, :, :], ACT.Exp).then_inc(S["exp_out"], 1)
            act.wait_ge(S["var_c"], 1)
            nc.scalar.activation(pair[:, 1, :], pair[:, 0, :], ACT.Sqrt).then_inc(S["std_c"], 1)
            act.wait_ge(S["wexp_in"], 1)
            nc.scalar.activation(gate[:, :, :], gate[:, :, :], ACT.Exp).then_inc(S["wexp_out"], 1)

        def ln_pe(pe, which):
            rhs = w_sb if which == "a" else wgat_sb
            width = D if which == "a" else CH

            def transpose(i, u):
                pe.wait_ge(S[f"xn_ready_{which}"], i * T5 + (u + 1))
                pe.wait_ge(S[f"xnT_copied_{which}"], i * T5 + (u + 1))
                for k in range(KD):
                    last = nc.tensor.transpose(bank[u][:, k * P:(k + 1) * P], xn[:, u, k * P:(k + 1) * P], ident[:, :])
                last.then_inc(S[f"xn_T_{which}"], 1)

            def project(i, u):
                pe.wait_ge(S[f"xnT_copied_{which}"], T5 + i * T5 + (u + 1))
                pe.wait_ge(S[f"proj_taken_{which}"], i * T5 + (u + 1))
                for k in range(KD):
                    last = nc.tensor.matmul(bank[5 + u % 3][:, 0:width], xnT[:, u, k, :], rhs[:, k, :],
                                            start=(k == 0), stop=(k == KD - 1))
                last.then_inc(S[f"proj_mm_{which}"], 1)

            with pe.Fori(0, NT // T5) as i:
                for u in range(T5 + 1):
                    if u < T5:
                        transpose(i, u)
                    if u:
                        project(i, u - 1)
            pe.wait_ge(S[f"proj_taken_{which}"], 2 + NT)

        @block.tensor
        def _(pe):
            pe.nop().then_inc(S["xn_T_a"], T5)
            pe.nop().then_inc(S["xn_T_b"], T5)
            pe.nop().then_inc(S["proj_mm_a"], T5)
            pe.nop().then_inc(S["proj_mm_b"], T5)
            pe.nop().then_inc(S["hots_used"], 2)
            pe.nop().then_inc(S["moved_mm"], 1)
            pe.nop().then_inc(S["slots_free"], U)
            pe.nop().then_inc(S["cnt_mm"], 1)
            pe.nop().then_inc(S["perm_used"], SUBS)
            pe.nop().then_inc(S["down_mm"], 2 * TB)
            pe.wait_ge(S["consts"], 1)
            pe.wait_ge(S["counts_ready"], 1)
            flat = cnt[0][:, :, :].rearrange("p b g -> p (b g)")
            nc.tensor.matmul(bank[0][:, 0:NT * NG], tri[:, :], flat, start=True, stop=True)
            nc.tensor.matmul(bank[1][:, 0:NT * NG], ones[:, :], flat, start=True, stop=True).then_inc(S["counts_mm"], 1)
            pe.wait_ge(S["ends_ready"], 1)
            nc.tensor.matmul(bank[2][0:NT, 0:1], bucket[0:1, 3, :], ones[0:1, 0:1], start=True, stop=True).then_inc(S["ends_mm"], 1)
            pe.wait_ge(S["geq_ready"], 1)
            nc.tensor.matmul(bank[3][0:1, 0:K1], ones[0:NT, 0:1], geq[:, :], start=True, stop=True).then_inc(S["geq_mm"], 1)
            pe.wait_ge(S["ld_w"], 16 * (8 + EX + 1))
            ln_pe(pe, "a")
            pe.wait_ge(S["keys_ready"], 1)
            for n in range(6):
                nc.tensor.transpose(bank[n][0:TK, 0:P], (lo2, keyc2)[n % 2][:, n // 2 * TK:(n // 2 + 1) * TK], ident[:, :]).then_inc(S["keys_T"], 1)
            for v in range(2):
                nc.tensor.matmul(bank[6 + v][:, 0:K1], zero_row[:, 0:P], zero_row[:, :], start=True, stop=False)
            pe.wait_ge(S["tile_hots_ready"], 1)
            pe.wait_ge(S["keys_T_copied"], 6)
            with pe.Fori(0, NG) as g:
                pe.wait_ge(S["ol_ready"], g + 1)
                pe.wait_ge(S["cnt_copied"], g + 1)
                for u in range(CG):
                    last = nc.tensor.matmul(bank[0][:, u * NT:(u + 1) * NT], ol1[:, u, :],
                                            OH[:, ds(g * CG + u, 1), :].rearrange("p a t -> p (a t)"), start=True, stop=True)
                last.then_inc(S["cnt_mm"], 1)
                pe.wait_ge(S["group_copied"], g + 1)
                pe.wait_ge(S["lane_hots_ready"], g + 1)
                for half in range(2):
                    pe.wait_ge(S["hots_ready"], g * 2 + (half + 1))
                    for c in range(HALF):
                        last = nc.tensor.matmul(bank[4][:, 0:2 * L], olane1[:, half, c, :], pay_oh[:, half, c, :],
                                                start=(half == 0 and c == 0), stop=(half == 1 and c == HALF - 1))
                    last.then_inc(S["hots_used"], 1)
                pe.wait_ge(S["group_copied"], g + 2)
                for v in range(2):
                    last = nc.tensor.transpose(bank[5][0:L, v * P:(v + 1) * P], group_sb[:, v, :], ident[:, :])
                last.then_inc(S["group_T_mm"], 1)
                pe.wait_ge(S["group_T_copied"], g + 1)
                pe.wait_ge(S["ogc_ready"], g + 1)
                for v in range(2):
                    last = nc.tensor.matmul(bank[6 + v][:, 0:K1], group_T[:, v, :], ogc[:, :], start=False, stop=False)
                last.then_inc(S["moved_mm"], 1)
            for v in range(2):
                last = nc.tensor.matmul(bank[6 + v][:, 0:K1], zero_row[:, 0:P], zero_row[:, :], start=False, stop=True)
            last.then_inc(S["moved_all"], 1)
            def sum_chunk(turn, u):
                pe.wait_ge(S["onehot_ready"], turn * U + (u + 1))
                pe.wait_ge(S["agg_free"], turn * U + (u + 1))
                pe.wait_ge(gathered[u], turn * 16 + 16)
                nc.tensor.matmul(agg_bank(u), S1[:, u, :], msgs[:, u, :], start=True, stop=True).then_inc(S["slots_free"], 1)

            def move(k, q, into):
                pe.wait_ge(S["perm_scaled"], k * SUBS + (q + 1))
                for u in range(q * SUB, (q + 1) * SUB):
                    last = nc.tensor.matmul(into[:, 0:C2], oval2[:, u, :], ocol[:, u, :], start=False, stop=False)
                last.then_inc(S["perm_used"], 1)

            pe.wait_ge(S["cnt_copied"], NG + 1)
            for u in range(U):
                sum_chunk(0, u)
            pe.wait_ge(S["tot2_ready"], 1)
            nc.tensor.matmul(bank[2][:, 0:NT], tri[:, :], bucket[:, 0, :], start=True, stop=True)
            nc.tensor.matmul(bank[3][:, 0:NT], ones[:, :], bucket[:, 0, :], start=True, stop=True).then_inc(S["base2_mm"], 1)
            with pe.Fori(1, COUNT_TURNS) as i:
                for u in range(U):
                    sum_chunk(i, u)
            pe.wait_ge(S["places_ready"], 1)
            def rank_turn(i, side):
                k = i * 2 + side
                for u in range(U):
                    sum_chunk(k + RANK_0, u)
                    if u == 0:
                        pe.wait_ge(S["olT_ready"], k + 1)
                        pe.wait_ge(S["r_used"], k + 1)
                        for c in range(U2):
                            last = nc.tensor.matmul(bank[6 + side][:, c * NT:(c + 1) * NT], olT[side][:, c, :],
                                                    PT[:, ds(k * U2 + c, 1), :].rearrange("p a t -> p (a t)"), start=True, stop=True)
                        last.then_inc(S["r_mm"], 1)

            with pe.Fori(0, T2 // 2) as i:
                for side in range(2):
                    rank_turn(i, side)
            for b in range(2):
                nc.tensor.matmul(bank[2 + b][:, 0:C2], zero_row[:, 0:P], zero_row[:, 0:C2], start=True, stop=False)
            for u in range(U):
                sum_chunk(PLACE_TURN, u)

            def move_turn(k, into):
                for u in range(U):
                    sum_chunk(k + MOVE_0, u)
                    if u in (3, 5, 7):
                        move(k, (u - 3) // 2, into)

            with pe.Fori(0, T2) as i:
                move_turn(i, bank[2])
            with pe.Fori(T2, T2 + LOOPS) as i:
                move_turn(i, bank[3])
            for b in range(2):
                last = nc.tensor.matmul(bank[2 + b][:, 0:C2], zero_row[:, 0:P], zero_row[:, 0:C2], start=False, stop=True)
            last.then_inc(S["perm_mm"], 1)
            pe.wait_ge(S["agg_free"], K1 + AGG)
            pe.wait_ge(S["perm_taken"], 1)
            ln_pe(pe, "b")

            def up(tokens, e, off, up_before):
                for j in range(KH):
                    pe.wait_ge(S["up_free"], up_before + (j + 1))
                    for k in range(KD):
                        last = nc.tensor.matmul(bank[j][:, 0:tokens], W1_sb[:, k, e, j * P:(j + 1) * P],
                                                xT[:, k, ds(off, tokens)], start=(k == 0), stop=(k == KD - 1))
                    last.then_inc(S["up_mm"], 1)

            def down(tiles, e, up_before, taken):
                pe.wait_ge(S["up_free"], up_before + 2 * KH)
                for t in range(tiles):
                    pe.wait_ge(S["down_taken"], taken + t)
                    for j in range(KH):
                        last = nc.tensor.matmul(bank[4 + t][:, 0:D], h_ff[:, e % 2, j, t * P:(t + 1) * P], W2_sb[:, e, j, :],
                                                start=(j == 0), stop=(j == KH - 1))
                    last.then_inc(S["down_mm"], 1)

            pe.wait_ge(S["xT_done"], NT)
            pe.wait_ge(S["ld_ffw"], 16 * 2 * EX)
            with pe.Fori(0, NBLK) as i:
                for e in range(EX + 1):
                    if e < EX:
                        up(BLK, e, i * BLK, (i * EX + e) * KH)
                    if e:
                        down(TB, e - 1, (i * EX + (e - 1)) * KH, (i * EX + (e - 1)) * TB + 1)
            for e in range(EX + 1):
                if e < EX:
                    up(P, e, NBLK * BLK, (NBLK * EX + e) * KH)
                if e:
                    m = NBLK * EX
                    down(1, e - 1, (m + e - 1) * KH, m * TB + 1 if e == 1 else TB + m * TB + e - 1)
            pe.wait_ge(S["down_taken"], TB + NBLK * EX * TB + EX)
            for q, (k, shift) in enumerate(((HEADS, 0), (HEADS, 0), (HEADS, 1), (NS, 0))):
                pe.wait_ge(S["cols_ready"], q + 1)
                nc.tensor.transpose(bank[0][0:k, 0:P], edge_cols[:, 0, 0:k], ident[:, :])
                nc.tensor.transpose(bank[0][0:k, P:2 * P], edge_cols[:, 1, 0:k], ident[:, :]).then_inc(S["cols_T"], 1)
                pe.wait_ge(S["across_ready"], q + 1)
                nc.tensor.transpose(bank[1][:, 0:k], across[0:k, 2, shift:shift + P], ident[0:k, 0:k]).then_inc(S["across_T"], 1)
            pe.wait_ge(S["gate_ready"], 1)
            for t in range(NT):
                nc.tensor.transpose(bank[2][0:EX, 0:P], gate[:, :, t], ident[:, :]).then_inc(S["gate_T"], 1)
                pe.wait_ge(S["gate_T_copied"], t + 1)
                if t >= 2:
                    pe.wait_ge(S["gb_used"], t - 1)
                nc.tensor.matmul(bank[3 + t % 2][:, 0:D], gT[:, t % 2, :], b2_sb[:, :], start=True, stop=True).then_inc(S["gb_mm"], 1)

        @block.vector
        def _(dve):
            steps = Steps(dve, S["dve_step"])
            V = nc.vector
            dve.nop().then_inc(S["agg_free"], AGG)
            dve.nop().then_inc(S["r_used"], 2)
            dve.nop().then_inc(S["gat_free"], SLOTS)

            dve.wait_ge(S["consts"], 1)
            dve.wait_ge(S["ld_src"], 32)
            dve.wait_ge(S["ld_dst"], 32)
            dve.wait_ge(S["ld_wt"], 32)
            steps.mark(V.tensor_copy(payload[:, 1, :], dst1))
            steps.done(V.tensor_single_scalar(tmp1, src1, 7, ALU.logical_shift_right))
            steps.mark(V.tensor_copy(tile1, tmp1))
            steps.done(V.tensor_single_scalar(src1, src1, P - 1, ALU.bitwise_and))
            steps.done(V.tensor_copy(lane1, src1))
            steps.done(V.scalar_tensor_tensor(payload[:, 1, :], payload[:, 1, :], float(P), lane1, ALU.mult, ALU.add))
            with dve.Fori(0, NT // T5) as i:
                steps.enter(i, 2 * T5)
                for u in range(T5):
                    steps.mark(V.tensor_scalar(ind5[:, u, :], tile1, iota_k[:, ds(i * T5 + u, 1)], None, ALU.is_equal))
                steps.wait()
                for u in range(T5):
                    steps.mark(V.tensor_tensor_scan(cum1[:, ds(i * T5 + u, 1), :].rearrange("p a c -> p (a c)"),
                                                    ones[:, 0:1].to_broadcast([P, C1]), ind5[:, u, :], 0.0, ALU.mult, ALU.add))
                steps.wait()
                steps.leave(NT // T5)
            ends = cum1.rearrange("p b (g c) -> p b g c", c=G)[:, :, :, G - 1]
            steps.mark(V.tensor_copy(cnt[0][:, :, 0:1], ends[:, :, 0:1]))
            steps.done(V.tensor_tensor(cnt[0][:, :, 1:NG], ends[:, :, 1:NG], ends[:, :, 0:NG - 1], ALU.subtract))
            dve.nop().then_inc(S["counts_ready"], 1)
            dve.wait_ge(S["counts_mm"], 1)
            flat = [c[:, :, :].rearrange("p b g -> p (b g)") for c in cnt]
            steps.mark(V.tensor_copy(flat[5], bank[1][:, 0:NT * NG]))
            steps.wait()
            steps.done(V.tensor_tensor_scan(flat[1], first_g[:, :, :].rearrange("p b g -> p (b g)"), flat[5],
                                            0.0, ALU.mult, ALU.add))
            total, number, last_, end_, first_ = (bucket[:, i, :] for i in range(5))
            steps.done(V.tensor_scalar(total, cnt[1][:, :, NG - 1], float(P - 1), None, ALU.add))
            steps.done(V.tensor_copy(bucket_i[:, :], total))
            steps.done(V.tensor_single_scalar(bucket_i[:, :], bucket_i[:, :], 7, ALU.logical_shift_right))
            steps.done(V.tensor_copy(number, bucket_i[:, :]))
            steps.done(V.tensor_tensor_scan(end_, ones[:, 0:NT], number, 0.0, ALU.mult, ALU.add))
            dve.nop().then_inc(S["ends_ready"], 1)
            steps.done(V.tensor_tensor(first_, end_, number, ALU.subtract))
            steps.done(V.scalar_tensor_tensor(cnt[1][:, :, :], first_.unsqueeze(2).to_broadcast([P, NT, NG]), float(P),
                                              cnt[1][:, :, :], ALU.mult, ALU.add))
            steps.done(V.tensor_tensor(flat[2], flat[1], flat[5], ALU.subtract))
            steps.done(V.tensor_copy(cnt_i[:, :, :], cnt[2][:, :, :]))
            steps.done(V.tensor_single_scalar(cnt_i[:, :, :], cnt_i[:, :, :], 7, ALU.logical_shift_right))
            steps.done(V.tensor_copy(cnt[3][:, :, :], cnt_i[:, :, :]))
            steps.done(V.tensor_scalar(flat[4], flat[1], float(P - 1), None, ALU.add))
            steps.done(V.tensor_copy(cnt_i[:, :, :], cnt[4][:, :, :]))
            steps.done(V.tensor_single_scalar(cnt_i[:, :, :], cnt_i[:, :, :], 7, ALU.logical_shift_right))
            steps.done(V.tensor_copy(cnt[4][:, :, :], cnt_i[:, :, :]))
            steps.done(V.tensor_tensor(by_g[0][:, :, :].rearrange("p g b -> p b g"), cnt[4][:, :, :], cnt[3][:, :, :], ALU.subtract))
            for g in range(NG):
                steps.mark(V.tensor_tensor_scan(by_g[1][:, g, :], ones[:, 0:NT], by_g[0][:, g, :], 0.0, ALU.mult, ALU.add))
            steps.wait()
            steps.done(V.tensor_tensor(by_g[0][:, :, :], by_g[1][:, :, :], by_g[0][:, :, :], ALU.subtract))
            steps.done(V.tensor_tensor(cnt[4][:, :, :], by_g[0][:, :, :].rearrange("p g b -> p b g"), cnt[3][:, :, :], ALU.subtract))
            steps.done(V.scalar_tensor_tensor(flat[5], flat[4], float(P), flat[2], ALU.mult, ALU.add))
            steps.done(V.tensor_tensor(flat[5], flat[5], bank[0][:, 0:NT * NG], ALU.add))
            steps.done(V.tensor_scalar(flat[5], flat[5], 1.0, None, ALU.subtract))
            steps.done(V.tensor_tensor(cnt[5][:, :, 1:NG], cnt[5][:, :, 1:NG], ends[:, :, 0:NG - 1], ALU.subtract))
            span = by_g[2][:, :, :]
            steps.done(V.tensor_scalar(span, by_g[1][:, :, :], iota_p[:, 0:1], None, ALU.is_le))
            steps.done(V.tensor_scalar(by_g[1][:, :, :], by_g[0][:, :, :], iota_p[:, 0:1], None, ALU.is_le))
            steps.done(V.tensor_tensor(span, by_g[1][:, :, :], span, ALU.subtract))
            steps.done(V.tensor_reduce(global_chunk[:, 0, :], span, AX, ALU.add))
            steps.done(V.tensor_tensor(span, span, cnt[4][:, :, :].rearrange("p b g -> p g b"), ALU.mult))
            steps.done(V.tensor_reduce(global_chunk[:, 1, :], span, AX, ALU.add))
            steps.done(V.tensor_scalar(global_chunk[:, 0, :], global_chunk[:, 0, :], -NO_CHUNK, NO_CHUNK, ALU.mult, ALU.add))
            steps.done(V.tensor_tensor(global_chunk[:, 0, :], global_chunk[:, 0, :], global_chunk[:, 1, :], ALU.subtract))
            steps.done(V.tensor_scalar(global_chunk[:, 2, :], global_chunk[:, 0, :], iota_p[:, 0:1], None, ALU.add))
            dve.wait_ge(S["ends_mm"], 1)
            steps.done(V.tensor_copy(end_col[:, :], bank[2][0:NT, 0:1]))
            V.tensor_scalar(geq[:, :], iota_k[0:NT, :], end_col[:, 0:1], None, ALU.is_ge).then_inc(S["geq_ready"], 1)
            dve.wait_ge(S["geq_mm"], 1)
            steps.done(V.tensor_scalar(tile_of_chunk[:, :], bank[3][0:1, 0:K1], float(NT - 1), None, ALU.min))
            steps.done(V.memset(place1, 0.0))
            with dve.Fori(0, NT // T5) as i:
                steps.enter(i, 3 * T5)
                for u in range(T5):
                    b = ds(i * T5 + u, 1)
                    steps.mark(V.tensor_tensor(at5[:, u, :].rearrange("p (g c) -> p g c", c=G),
                                               cum1[:, b, :].rearrange("p a (g c) -> p (a g) c", c=G),
                                               cnt[5][:, b, :].rearrange("p a g -> p (a g)").unsqueeze(2).to_broadcast([P, NG, G]),
                                               ALU.add))
                steps.wait()
                for u in range(T5):
                    steps.mark(V.scalar_tensor_tensor(in5[:, u, :], tile1, iota_k[:, ds(i * T5 + u, 1)], at5[:, u, :],
                                                      ALU.is_equal, ALU.mult))
                steps.wait()
                for u in range(T5):
                    steps.done(V.tensor_tensor(place1, place1, in5[:, u, :], ALU.add))
                steps.leave(NT // T5)
            steps.done(V.tensor_copy(tmp1, place1))
            steps.done(V.tensor_single_scalar(src1, tmp1, P - 1, ALU.bitwise_and))
            steps.mark(V.tensor_copy(lane1, src1))
            steps.done(V.tensor_single_scalar(tmp1, tmp1, 7, ALU.logical_shift_right))
            steps.mark(V.tensor_copy(chunk1, tmp1))
            dve.wait_ge(S["ld_keys"], 32)
            steps.done(V.tensor_single_scalar(key_tile, key2[:, :], 7, ALU.logical_shift_right))
            steps.done(V.tensor_single_scalar(key2[:, :], key2[:, :], P - 1, ALU.bitwise_and))
            dve.nop().then_inc(S["ranks_done"], 1)

            def layer_norm(which):
                with dve.Fori(0, NT // T5) as i:
                    steps.enter(i, 2 * T5 + 1)
                    for u in range(T5):
                        steps.mark(V.bn_stats(stats[:, u, :], xs[:, ds(i * T5 + u, 1), :].rearrange("p a d -> p (a d)")))
                    steps.wait()
                    dve.nop(nofuse=True)
                    for u in range(T5):
                        steps.mark(V.bn_aggr(stats[:, T5 + u, 0:2], stats[:, u, :]))
                    steps.wait()
                    steps.done(V.tensor_copy(mv[:, ds(i * T5, T5), :], stats[:, T5:2 * T5, 0:2]))
                    steps.leave(NT // T5)
                inverse_deviation(rstd, mv[:, :, 1], which)
                with dve.Fori(0, NT // T5) as i:
                    for u in range(T5):
                        t = ds(i * T5 + u, 1)
                        dve.wait_ge(S[f"xn_T_{which}"], i * T5 + (u + 1))
                        V.tensor_scalar(xn[:, u, :], xs[:, t, :].rearrange("p a d -> p (a d)"),
                                        mv[:, t, 0:1].rearrange("p a s -> p (a s)"), rstd[:, 3, t],
                                        ALU.subtract, ALU.mult).then_inc(S[f"xn_ready_{which}"], 1)

            def inverse_deviation(r, variance, which):
                steps.done(V.tensor_scalar(r[:, 0, :], variance, LN_EPS, None, ALU.add))
                dve.nop().then_inc(S[f"var_{which}"], 1)
                dve.wait_ge(S[f"std_{which}"], 1)
                steps.done(V.reciprocal(r[:, 2, :], r[:, 1, :]))
                steps.done(V.tensor_tensor(r[:, 3, :], r[:, 2, :], r[:, 2, :], ALU.mult))
                steps.done(V.tensor_tensor(r[:, 3, :], r[:, 3, :], r[:, 0, :], ALU.mult))
                steps.done(V.tensor_scalar(r[:, 3, :], r[:, 3, :], -0.5, 1.5, ALU.mult, ALU.add))
                steps.done(V.tensor_tensor(r[:, 3, :], r[:, 3, :], r[:, 2, :], ALU.mult))

            dve.wait_ge(S["ld_x"], 32)
            dve.wait_ge(S["ld_w"], 16 * (8 + EX + 1))
            layer_norm("a")
            dve.wait_ge(S["xn_ready_a"], NT)
            steps.done(V.tensor_tensor(xs[:, :, :], xs[:, :, :], bias_b[:, :].unsqueeze(1).to_broadcast([P, NT, D]), ALU.add))

            with dve.Fori(0, NG) as g:
                steps.enter(g, 2)
                for half in range(2):
                    dve.wait_ge(S["hots_used"], g * 2 + (half + 1))
                    col = ds(g * G + half * HALF, HALF)
                    bc = lambda v, n: v.unsqueeze(2).to_broadcast([P, HALF, n])
                    steps.mark(V.tensor_tensor(ochunk[:, half, :, :], iota16[:, 0:L].unsqueeze(1).to_broadcast([P, HALF, L]),
                                               bc(chunk1[:, col], L), ALU.is_equal))
                    if half:
                        V.tensor_tensor(olane1[:, half, :, :], iota16[:, 0:P].unsqueeze(1).to_broadcast([P, HALF, P]),
                                        bc(lane1[:, col], P), ALU.is_equal)
                    steps.wait()
                    view = pay_oh[:, half, :, :].rearrange("p c (v l) -> p c v l", v=2)
                    for v in range(2):
                        last = V.tensor_tensor(view[:, :, v, :], ochunk[:, half, :, :], bc(payload[:, v, col], L), ALU.mult)
                    last.then_inc(S["hots_ready"], 1)
                dve.wait_ge(S["moved_mm"], g + 1)
                V.tensor_scalar(ogc[:, :], iota_k[0:L, :], global_chunk[0:L, 2, ds(g, 1)], None, ALU.is_equal).then_inc(S["ogc_ready"], 1)
                steps.leave(NG)
            dve.wait_ge(S["moved_all"], 1)
            steps.mark(V.tensor_copy(w_s, bank[6][:, 0:K1]))
            steps.done(V.tensor_copy(pack_i, bank[7][:, 0:K1]))
            steps.mark(V.tensor_single_scalar(idx_s, pack_i, 7, ALU.logical_shift_right))
            steps.done(V.tensor_single_scalar(pack_i, pack_i, P - 1, ALU.bitwise_and))
            steps.done(V.tensor_copy(loc_s, pack_i))
            dve.nop().then_inc(S["edges_ready"], 1)

            def dest_hots(turn, u):
                c = ds(turn * U + u, 1)
                V.tensor_scalar(S1[:, u, :], iota_k[:, 0:P], loc_s[:, c], w_s[:, c], ALU.is_equal, ALU.mult).then_inc(S["onehot_ready"], 1)

            def tiles_of(turn):
                return nc.values_load_multi_w_load_instructions(
                    tile_of_chunk[0:1, ds(turn * U, U)], engines=[mybir.EngineType.DVE], min_val=0, max_val=NT - 1,
                    skip_runtime_bounds_check_because="a count of buckets, of which the smaller of it and NT - 1 was taken")[1]

            def sum_chunk(turn, tiles, u, last=False):
                dve.wait_ge(S["slots_free"], U + turn * U + (u + 1))
                dve.wait_ge(S["agg_free"], AGG + turn * U + u)
                acc = xs[:, ds(tiles[u], 1), :].rearrange("p a d -> p (a d)")
                V.tensor_tensor(acc, acc, agg_bank(u), ALU.add).then_inc(S["agg_free"], 1)
                if not last:
                    dest_hots(turn + 1, u)

            for u in range(U):
                dest_hots(0, u)
            tot2, base2 = bucket[:, 0, :], bucket[:, 1, :]
            dve.wait_ge(S["cnt_copied"], NG + 1)
            tiles = tiles_of(0)
            for u in range(U):
                sum_chunk(0, tiles, u)
                if u < NT // T5:
                    some = slice(u * T5, (u + 1) * T5)
                    steps.mark(V.tensor_reduce(tot2[:, some], CT[:, :, some].rearrange("p c t -> p t c"), AX, ALU.add))
                if u == NT // T5 - 1:
                    steps.wait()
                    dve.nop().then_inc(S["tot2_ready"], 1)
            dve.wait_ge(S["base2_mm"], 1)
            steps.done(V.tensor_copy(bucket[:, 2, :], bank[3][:, 0:NT]))
            steps.done(V.tensor_tensor_scan(bucket[:, 3, :], ones[:, 0:NT], bucket[:, 2, :], 0.0, ALU.mult, ALU.add))
            steps.done(V.tensor_tensor(base2, bucket[:, 3, :], bucket[:, 2, :], ALU.subtract))
            steps.done(V.tensor_tensor(base2, base2, bank[2][:, 0:NT], ALU.add))
            steps.done(V.tensor_tensor(bucket[:, 4, :], base2, tot2, ALU.add))
            steps.done(V.tensor_scalar(endpos[:, :], bucket[:, 4, :], 1.0, None, ALU.subtract))
            steps.mark(V.tensor_copy(PT[:, 0, :], base2))
            for turn in range(1, COUNT_TURNS):
                tiles = tiles_of(turn)
                for u in range(U):
                    sum_chunk(turn, tiles, u)
                    for t in range((turn - 1) * U + u, NT, (COUNT_TURNS - 1) * U):
                        steps.mark(V.tensor_tensor_scan(PT[:, 1:C2T + 1, t], ones[:, 0:1].to_broadcast([P, C2T]), CT[:, :, t],
                                                        bucket[:, 1, t:t + 1], ALU.mult, ALU.add))
            steps.wait()

            dve.nop().then_inc(S["places_ready"], 1)

            def rank_turn(i, side):
                k = i * 2 + side
                tiles = tiles_of(k + RANK_0)
                dve.wait_ge(rows_landed[side], i * 16 + 16)
                for u in range(U):
                    sum_chunk(k + RANK_0, tiles, u)
                    for c in range(2 * u, min(2 * u + 2, U2)):
                        last = V.scalar_tensor_tensor(same[:, c, :], rows2[:, side, c, 1, :], keyc2[:, ds(k * U2 + c, 1)], tri16[:, :],
                                                      ALU.is_equal, ALU.mult, accum_out=rank2[:, ds(k * U2 + c, 1)])
                        if c == U2 - 1:
                            last.then_inc(S["ranked"], 1)
                dve.wait_ge(S["r_mm"], k + 1)
                steps.done(V.tensor_tensor(rsel, bank[6 + side][:, 0:U2 * NT].rearrange("p (u t) -> p u t", u=U2),
                                           OH[:, ds(k * U2, U2), :], ALU.mult))
                V.tensor_reduce(pos2[:, ds(k * U2, U2)], rsel, AX, ALU.add).then_inc(S["r_used"], 1)

            with dve.Fori(0, T2 // 2) as i:
                steps.enter(i, 2)
                for side in range(2):
                    rank_turn(i, side)
                steps.leave(T2 // 2)
            dve.wait_ge(S["r_used"], T2 + 2)
            dve.wait_ge(S["ranked"], T2)
            steps.done(V.tensor_tensor(pos2, pos2, rank2[:, :], ALU.add))
            main = slice(0, C2T)
            steps.done(V.tensor_scalar(tmp2, pos2, 1.0 / C2, 0.5 / C2 - 0.5, ALU.mult, ALU.add))
            steps.done(V.tensor_copy(tmp2i, tmp2))
            steps.done(V.tensor_copy(lane2[:, main], tmp2i))
            steps.done(V.scalar_tensor_tensor(col2[:, main], lane2[:, main], -float(C2), pos2, ALU.mult, ALU.add))
            for test, bound, sign in ((ALU.is_lt, 0.0, 1.0), (ALU.is_ge, float(C2), -1.0)):
                steps.done(V.tensor_scalar(tmp2, col2[:, main], bound, None, test))
                steps.mark(V.scalar_tensor_tensor(lane2[:, main], tmp2, -sign, lane2[:, main], ALU.mult, ALU.add))
                steps.done(V.scalar_tensor_tensor(col2[:, main], tmp2, sign * C2, col2[:, main], ALU.mult, ALU.add))
            again = slice(C2T, C2T + LOOPS * U2)
            steps.mark(V.tensor_copy(lane2[:, again], lane2[:, 0:LOOPS * U2]))
            steps.mark(V.tensor_copy(col2[:, again], col2[:, 0:LOOPS * U2]))
            steps.mark(V.memset(src_sorted[:, :], 0))
            tiles = tiles_of(PLACE_TURN)
            for u in range(U):
                sum_chunk(PLACE_TURN, tiles, u)
            steps.wait()

            def move_hots(k, q):
                dve.wait_ge(S["perm_used"], k * SUBS + (q + 1))
                for u in range(q * SUB, (q + 1) * SUB):
                    V.tensor_scalar(ocol[:, u, :], iota16[:, 0:C2], col2[:, ds(k * U2 + u, 1)], None, ALU.is_equal)
                V.tensor_tensor(olane2[:, q * SUB:(q + 1) * SUB, :], iota16[:, 0:P].unsqueeze(1).to_broadcast([P, SUB, P]),
                                lane2[:, ds(k * U2 + q * SUB, SUB)].unsqueeze(2).to_broadcast([P, SUB, P]),
                                ALU.is_equal).then_inc(S["perm_ready"], 1)

            def move_turn(k, last=False):
                tiles = tiles_of(k + MOVE_0)
                for u in range(U):
                    sum_chunk(k + MOVE_0, tiles, u, last)
                    if u in (0, 2, 4):
                        move_hots(k, u // 2)

            with dve.Fori(0, T2 + LOOPS - 1) as i:
                move_turn(i)
            move_turn(T2 + LOOPS - 1, True)
            dve.wait_ge(S["agg_free"], AGG + K1)
            dve.wait_ge(S["perm_mm"], 1)
            steps.mark(V.tensor_copy(starts[:, :], bank[3][:, 0:C2]))
            steps.done(V.tensor_scalar(src_sorted[:, 0:C2], bank[2][:, 0:C2], MIDDLE, None, ALU.add))
            dve.nop().then_inc(S["perm_taken"], 1)

            layer_norm("b")
            dve.wait_ge(S["proj_taken_b"], NT + 2)
            for a in range(2):
                steps.done(V.tensor_tensor(agg[:, :, :], GT[:, 0:NT, 0:CH], att_b[:, a, :].unsqueeze(1).to_broadcast([P, NT, CH]), ALU.mult))
                steps.done(V.tensor_reduce(GT[:, 0:NT, CH + a * HEADS:CH + (a + 1) * HEADS],
                                           agg[:, :, :].rearrange("p t (h e) -> p t h e", e=EX), AX, ALU.add))
            dve.nop().then_inc(S["table_ready"], 1)

            dve.wait_ge(S["table_sent"], 16)
            with dve.Fori(0, C2G // SLOTS) as i:
                for u in range(SLOTS):
                    dve.wait_ge(gat_in[u], i * 16 + 16)
                    V.tensor_copy(GT[:, ds(i * SLOTS + u, 1), :].rearrange("p a r -> p (a r)"), gat_slot[:, u, :]).then_inc(S["gat_free"], 1)
            dve.wait_ge(S["gat_free"], SLOTS + C2G)
            steps.mark(V.tensor_scalar(keep, starts[:, :], -1.0, 1.0, ALU.mult, ALU.add))
            steps.mark(V.tensor_scalar(drop_f, starts[:, :], -BIG, None, ALU.mult))
            steps.mark(V.tensor_scalar(drop_r[:, 0:C2 - 1], starts[:, 1:C2], -BIG, None, ALU.mult))
            steps.mark(V.memset(drop_r[:, C2 - 1:C2], 0.0))
            steps.done(V.tensor_reduce(flag_any[:, 0:1], starts[:, :], AX, ALU.max))
            steps.mark(V.tensor_scalar(flag_any[:, 1:2], flag_any[:, 0:1], -1.0, 1.0, ALU.mult, ALU.add))
            steps.done(V.tensor_scalar(flag_any[:, 2:3], flag_any[:, 0:1], -BIG, None, ALU.mult))
            steps.done(V.memset(across[:, 2, :], 0.0))

            turns = [0]

            def over_partitions(k, last_cols, flag, op0, op1, nothing, reverse):
                q = turns[0]
                turns[0] += 1
                steps.mark(V.tensor_copy(edge_cols[:, 0, 0:k], last_cols))
                steps.done(V.tensor_copy(edge_cols[:, 1, 0:k], flag_any[:, flag:flag + 1].to_broadcast([P, k])))
                dve.nop().then_inc(S["cols_ready"], 1)
                dve.wait_ge(S["cols_T"], q + 1)
                steps.mark(V.tensor_copy(across[0:k, 0, 0:P], bank[0][0:k, 0:P]))
                steps.mark(V.tensor_copy(across[0:k, 1, 0:P], bank[0][0:k, P:2 * P]))
                edge = P if reverse else 0
                steps.done(V.memset(across[0:k, 2, edge:edge + 1], nothing))
                o = across[0:k, 2, 0:P][:, ::-1] if reverse else across[0:k, 2, 1:P + 1]
                l, f = across[0:k, 0, 0:P], across[0:k, 1, 0:P]
                if reverse:
                    l, f = l[:, ::-1], f[:, ::-1]
                steps.done(V.tensor_tensor_scan(o, f, l, nothing, op0, op1))
                dve.nop().then_inc(S["across_ready"], 1)
                dve.wait_ge(S["across_T"], q + 1)
                steps.done(V.tensor_copy(carry[:, 0, 0:k], bank[1][:, 0:k]))

            steps.done(V.tensor_tensor(s_e, GT[:, 0:C2, CH + HEADS:ROW].rearrange("p c h -> p h c"),
                                       starts[:, :].unsqueeze(1).to_broadcast([P, HEADS, C2]), ALU.mult))

            def spread(initial):
                for h in range(HEADS):
                    steps.mark(V.tensor_tensor_scan(ad_e[:, h, :], keep, s_e[:, h, :], initial(h), ALU.mult, ALU.add))
                steps.wait()

            spread(lambda h: 0.0)
            over_partitions(HEADS, ad_e[:, :, C2 - 1], 1, ALU.mult, ALU.add, 0.0, False)
            spread(lambda h: carry[:, 0, h:h + 1])
            steps.done(V.tensor_tensor(e_e, GT[:, 0:C2, CH:CH + HEADS].rearrange("p c h -> p h c"), ad_e, ALU.add))
            flat_e = e_e.rearrange("p h c -> p (h c)")
            steps.done(V.scalar_tensor_tensor(flat_e, flat_e, 0.2, flat_e, ALU.mult, ALU.max))

            def scan_max(o, flags, initial, reverse):
                for h in range(HEADS):
                    a, b, c = o[:, h, :], flags, e_e[:, h, :]
                    if reverse:
                        a, b, c = a[:, ::-1], b[:, ::-1], c[:, ::-1]
                    steps.mark(V.tensor_tensor_scan(a, b, c, initial(h), ALU.add, ALU.max))
                steps.wait()

            scan_max(f_e, drop_f, lambda h: -BIG, False)
            over_partitions(HEADS, f_e[:, :, C2 - 1], 2, ALU.add, ALU.max, -BIG, False)
            scan_max(f_e, drop_f, lambda h: carry[:, 0, h:h + 1], False)
            scan_max(s_e, drop_r, lambda h: -BIG, True)
            steps.done(V.tensor_scalar(carry[:, 1, 0:HEADS], s_e[:, :, 0], drop_f[:, 0:1], None, ALU.add))
            over_partitions(HEADS, carry[:, 1, 0:HEADS], 2, ALU.add, ALU.max, -BIG, True)
            scan_max(s_e, drop_r, lambda h: carry[:, 0, h:h + 1], True)
            flat_f, flat_s = f_e.rearrange("p h c -> p (h c)"), s_e.rearrange("p h c -> p (h c)")
            steps.done(V.tensor_tensor(flat_f, flat_f, flat_s, ALU.max))
            steps.done(V.tensor_tensor(flat_e, flat_e, flat_f, ALU.subtract))
            dve.nop().then_inc(S["exp_in"], 1)
            dve.wait_ge(S["exp_out"], 1)
            steps.mark(V.tensor_copy(V20[:, 0:HEADS, :], e_e))
            for h in range(HEADS):
                steps.mark(V.tensor_tensor(V20[:, HEADS + h * EX:HEADS + (h + 1) * EX, :],
                                           GT[:, 0:C2, h * EX:(h + 1) * EX].rearrange("p c e -> p e c"),
                                           e_e[:, h:h + 1, :].to_broadcast([P, EX, C2]), ALU.mult))
            steps.wait()

            def scan_sums(initial):
                for s in range(NS):
                    steps.mark(V.tensor_tensor_scan(VS[:, :, s], keep, V20[:, s, :], initial(s), ALU.mult, ALU.add))
                steps.wait()

            scan_sums(lambda s: 0.0)
            over_partitions(NS, VS[:, C2 - 1, :], 1, ALU.mult, ALU.add, 0.0, False)
            scan_sums(lambda s: carry[:, 0, s:s + 1])
            dve.nop().then_inc(S["sums_ready"], 1)
            dve.wait_ge(sums_in, 16 * NT)
            den = node_sums[:, :, 0:HEADS]
            steps.done(V.tensor_scalar(den, den, 1e-16, None, ALU.add))
            steps.done(V.reciprocal(den, den))
            steps.done(V.tensor_tensor(agg[:, :, :].rearrange("p t (h e) -> p t h e", e=EX),
                                       node_sums[:, :, HEADS:NS].rearrange("p t (h e) -> p t h e", e=EX),
                                       den.unsqueeze(3).to_broadcast([P, NT, HEADS, EX]), ALU.mult))

            def row(i):
                return gam_b[:, i, :].unsqueeze(1).to_broadcast([P, NT, CH])

            def node(v):
                return v.unsqueeze(2).to_broadcast([P, NT, CH])

            steps.done(V.tensor_tensor(agg[:, :, :], agg[:, :, :], row(2), ALU.add))
            steps.done(V.tensor_reduce(pair[:, 4, :], agg[:, :, :], AX, ALU.add))
            steps.done(V.tensor_scalar(pair[:, 4, :], pair[:, 4, :], 1.0 / CH, None, ALU.mult))
            steps.done(V.tensor_tensor(agg[:, :, :], agg[:, :, :], node(pair[:, 4, :]), ALU.subtract))
            steps.done(V.tensor_tensor(agg2[:, :, :], agg[:, :, :], agg[:, :, :], ALU.mult))
            steps.done(V.tensor_reduce(pair[:, 5, :], agg2[:, :, :], AX, ALU.add))
            steps.done(V.tensor_scalar(pair[:, 5, :], pair[:, 5, :], 1.0 / CH, None, ALU.mult))
            inverse_deviation(pair, pair[:, 5, :], "c")
            steps.done(V.tensor_tensor(agg[:, :, :], agg[:, :, :], node(pair[:, 3, :]), ALU.mult))
            steps.done(V.tensor_tensor(agg[:, :, :], agg[:, :, :], row(0), ALU.mult))
            steps.done(V.tensor_tensor(agg[:, :, :], agg[:, :, :], row(1), ALU.add))
            steps.done(V.tensor_reduce(sc4[:, :, :].rearrange("p e t -> p t e"),
                                       agg[:, :, :].rearrange("p t (h e) -> p t e h", e=EX), AX, ALU.add))
            flat4 = sc4[:, :, :].rearrange("p e t -> p (e t)")
            steps.done(V.tensor_scalar(flat4, flat4, 1.0 / HEADS, None, ALU.mult))
            steps.done(V.memset(rank4[:, :, :], 0.0))
            for a in range(EX):
                for b in range(a + 1, EX):
                    steps.done(V.tensor_tensor(pair[:, 0, :], sc4[:, a, :], sc4[:, b, :], ALU.is_ge))
                    steps.mark(V.tensor_tensor(rank4[:, b, :], rank4[:, b, :], pair[:, 0, :], ALU.add))
                    steps.mark(V.scalar_tensor_tensor(rank4[:, a, :], rank4[:, a, :], 1.0, pair[:, 0, :], ALU.add, ALU.subtract))
                    steps.wait()
            flat_r = rank4[:, :, :].rearrange("p e t -> p (e t)")
            steps.done(V.tensor_scalar(flat_r, flat_r, 2.0, None, ALU.is_lt))
            steps.done(V.tensor_reduce(pair[:, 1, :], sc4[:, :, :].rearrange("p e t -> p t e"), AX, ALU.max))
            steps.done(V.tensor_tensor(gate[:, :, :], sc4[:, :, :], pair[:, 1, :].unsqueeze(1).to_broadcast([P, EX, NT]), ALU.subtract))
            dve.nop().then_inc(S["wexp_in"], 1)
            dve.wait_ge(S["wexp_out"], 1)
            steps.done(V.tensor_tensor(gate[:, :, :], gate[:, :, :], rank4[:, :, :], ALU.mult))
            steps.done(V.tensor_reduce(pair[:, 2, :], gate[:, :, :].rearrange("p e t -> p t e"), AX, ALU.add))
            steps.done(V.reciprocal(pair[:, 3, :], pair[:, 2, :]))
            steps.done(V.tensor_tensor(gate[:, :, :], gate[:, :, :], pair[:, 3, :].unsqueeze(1).to_broadcast([P, EX, NT]), ALU.mult))
            dve.nop().then_inc(S["gate_ready"], 1)

            for t in range(NT):
                dve.wait_ge(S["gate_T"], t + 1)
                V.tensor_copy(gT[:, t % 2, :], bank[2][0:EX, 0:P]).then_inc(S["gate_T_copied"], 1)
                dve.wait_ge(y_loaded[t % 3], 16 * (t // 3 + 1))
                for e in range(EX):
                    steps.done(V.scalar_tensor_tensor(xs[:, t, :], y_in[:, t % 3, e, :], gate[:, e, t:t + 1], xs[:, t, :],
                                                      ALU.mult, ALU.add))
                dve.nop().then_inc(S["y_used"], 1)
                dve.wait_ge(S["gb_mm"], t + 1)
                steps.done(V.tensor_tensor(xs[:, t, :], xs[:, t, :], bank[3 + t % 2][:, 0:D], ALU.add))
                dve.nop().then_inc(S["gb_used"], 1)
                dve.nop().then_inc(S["out_ready"], 1)


_NAMES = ["x", "src", "dst", "edge_weight", "L0_gnn_W", "L0_gnn_bias", "L0_ffn_W_gat", "L0_ffn_att_src", "L0_ffn_att_dst",
          "L0_ffn_b_gat", "L0_ffn_ln_gamma", "L0_ffn_ln_beta", "L0_ffn_W1", "L0_ffn_b1", "L0_ffn_W2", "L0_ffn_b2",
          "L0_ffn_edge_index"]


def kernel(**inputs):
    import numpy as _np
    import concourse.bacc as _bacc
    from concourse import mybir as _mybir
    from concourse.bass_utils import run_bass_kernel_spmd as _run

    nc = _bacc.Bacc("TRN2", target_bir_lowering=False, num_devices=1)
    arrays, args = {}, []
    for name in _NAMES:
        a = _np.ascontiguousarray(inputs[name])
        arrays[f"in_{name}"] = a
        args.append(nc.dram_tensor(f"in_{name}", a.shape, _mybir.dt.from_np(a.dtype), kind="ExternalInput").ap())
    shape = inputs["x"].shape
    args.append(nc.dram_tensor("out_rows", shape, _mybir.dt.float32, kind="ExternalOutput").ap())
    gnn_moe_kernel(nc, *args)
    return _run(nc, [arrays], core_ids=[0]).results[0]["out_rows"]
```

```python
import concourse.bass as bass
from concourse import mybir
from contextlib import ExitStack

P = 128


class Steps:

    def __init__(self, engine, sem):
        self.engine, self.sem, self.value, self.offset = engine, sem, 0, 0

    def mark(self, instruction):
        self.value += 1
        instruction.then_inc(self.sem, 1)

    def wait(self):
        self.engine.wait_ge(self.sem, self.value + self.offset)

    def wait_but_last(self):
        self.engine.wait_ge(self.sem, self.value + self.offset - 1)

    def done(self, instruction):
        self.mark(instruction)
        self.wait()

    def enter(self, index, per_turn):
        self.begun, self.per_turn, self.offset = self.value, per_turn, index * per_turn

    def leave(self, turns):
        assert self.value == self.begun + self.per_turn, self.value - self.begun
        self.value, self.offset = self.begun + turns * self.per_turn, 0


def gnn_moe_kernel(nc, x, src, dst, edge_weight, W, bias, W_gat, att_src, att_dst, b_gat,
                   ln_gamma, ln_beta, W1, b1, W2, b2, edge_index, out):
    F32, I32, F16, BF16 = mybir.dt.float32, mybir.dt.int32, mybir.dt.float16, mybir.dt.bfloat16
    ALU, ACT, AX = mybir.AluOpType, mybir.ActivationFunctionType, mybir.AxisListType.X
    ds = bass.ds

    N, D = x.shape
    KD = D // P
    NT = -(-N // P)
    N_LAST = N - (NT - 1) * P
    NP_ = NT * P
    E1 = src.shape[0]
    HALF = 13
    G = 2 * HALF
    NG = -(-E1 // (P * G))
    C1 = NG * G
    E1_LAST = E1 - (P - 1) * C1
    U = 8
    K1 = -(-((P * C1 + (P - 1) * NT) // P) // U) * U
    L = -(-(P * G + 2 * (P - 1) * NT) // P // 2) * 2
    EX, _, HID = W1.shape
    KH = HID // P
    HEADS = att_src.shape[0]
    CH = HEADS * EX
    ROW = CH + 2 * HEADS
    E2 = edge_index.shape[1]
    C2E = E2 // P
    C2 = NT + C2E
    U2 = 12
    T2 = -(-C2 // U2)
    C2T = T2 * U2
    CG = -(-C2T // NG)
    SUB = 4
    SUBS = U2 // SUB
    LOOPS = -(-NT // U2)
    COUNT_TURNS = 3
    RANK_0 = COUNT_TURNS
    PLACE_TURN = RANK_0 + T2
    MOVE_0 = PLACE_TURN + 1
    MARK_0 = MOVE_0 + T2
    SLOTS = 6
    C2G = -(-C2 // SLOTS) * SLOTS
    NS = CH + HEADS
    T5 = 5
    assert NG % 2 == 0 and T2 % 2 == 0 and C2T % 3 == 0 and CG * NG == C2T and K1 // U == MARK_0 + LOOPS
    assert U2 % SUB == 0 and CG * NT <= 512
    assert NT % T5 == 0 and P * C2E == E2 and HID % P == 0 and L <= P and 0 < E1_LAST <= C1
    LN_EPS = 1e-5
    BIG = 1e30
    MIDDLE = float(NP_ // 2)
    NO_CHUNK = 4096.0
    GROUPS4 = -(-NT // 4)
    BLK = 512
    TB = BLK // P
    NBLK = NT // TB
    assert NT == NBLK * TB + 1 and NP_ // 2 <= 2048

    ctx = ExitStack()
    with ctx:
        def sb(name, shape, dt=F32):
            return ctx.enter_context(nc.sbuf_tensor(name, shape, dt))

        def sem(name):
            return ctx.enter_context(nc.semaphore(name))

        h_dram = nc.dram_tensor("h_rows", [NP_, D], F32, kind="Internal").ap()
        gat_dram = nc.dram_tensor("gat_rows", [NP_, ROW], F32, kind="Internal").ap()
        sums_dram = nc.dram_tensor("gat_sums", [P * C2, NS], F32, kind="Internal").ap()
        rows_dram = nc.dram_tensor("gat_key_rows", [C2T, 2, P], F16, kind="Internal").ap()
        y_dram = nc.dram_tensor("expert_rows", [NP_, EX, D], F32, kind="Internal").ap()

        xs = sb("xs", [P, NT, D])
        big_t = sb("big_t", [P, KD * NP_])
        big_w = sb("big_w", [P, 2 * EX * KD * HID])
        big_h = sb("big_h", [P, 2 * KH * BLK])
        big_g = sb("big_g", [P, max(C2G * ROW, (C2T + 1) * NT)])
        big_y = sb("big_y", [P, 2 * TB * D])
        REGION = max(4 * K1 + 9 * C1, (4 * HEADS + 3) * C2)
        region = sb("region", [P, REGION])

        def part(place, start, shape, dt=F32):
            n = 1
            for s in shape:
                n *= s
            words = n if dt in (F32, I32) else -(-n // 2)
            assert start + words <= place.shape[1], (place.shape, start, shape)
            v = place[:, start:start + words]
            if dt is not F32:
                v = v.bitcast(dt)
            if len(shape) == 2:
                v = v.rearrange("p (a b) -> p a b", b=shape[1])
            elif len(shape) == 3:
                v = v.rearrange("p (a b c) -> p a b c", b=shape[1], c=shape[2])
            return v, start + words

        xT, _ = part(big_t, 0, [KD, NP_])
        ind5, n_ = part(big_t, 0, [T5, C1])
        at5, n_ = part(big_t, n_, [T5, C1])
        in5, n_ = part(big_t, n_, [T5, C1])
        rows2, n_ = part(big_t, 0, [2, U2, 2 * P], F16)
        rows2 = rows2.rearrange("p s u (v e) -> p s u v e", v=2)
        olT0, n_ = part(big_t, n_, [U2, P])
        rsel, n_ = part(big_t, n_, [U2, NT])
        same, n_ = part(big_t, n_, [U2, P], F16)
        ocol, n_ = part(big_t, 0, [U2, C2], F16)
        olane2, n_ = part(big_t, n_, [U2, P], F16)
        oval2, n_ = part(big_t, n_, [U2, P], F16)
        V20, _ = part(big_t, 0, [NS, C2])
        W1_sb, n_ = part(big_w, 0, [KD, EX, HID])
        W2_sb, _ = part(big_w, n_, [EX, KH, D])
        cum1, _ = part(big_w, 0, [NT, C1], F16)
        OH, n_ = part(big_w, 0, [C2T, NT], BF16)
        CT, n_ = part(big_w, n_, [C2T, NT], BF16)
        TK = C2T // 3
        key_rows, _ = part(big_w, n_, [3, 2 * P], F16)
        key_rows = key_rows.rearrange("p b (v e) -> p b v e", v=2)[0:TK, :, :, :]
        VS, _ = part(big_w, 0, [C2, NS])
        h_ff, _ = part(big_h, 0, [2, KH, BLK])
        olane1, _ = part(big_h, 0, [2, HALF, P])
        GT, _ = part(big_g, 0, [C2G, ROW])
        ochunk, n_ = part(big_g, 0, [2, HALF, L])
        pay_oh, n_ = part(big_g, n_, [2, HALF, 2 * L])
        PT, _ = part(big_g, 0, [C2T + 1, NT])
        y_sb, _ = part(big_y, 0, [2, TB * D])
        y_sb = y_sb.rearrange("p s (t d) -> p s t d", d=D)
        h_out, _ = part(big_y, 0, [T5, D])
        olT = (olT0, part(big_y, 0, [U2, P])[0])

        idx_s, n_ = part(region, 0, [K1], I32)
        w_s, n_ = part(region, n_, [K1])
        loc_s, n_ = part(region, n_, [K1])
        pack_i, n_ = part(region, n_, [K1], I32)
        n_sorting = n_
        lane1, n_ = part(region, n_, [C1])
        chunk1, n_ = part(region, n_, [C1])
        payload, n_ = part(region, n_, [2, C1])
        n_ranked = n_
        src1, n_ = part(region, n_, [C1], I32)
        dst1, n_ = part(region, n_, [C1], I32)
        tile1, n_ = part(region, n_, [C1])
        place1, n_ = part(region, n_, [C1])
        tmp1, n_ = part(region, n_, [C1], I32)
        ol1, n_ = part(region, n_ranked, [CG, P], BF16)
        lo2, n_ = part(region, n_, [C2T])
        hi2, n_ = part(region, n_, [C2T])
        val2, n_ = part(region, n_, [C2T + LOOPS * U2])
        pos2, n_ = part(region, n_sorting, [C2T])
        lane2, n_ = part(region, n_, [C2T + LOOPS * U2])
        col2, n_ = part(region, n_, [C2T + LOOPS * U2])
        tmp2, n_ = part(region, n_, [C2T])
        tmp2i, n_ = part(region, n_, [C2T], I32)
        ad_e, n_ = part(region, 0, [HEADS, C2])
        e_e, n_ = part(region, n_, [HEADS, C2])
        f_e, n_ = part(region, n_, [HEADS, C2])
        s_e, n_ = part(region, n_, [HEADS, C2])
        keep, n_ = part(region, n_, [C2])
        drop_f, n_ = part(region, n_, [C2])
        drop_r, n_ = part(region, n_, [C2])

        ident = sb("ident", [P, P])
        tri = sb("tri", [P, P])
        ones = sb("ones", [P, P])
        iota16 = sb("iota16", [P, 512], F16)
        iota_k = sb("iota_k", [P, K1])
        iota_p = sb("iota_p", [P, 1])
        first_g, _ = part(big_h, 0, [NT, NG])
        bias_b = sb("bias_b", [P, D])
        w_sb = sb("w_sb", [P, KD, D])
        wgat_sb = sb("wgat_sb", [P, KD, CH])
        att_b = sb("att_b", [P, 2, CH])
        gam_b = sb("gam_b", [P, 3, CH])
        b1_sb = sb("b1_sb", [P, EX, KH])
        b2_sb = sb("b2_sb", [EX, D])
        stats = sb("stats", [P, 2 * T5, 6])
        mv = sb("mv", [P, NT, 2])
        rstd = sb("rstd", [P, 4, NT])
        eps_c = sb("eps_c", [P, 1])
        xn = sb("xn", [P, T5, D])
        xnT = sb("xnT", [P, T5, KD, P])
        bucket = sb("bucket", [P, 6, NT])
        bucket_i = sb("bucket_i", [P, NT], I32)
        global_chunk = sb("global_chunk", [P, 3, NG])
        ogc = sb("ogc", [L, 2, K1])
        keyc2 = sb("keyc2", [P, C2T])
        rank2 = sb("rank2", [P, C2T])
        tri16 = sb("tri16", [P, P], F16)
        lane_now = sb("lane_now", [P, HALF])
        group_sb = sb("group_sb", [P, 2, L])
        group_T = sb("group_T", [L, 2, P])
        zero_row = sb("zero_row", [1, K1])
        end_col = sb("end_col", [NT, 1])
        geq = ogc[0:NT, 0, :]
        tile_of_chunk = sb("tile_of_chunk", [1, K1], I32)
        idx_turn = sb("idx_turn", [P, 2, U], I32)
        big_m = sb("big_m", [P, U * (D + P)])
        msgs, n_ = part(big_m, 0, [U, D])
        S1, _ = part(big_m, n_, [U, P])
        cnt = [part(big_m, i * NT * NG, [NT, NG])[0] for i in range(6)]
        cnt_i, _ = part(big_m, 6 * NT * NG, [NT, NG], I32)
        by_g = [part(big_y, i * NT * NG, [NG, NT])[0] for i in range(3)]
        key2 = sb("key2", [P, C2], I32)
        src2 = sb("src2", [P, C2], I32)
        endpos = sb("endpos", [P, NT], I32)
        starts = sb("starts", [P, C2])
        src_sorted = sb("src_sorted", [P, C2G], I32)
        gat_slot = sb("gat_slot", [P, SLOTS, ROW])
        edge_cols = sb("edge_cols", [P, 2, NS])
        across = sb("across", [NS, 3, P + 1])
        carry = sb("carry", [P, 2, NS])
        flag_any = sb("flag_any", [P, 4])
        key_tile, _ = part(starts, 0, [C2], I32)
        node_sums, n_ = part(big_m, 0, [NT, NS])
        agg, n_ = part(big_m, n_, [NT, CH])
        agg2, n_ = part(big_m, n_, [NT, CH])
        sc4 = sb("sc4", [P, EX, NT])
        gate = sb("gate", [P, EX, NT])
        rank4 = sb("rank4", [P, EX, NT])
        pair = bucket
        gT, n_ = part(big_g, 0, [NT, P])
        gT = gT[0:EX, :, :]
        diag, n_ = part(big_g, n_, [4, P])
        y_in = [part(big_h, i * EX * D, [EX, D])[0] for i in range(4)] + [part(big_w, C2 * NS + i * EX * D, [EX, D])[0] for i in range(2)]
        YS = len(y_in)

        bank = [ctx.enter_context(nc.psum_tensor(f"bank{i}", [P, 512], F32)) for i in range(8)]

        AGG = 4

        def agg_bank(u):
            return bank[(0, 1, 4, 5)[u % AGG]][:, 0:D]

        names = """ld_src ld_dst ld_wt ld_x ld_w ld_keys ld_ffw pads_set consts dve_step pool_step
            counts_ready counts_mm ends_ready ends_mm geq_ready geq_mm
            var_a std_a xn_ready_a xn_T_a xnT_copied_a proj_mm_a proj_taken_a
            var_b std_b xn_ready_b xn_T_b xnT_copied_b proj_mm_b proj_taken_b xT_done
            hots_ready hots_used group_copied group_T_mm group_T_copied ogc_ready moved_mm
            moved_all edges_ready onehot_ready slots_free idx_copied idx_read agg_free
            ranks_done lane_hots_ready keys_ready tile_hots_ready squares_ready ol_ready cnt_mm cnt_copied tot2_ready base2_mm places_ready
            keys_T keys_T_copied key_rows_sent olT_squares olT_ready ranked r_mm r_used
            lanes_ready lane_squares lane_hots perm_ready perm_scaled perm_used perm_mm perm_taken
            table_ready table_sent gat_free gat_idx_copied gat_idx_read
            up_mm up_free down_mm down_taken y_ready
            cols_ready cols_T across_ready across_T exp_in exp_out
            sums_ready sums_sent var_c std_c wexp_in wexp_out
            gate_ready gate_T gate_T_copied diag_ready gb_mm gb_used out_ready out_sent""".split()
        S = {n: sem(n) for n in names}
        h_sent = [sem(f"h_sent{u}") for u in range(T5)]
        gathered = [sem(f"gathered{u}") for u in range(U)]
        gat_in = [sem(f"gat_in{u}") for u in range(SLOTS)]
        y_stored = [sem(f"y_stored{s}") for s in range(2)]
        rows_landed = [sem(f"rows_landed{s}") for s in range(2)]
        y_loaded = [sem(f"y_loaded{s}") for s in range(YS)]
        sums_in = sem("sums_in")

        block = ctx.enter_context(nc.Block())

        @block.sync
        def _(sp):
            sp.wait_ge(S["pads_set"], 1)
            for place, array, landed in ((src1, src, "ld_src"), (dst1, dst, "ld_dst"),
                                         (payload[:, 0, :], edge_weight, "ld_wt")):
                sp.dma_start(place[0:P - 1, :], array[0:(P - 1) * C1].rearrange("(p c) -> p c", c=C1)).then_inc(S[landed], 16)
                sp.dma_start(place[P - 1:P, 0:E1_LAST], array[(P - 1) * C1:E1].rearrange("(p c) -> p c", p=1)).then_inc(S[landed], 16)
            sp.dma_start(xs[:, 0:NT - 1, :], x[0:(NT - 1) * P, :].rearrange("(t p) d -> p t d", p=P)).then_inc(S["ld_x"], 16)
            sp.dma_start(xs[0:N_LAST, NT - 1, :], x[(NT - 1) * P:N, :]).then_inc(S["ld_x"], 16)
            sp.dma_start(w_sb[:, :, :], W.rearrange("(k p) n -> p k n", p=P)).then_inc(S["ld_w"], 16)
            sp.dma_start(wgat_sb[:, :, :], W_gat.rearrange("(k p) n -> p k n", p=P)).then_inc(S["ld_w"], 16)
            sp.dma_start(bias_b[:, :], bias.unsqueeze(0).to_broadcast([P, D])).then_inc(S["ld_w"], 16)
            for i, v in enumerate((att_src, att_dst)):
                sp.dma_start(att_b[:, i, :], v.rearrange("h e -> (h e)").unsqueeze(0).to_broadcast([P, CH])).then_inc(S["ld_w"], 16)
            for i, v in enumerate((ln_gamma, ln_beta, b_gat)):
                sp.dma_start(gam_b[:, i, :], v.unsqueeze(0).to_broadcast([P, CH])).then_inc(S["ld_w"], 16)
            with nc.allow_non_contiguous_dma(reason="2048 bias words, once"):
                for e in range(EX):
                    sp.dma_start(b1_sb[:, e, :], b1[e, :].rearrange("(j p) -> p j", p=P)).then_inc(S["ld_w"], 16)
            sp.dma_start(b2_sb[:, :], b2).then_inc(S["ld_w"], 16)
            sp.dma_start(key2[:, NT:C2], edge_index[1, :].rearrange("(p c) -> p c", c=C2E)).then_inc(S["ld_keys"], 16)
            sp.dma_start(src2[:, NT:C2], edge_index[0, :].rearrange("(p c) -> p c", c=C2E)).then_inc(S["ld_keys"], 16)
            with sp.Fori(0, NT // T5) as i:
                for u in range(T5):
                    sp.wait_ge(S["proj_taken_a"], 2 + i * T5 + (u + 1))
                    sp.dma_start(h_dram[ds((i * T5 + u) * P, P), :], h_out[:, u, :]).then_inc(h_sent[u], 16)
            sp.wait_ge(S["keys_T_copied"], 6)
            sp.dma_start(rows_dram.rearrange("(b c) v e -> c b v e", b=3), key_rows[:, :, :, :]).then_inc(S["key_rows_sent"], 16)
            sp.wait_ge(S["key_rows_sent"], 16)
            sp.wait_ge(S["moved_all"], 1)
            def load_rows(k, side):
                sp.dma_start(rows2[:, side, :, :, :], rows_dram[ds(k * U2, U2), :, :].unsqueeze(0).to_broadcast([P, U2, 2, P])
                             ).then_inc(rows_landed[side], 16)

            for side in range(2):
                load_rows(side, side)
            with sp.Fori(1, T2 // 2) as i:
                for side in range(2):
                    sp.wait_ge(S["ranked"], i * 2 + side - 1)
                    sp.wait_ge(S["olT_ready"], i * 2 + side - 1)
                    load_rows(i * 2 + side, side)
            sp.wait_ge(S["perm_taken"], 1)
            for e in range(EX):
                sp.dma_start(W1_sb[:, :, e, :], W1[e, :, :].rearrange("(k p) n -> p k n", p=P)).then_inc(S["ld_ffw"], 16)
                sp.dma_start(W2_sb[:, e, :, :], W2[e, :, :].rearrange("(k p) n -> p k n", p=P)).then_inc(S["ld_ffw"], 16)
            sp.wait_ge(S["table_ready"], 1)
            sp.dma_start(gat_dram.rearrange("(t p) r -> p t r", p=P), GT[:, 0:NT, :]).then_inc(S["table_sent"], 16)

            def store_y(tile0, tiles, e, nth):
                sp.wait_ge(S["y_ready"], nth)
                sp.dma_start(y_dram[ds(tile0 * P, tiles * P), e, :].rearrange("(t p) d -> p t d", p=P),
                             y_sb[:, e % 2, 0:tiles, :]).then_inc(y_stored[e % 2], 16)

            with sp.Fori(0, NBLK) as i:
                for e in range(EX):
                    store_y(i * TB, TB, e, i * EX + (e + 1))
            for e in range(EX):
                store_y(NBLK * TB, 1, e, NBLK * EX + e + 1)
            for s in range(2):
                sp.wait_ge(y_stored[s], 16 * (EX // 2) * (NBLK + 1))
            sp.wait_ge(S["down_mm"], 2 * TB + EX * (NBLK * TB + 1))

            def load_y(t):
                sp.dma_start(y_in[t % YS], y_dram[t * P:(t + 1) * P, :, :]).then_inc(y_loaded[t % YS], 16)

            for t in range(YS):
                load_y(t)
            sp.wait_ge(S["sums_ready"], 1)
            sp.dma_start(sums_dram.rearrange("(p c) s -> p (c s)", p=P), VS.rearrange("p c s -> p (c s)")).then_inc(S["sums_sent"], 16)
            for t in range(NT):
                sp.wait_ge(S["out_ready"], t + 1)
                rows = P if t < NT - 1 else N_LAST
                sp.dma_start(out[t * P:t * P + rows, :], xs[0:rows, t, :]).then_inc(S["out_sent"], 16)
                if t + YS < NT:
                    load_y(t + YS)
            sp.wait_ge(S["out_sent"], 16 * NT)

        @block.gpsimd
        def _(pool):
            steps = Steps(pool, S["pool_step"])
            steps.mark(pool.memset(xs[:, NT - 1, :], 0.0))
            for v in (src1, dst1, payload[:, 0, :]):
                steps.mark(pool.memset(v, 0))
            steps.wait()
            pool.nop().then_inc(S["pads_set"], 1)
            steps.mark(pool.memset(ident[:, :], 0.0))
            steps.mark(pool.memset(ones[:, :], 1.0))
            steps.mark(pool.memset(tri[:, :], 1.0))
            steps.mark(pool.memset(first_g[:, :, :], 1.0))
            steps.mark(pool.memset(zero_row[:, :], 0.0))
            steps.mark(pool.memset(eps_c[:, :], LN_EPS))
            for v, pattern, cm in ((iota16[:, :], [[1, 512]], 0), (iota_k[:, :], [[1, K1]], 0), (iota_p[:, :], [[0, 1]], 1)):
                steps.mark(pool.iota(v, pattern=pattern, base=0, channel_multiplier=cm, allow_small_or_imprecise_dtypes=True))
            steps.wait()
            steps.mark(pool.memset(first_g[:, :, 0:1], 0.0))
            steps.mark(pool.affine_select(out=ident[:, :], in_=ident[:, :], compare_op=ALU.not_equal, fill=1.0, base=0,
                                          pattern=[[-1, P]], channel_multiplier=1))
            steps.mark(pool.affine_select(out=tri[:, :], in_=tri[:, :], compare_op=ALU.is_gt, fill=0.0, base=0,
                                          pattern=[[1, P]], channel_multiplier=-1))
            steps.mark(pool.iota(key2[:, 0:NT], pattern=[[P, NT]], base=0, channel_multiplier=1))
            steps.mark(pool.iota(src2[:, 0:NT], pattern=[[P, NT]], base=0, channel_multiplier=1))
            steps.wait()
            steps.done(pool.memset(tri16[:, :], 1.0))
            steps.done(pool.affine_select(out=tri16[:, :], in_=tri16[:, :], compare_op=ALU.is_gt, fill=0.0, base=0,
                                          pattern=[[-1, P]], channel_multiplier=1))
            pool.nop().then_inc(S["consts"], 1)

            pool.wait_ge(S["ranks_done"], 1)
            pool.wait_ge(S["ld_keys"], 32)
            steps.mark(pool.memset(lo2, -1.0))
            steps.mark(pool.memset(hi2, -1.0))
            steps.mark(pool.memset(val2, 0.0))
            steps.wait()
            steps.mark(pool.tensor_copy(lo2[:, 0:C2], key2[:, :]))
            steps.mark(pool.memset(keyc2[:, :], 0.0))
            steps.mark(pool.tensor_copy(hi2[:, 0:C2], key_tile))
            steps.mark(pool.tensor_scalar(val2[:, 0:C2], src2[:, :], MIDDLE, None, ALU.subtract))
            steps.wait()
            steps.done(pool.tensor_scalar(keyc2[:, 0:C2], hi2[:, 0:C2], float(P), MIDDLE, ALU.mult, ALU.subtract))
            steps.mark(pool.tensor_tensor(keyc2[:, 0:C2], keyc2[:, 0:C2], lo2[:, 0:C2], ALU.add))
            steps.mark(pool.memset(val2[:, C2T:C2T + NT], 1.0))
            steps.wait()
            pool.nop().then_inc(S["keys_ready"], 1)
            for t in range(NT):
                steps.mark(pool.tensor_scalar(OH[:, :, t], hi2, float(t), None, ALU.is_equal))
            steps.wait()
            pool.nop().then_inc(S["tile_hots_ready"], 1)
            with pool.Fori(0, NG) as g:
                pool.wait_ge(S["hots_used"], g * 2 + 1)
                steps.enter(g, 1)
                steps.done(pool.tensor_copy(lane_now[:, :], lane1[:, ds(g * G, HALF)]))
                steps.leave(NG)
                pool.nop(nofuse=True)
                for c in range(HALF):
                    last = pool.tensor_scalar(olane1[:, 0, c, :], iota_k[:, 0:P], lane_now[:, c:c + 1], None, ALU.is_equal)
                last.then_inc(S["lane_hots_ready"], 1)

            pool.wait_ge(S["edges_ready"], 1)
            for u in range(T5):
                pool.wait_ge(h_sent[u], 16 * (NT // T5))
            def gather_turn(turn, side, slots, rows, numbers, table, free, copied, landed):
                pool.tensor_copy(idx_turn[:, side, 0:slots], numbers[:, ds(turn * slots, slots)]).then_inc(copied, 1)
                pool.wait_ge(copied, turn + 1)
                for u in range(slots):
                    pool.wait_ge(free, turn * slots + (u + 1))
                    pool.nop(nofuse=True)
                    pool.indirect_dma_start(rows[:, u, :], None, table,
                                            bass.IndirectOffsetOnAxis(ap=idx_turn[:, side, u:u + 1], axis=0)).then_inc(landed[u], 16)

            def gather_all(turns, *how):
                with pool.Fori(0, turns // 2) as i:
                    gather_turn(i * 2, 0, *how)
                    gather_turn(i * 2 + 1, 1, *how)
                for turn in range(turns // 2 * 2, turns):
                    gather_turn(turn, 0, *how)

            gather_all(K1 // U, U, msgs, idx_s, h_dram, S["slots_free"], S["idx_copied"], gathered)

            pool.wait_ge(S["slots_free"], U + K1)
            pool.wait_ge(S["perm_taken"], 1)
            pool.wait_ge(S["table_sent"], 16)
            gather_all(C2G // SLOTS, SLOTS, gat_slot, src_sorted, gat_dram, S["gat_free"], S["gat_idx_copied"], gat_in)

            pool.wait_ge(S["sums_sent"], 16)
            for t in range(NT):
                pool.indirect_dma_start(node_sums[:, t, :], None, sums_dram,
                                        bass.IndirectOffsetOnAxis(ap=endpos[:, t:t + 1], axis=0)).then_inc(sums_in, 16)

        def ln_act(act, which):
            out_rows = (lambda i, u: h_out[:, u, :]) if which == "a" else (lambda i, u: GT[:, ds(i * T5 + u, 1), 0:CH])

            def copy(i, u):
                act.wait_ge(S[f"xn_T_{which}"], T5 + i * T5 + (u + 1))
                act.wait_ge(S[f"proj_mm_{which}"], i * T5 + (u + 1))
                if which == "b":
                    act.wait_ge(S["xT_done"], i * T5 + (u + 1))
                view = bank[u][:, 0:D].rearrange("p (k n) -> p k n", k=KD)
                nc.scalar.activation(xnT[:, u, :, :], view, ACT.Copy).then_inc(S[f"xnT_copied_{which}"], 1)

            def take(i, u, first):
                act.wait_ge(S[f"proj_mm_{which}"], T5 + i * T5 + (u + 1))
                if which == "a" and not first:
                    act.wait_ge(h_sent[u], i * 16)
                width = D if which == "a" else CH
                nc.scalar.activation(out_rows(i, u), bank[5 + u % 3][:, 0:width], ACT.Copy).then_inc(S[f"proj_taken_{which}"], 1)

            def turn(i, first=False):
                for u in range(T5 + 1):
                    if u < T5:
                        copy(i, u)
                    if u:
                        take(i, u - 1, first)

            turn(0, True)
            with act.Fori(1, NT // T5) as i:
                turn(i)

        @block.scalar
        def _(act):
            act.nop().then_inc(S["xnT_copied_a"], T5)
            act.nop().then_inc(S["xnT_copied_b"], T5)
            act.nop().then_inc(S["proj_taken_a"], 2)
            act.nop().then_inc(S["proj_taken_b"], 2)
            act.nop().then_inc(S["group_copied"], 2)
            act.nop().then_inc(S["cnt_copied"], 1)
            act.nop().then_inc(S["perm_scaled"], 1)
            act.nop().then_inc(S["up_free"], KH)
            act.nop().then_inc(S["down_taken"], TB)
            act.wait_ge(S["var_a"], 1)
            nc.scalar.activation(rstd[:, 1, :], rstd[:, 0, :], ACT.Sqrt).then_inc(S["std_a"], 1)
            ln_act(act, "a")
            for n in range(6):
                act.wait_ge(S["keys_T"], n + 1)
                nc.scalar.activation(key_rows[:, n // 2, n % 2, :], bank[n][0:TK, 0:P], ACT.Copy).then_inc(S["keys_T_copied"], 1)
            act.wait_ge(S["keys_ready"], 1)

            def group_leaves(g, side):
                act.wait_ge(S["hots_used"], g * 2 + 4)
                act.wait_ge(S["group_T_mm"], g + 1)
                nc.scalar.activation(group_sb[:, :, :], bank[3 + side][:, 0:2 * L].rearrange("p (v l) -> p v l", v=2),
                                     ACT.Copy).then_inc(S["group_copied"], 1)

            def counts_leave(g):
                act.wait_ge(S["cnt_mm"], g + 2)
                nc.scalar.activation(CT[:, ds(g * CG, CG), :], bank[0][:, 0:CG * NT].rearrange("p (u t) -> p u t", u=CG),
                                     ACT.Copy).then_inc(S["cnt_copied"], 1)

            def group_T_leaves(g):
                act.wait_ge(S["group_T_mm"], g + 2)
                act.wait_ge(S["moved_mm"], g + 2)
                nc.scalar.activation(group_T[:, :, :], bank[5][0:L, 0:2 * P].rearrange("p (v l) -> p v l", v=2),
                                     ACT.Copy).then_inc(S["group_T_copied"], 1)

            def squares(g, columns):
                for u in columns:
                    last = nc.scalar.activation(ol1[:, u, :], iota16[:, 0:P], ACT.Square, scale=-1.0, bias=lo2[:, ds(g * CG + u, 1)])
                last.then_inc(S["squares_ready"], 1)

            def sort_turn(g, side, first=False):
                if not first:
                    group_leaves(g - 1, 1 - side)
                    counts_leave(g - 1)
                squares(g, range(CG // 2))
                if not first:
                    group_T_leaves(g - 1)
                squares(g, range(CG // 2, CG))
                act.wait_ge(S["squares_ready"], g * 2 + 2)
                nc.scalar.activation(ol1, ol1, ACT.Relu, scale=-2.0, bias=ones[:, 0:1]).then_inc(S["ol_ready"], 1)

            sort_turn(0, 0, True)
            sort_turn(1, 1)
            with act.Fori(1, NG // 2) as i:
                for side in range(2):
                    sort_turn(i * 2 + side, side)
            group_leaves(NG - 1, 1)
            counts_leave(NG - 1)
            group_T_leaves(NG - 1)
            def row_hots(i, side, first):
                k = i * 2 + side
                act.wait_ge(rows_landed[side], i * 16 + 16)
                if not first:
                    act.wait_ge(S["r_mm"], k - 1)
                nc.scalar.activation(olT[side], rows2[:, side, :, 0, :], ACT.Square, scale=-1.0, bias=iota_p[:, 0:1]).then_inc(S["olT_squares"], 1)
                act.wait_ge(S["olT_squares"], k + 1)
                nc.scalar.activation(olT[side], olT[side], ACT.Relu, scale=-2.0, bias=ones[:, 0:1]).then_inc(S["olT_ready"], 1)

            for u in range(T5):
                act.wait_ge(h_sent[u], 16 * (NT // T5))
            for side in range(2):
                row_hots(0, side, True)
            with act.Fori(1, T2 // 2) as i:
                for side in range(2):
                    row_hots(i, side, False)
            act.wait_ge(S["lanes_ready"], 1)
            with act.Fori(0, T2 + LOOPS) as i:
                act.wait_ge(S["perm_scaled"], i * SUBS + 1)
                for u in range(U2):
                    last = nc.scalar.activation(olane2[:, u, :], iota16[:, 0:P], ACT.Square, scale=-1.0, bias=lane2[:, ds(i * U2 + u, 1)])
                last.then_inc(S["lane_squares"], 1)
                act.wait_ge(S["lane_squares"], i + 1)
                nc.scalar.activation(olane2, olane2, ACT.Relu, scale=-2.0, bias=ones[:, 0:1]).then_inc(S["lane_hots"], 1)
                act.wait_ge(S["lane_hots"], i + 1)
                for q in range(SUBS):
                    act.wait_ge(S["perm_used"], i * SUBS + (q + 1))
                    for u in range(q * SUB, (q + 1) * SUB):
                        last = nc.scalar.activation(oval2[:, u, :], olane2[:, u, :], ACT.Copy, scale=val2[:, ds(i * U2 + u, 1)])
                    last.then_inc(S["perm_scaled"], 1)
            act.wait_ge(S["var_b"], 1)
            nc.scalar.activation(rstd[:, 1, :], rstd[:, 0, :], ACT.Sqrt).then_inc(S["std_b"], 1)
            ln_act(act, "b")

            def hidden(tokens, e, up_before, down_before):
                act.wait_ge(S["down_mm"], 2 * TB + down_before)
                for j in range(KH):
                    act.wait_ge(S["up_mm"], up_before + (j + 1))
                    nc.scalar.activation(h_ff[:, e % 2, j, 0:tokens], bank[j][:, 0:tokens], ACT.Gelu,
                                         bias=b1_sb[:, e, j:j + 1]).then_inc(S["up_free"], 1)

            def rows(tiles, e, down_before, stored_before):
                if stored_before is not None:
                    act.wait_ge(y_stored[e % 2], stored_before)
                for t in range(tiles):
                    act.wait_ge(S["down_mm"], 2 * TB + down_before + (t + 1))
                    nc.scalar.activation(y_sb[:, e % 2, t, :], bank[4 + t][:, 0:D], ACT.Copy).then_inc(S["down_taken"], 1)
                act.wait_ge(S["down_taken"], TB + down_before + tiles)
                act.nop().then_inc(S["y_ready"], 1)

            def block_act(i, first):
                for e in range(EX + 1):
                    if e < EX:
                        hidden(BLK, e, (i * EX + e) * KH, (i * EX + (e - 1)) * TB)
                    if e:
                        stored = None if first and e - 1 < 2 else (i * (EX // 2) + (e - 1) // 2) * 16
                        rows(TB, e - 1, (i * EX + (e - 1)) * TB, stored)

            act.wait_ge(S["ld_w"], 16 * (8 + EX + 1))
            block_act(0, True)
            with act.Fori(1, NBLK) as i:
                block_act(i, False)
            all_before = NBLK * EX * TB
            for e in range(EX + 1):
                if e < EX:
                    hidden(P, e, (NBLK * EX + e) * KH, all_before - TB if e == 0 else all_before + e - 1)
                if e:
                    rows(1, e - 1, all_before + e - 1, (NBLK * (EX // 2) + (e - 1) // 2) * 16)
            act.wait_ge(S["exp_in"], 1)
            nc.scalar.activation(e_e[:, :, :], e_e[:, :, :], ACT.Exp).then_inc(S["exp_out"], 1)
            act.wait_ge(S["var_c"], 1)
            nc.scalar.activation(pair[:, 1, :], pair[:, 0, :], ACT.Sqrt).then_inc(S["std_c"], 1)
            act.wait_ge(S["wexp_in"], 1)
            nc.scalar.activation(gate[:, :, :], gate[:, :, :], ACT.Exp).then_inc(S["wexp_out"], 1)
            act.wait_ge(S["gate_ready"], 1)
            for j in range(GROUPS4):
                tiles = min(4, NT - j * 4)
                act.wait_ge(S["gate_T"], j + 1)
                nc.scalar.activation(gT[:, 4 * j:4 * j + tiles, :],
                                     bank[2 + j % 2][0:EX, 0:tiles * P].rearrange("p (t n) -> p t n", n=P), ACT.Copy).then_inc(S["gate_T_copied"], 1)
                for t in range(4 * j, 4 * j + tiles):
                    if t >= 4:
                        act.wait_ge(S["gb_mm"], t - 3)
                    nc.scalar.activation(diag[:, t % 4, :], ident[:, :], ACT.Copy, scale=gate[:, EX - 1, t:t + 1]).then_inc(S["diag_ready"], 1)

        def ln_pe(pe, which):
            rhs = w_sb if which == "a" else wgat_sb
            width = D if which == "a" else CH

            def transpose(i, u):
                pe.wait_ge(S[f"xn_ready_{which}"], i * T5 + (u + 1))
                pe.wait_ge(S[f"xnT_copied_{which}"], i * T5 + (u + 1))
                for k in range(KD):
                    last = nc.tensor.transpose(bank[u][:, k * P:(k + 1) * P], xn[:, u, k * P:(k + 1) * P], ident[:, :])
                last.then_inc(S[f"xn_T_{which}"], 1)

            def project(i, u):
                pe.wait_ge(S[f"xnT_copied_{which}"], T5 + i * T5 + (u + 1))
                pe.wait_ge(S[f"proj_taken_{which}"], i * T5 + (u + 1))
                for k in range(KD):
                    last = nc.tensor.matmul(bank[5 + u % 3][:, 0:width], xnT[:, u, k, :], rhs[:, k, :],
                                            start=(k == 0), stop=(k == KD - 1))
                last.then_inc(S[f"proj_mm_{which}"], 1)

            with pe.Fori(0, NT // T5) as i:
                for u in range(T5 + 1):
                    if u < T5:
                        transpose(i, u)
                    if u:
                        project(i, u - 1)
            pe.wait_ge(S[f"proj_taken_{which}"], 2 + NT)

        @block.tensor
        def _(pe):
            pe.nop().then_inc(S["xn_T_a"], T5)
            pe.nop().then_inc(S["xn_T_b"], T5)
            pe.nop().then_inc(S["proj_mm_a"], T5)
            pe.nop().then_inc(S["proj_mm_b"], T5)
            pe.nop().then_inc(S["hots_used"], 2)
            pe.nop().then_inc(S["moved_mm"], 2)
            pe.nop().then_inc(S["group_T_mm"], 1)
            pe.nop().then_inc(S["slots_free"], U)
            pe.nop().then_inc(S["cnt_mm"], 1)
            pe.nop().then_inc(S["perm_used"], SUBS)
            pe.nop().then_inc(S["down_mm"], 2 * TB)
            pe.wait_ge(S["consts"], 1)
            pe.wait_ge(S["counts_ready"], 1)
            flat = cnt[0][:, :, :].rearrange("p b g -> p (b g)")
            nc.tensor.matmul(bank[0][:, 0:NT * NG], tri[:, :], flat, start=True, stop=True)
            nc.tensor.matmul(bank[1][:, 0:NT * NG], ones[:, :], flat, start=True, stop=True).then_inc(S["counts_mm"], 1)
            pe.wait_ge(S["ends_ready"], 1)
            nc.tensor.matmul(bank[2][0:NT, 0:1], bucket[0:1, 3, :], ones[0:1, 0:1], start=True, stop=True).then_inc(S["ends_mm"], 1)
            pe.wait_ge(S["geq_ready"], 1)
            nc.tensor.matmul(bank[3][0:1, 0:K1], ones[0:NT, 0:1], geq, start=True, stop=True).then_inc(S["geq_mm"], 1)
            pe.wait_ge(S["ld_w"], 16 * (8 + EX + 1))
            ln_pe(pe, "a")
            pe.wait_ge(S["keys_ready"], 1)
            for n in range(6):
                nc.tensor.transpose(bank[n][0:TK, 0:P], (lo2, keyc2)[n % 2][:, n // 2 * TK:(n // 2 + 1) * TK], ident[:, :]).then_inc(S["keys_T"], 1)
            for v in range(2):
                nc.tensor.matmul(bank[6 + v][:, 0:K1], zero_row[:, 0:P], zero_row[:, :], start=True, stop=False)
            pe.wait_ge(S["tile_hots_ready"], 1)
            pe.wait_ge(S["keys_T_copied"], 6)

            def sum_half(g, side, half):
                if half == 0:
                    pe.wait_ge(S["group_copied"], g + 1)
                    pe.wait_ge(S["lane_hots_ready"], g + 1)
                pe.wait_ge(S["hots_ready"], g * 2 + (half + 1))
                for c in range(HALF):
                    last = nc.tensor.matmul(bank[3 + side][:, 0:2 * L], olane1[:, half, c, :], pay_oh[:, half, c, :],
                                            start=(half == 0 and c == 0), stop=(half == 1 and c == HALF - 1))
                last.then_inc(S["hots_used"], 1)

            def transpose_group(g):
                pe.wait_ge(S["group_copied"], g + 3)
                for v in range(2):
                    last = nc.tensor.transpose(bank[5][0:L, v * P:(v + 1) * P], group_sb[:, v, :], ident[:, :])
                last.then_inc(S["group_T_mm"], 1)

            def move_group(g, side):
                pe.wait_ge(S["group_T_copied"], g + 1)
                pe.wait_ge(S["ogc_ready"], g + 1)
                for v in range(2):
                    last = nc.tensor.matmul(bank[6 + v][:, 0:K1], group_T[:, v, :], ogc[:, side, :], start=False, stop=False)
                last.then_inc(S["moved_mm"], 1)

            def sort_turn(g, side, first=False):
                sum_half(g, side, 0)
                if not first:
                    transpose_group(g - 1)
                sum_half(g, side, 1)
                if not first:
                    move_group(g - 1, 1 - side)
                pe.wait_ge(S["ol_ready"], g + 1)
                pe.wait_ge(S["cnt_copied"], g + 1)
                for u in range(CG):
                    last = nc.tensor.matmul(bank[0][:, u * NT:(u + 1) * NT], ol1[:, u, :],
                                            OH[:, ds(g * CG + u, 1), :].rearrange("p a t -> p (a t)"), start=True, stop=True)
                last.then_inc(S["cnt_mm"], 1)

            sort_turn(0, 0, True)
            sort_turn(1, 1)
            with pe.Fori(1, NG // 2) as i:
                for side in range(2):
                    sort_turn(i * 2 + side, side)
            transpose_group(NG - 1)
            move_group(NG - 1, 1)
            for v in range(2):
                last = nc.tensor.matmul(bank[6 + v][:, 0:K1], zero_row[:, 0:P], zero_row[:, :], start=False, stop=True)
            last.then_inc(S["moved_all"], 1)
            def sum_chunk(turn, u):
                pe.wait_ge(S["onehot_ready"], turn * U + (u + 1))
                pe.wait_ge(S["agg_free"], turn * U + (u + 1))
                pe.wait_ge(gathered[u], turn * 16 + 16)
                nc.tensor.matmul(agg_bank(u), S1[:, u, :], msgs[:, u, :], start=True, stop=True).then_inc(S["slots_free"], 1)

            def move(k, q, into):
                pe.wait_ge(S["perm_scaled"], k * SUBS + (q + 2))
                pe.wait_ge(S["perm_ready"], k * SUBS + (q + 1))
                for u in range(q * SUB, (q + 1) * SUB):
                    last = nc.tensor.matmul(into[:, 0:C2], oval2[:, u, :], ocol[:, u, :], start=False, stop=False)
                last.then_inc(S["perm_used"], 1)

            pe.wait_ge(S["cnt_copied"], NG + 1)
            for u in range(U):
                sum_chunk(0, u)
            pe.wait_ge(S["tot2_ready"], 1)
            nc.tensor.matmul(bank[2][:, 0:NT], tri[:, :], bucket[:, 0, :], start=True, stop=True)
            nc.tensor.matmul(bank[3][:, 0:NT], ones[:, :], bucket[:, 0, :], start=True, stop=True).then_inc(S["base2_mm"], 1)
            with pe.Fori(1, COUNT_TURNS) as i:
                for u in range(U):
                    sum_chunk(i, u)
            pe.wait_ge(S["places_ready"], 1)
            def rank_turn(i, side):
                k = i * 2 + side
                for u in range(U):
                    sum_chunk(k + RANK_0, u)
                    if u == 0:
                        pe.wait_ge(S["olT_ready"], k + 1)
                        pe.wait_ge(S["r_used"], k + 1)
                        for c in range(U2):
                            last = nc.tensor.matmul(bank[6 + side][:, c * NT:(c + 1) * NT], olT[side][:, c, :],
                                                    PT[:, ds(k * U2 + c, 1), :].rearrange("p a t -> p (a t)"), start=True, stop=True)
                        last.then_inc(S["r_mm"], 1)

            with pe.Fori(0, T2 // 2) as i:
                for side in range(2):
                    rank_turn(i, side)
            for b in range(2):
                nc.tensor.matmul(bank[2 + b][:, 0:C2], zero_row[:, 0:P], zero_row[:, 0:C2], start=True, stop=False)
            for u in range(U):
                sum_chunk(PLACE_TURN, u)

            def move_turn(k, into):
                for u in range(U):
                    sum_chunk(k + MOVE_0, u)
                    if u in (3, 5, 7):
                        move(k, (u - 3) // 2, into)

            with pe.Fori(0, T2) as i:
                move_turn(i, bank[2])
            with pe.Fori(T2, T2 + LOOPS) as i:
                move_turn(i, bank[3])
            for b in range(2):
                last = nc.tensor.matmul(bank[2 + b][:, 0:C2], zero_row[:, 0:P], zero_row[:, 0:C2], start=False, stop=True)
            last.then_inc(S["perm_mm"], 1)
            pe.wait_ge(S["agg_free"], K1 + AGG)
            pe.wait_ge(S["perm_taken"], 1)
            ln_pe(pe, "b")

            def up(tokens, e, off, up_before):
                for j in range(KH):
                    pe.wait_ge(S["up_free"], up_before + (j + 1))
                    for k in range(KD):
                        last = nc.tensor.matmul(bank[j][:, 0:tokens], W1_sb[:, k, e, j * P:(j + 1) * P],
                                                xT[:, k, ds(off, tokens)], start=(k == 0), stop=(k == KD - 1))
                    last.then_inc(S["up_mm"], 1)

            def down(tiles, e, up_before, taken):
                pe.wait_ge(S["up_free"], up_before + 2 * KH)
                for t in range(tiles):
                    pe.wait_ge(S["down_taken"], taken + t)
                    for j in range(KH):
                        last = nc.tensor.matmul(bank[4 + t][:, 0:D], h_ff[:, e % 2, j, t * P:(t + 1) * P], W2_sb[:, e, j, :],
                                                start=(j == 0), stop=(j == KH - 1))
                    last.then_inc(S["down_mm"], 1)

            pe.wait_ge(S["xT_done"], T5 + NT)
            pe.wait_ge(S["ld_ffw"], 16 * 2 * EX)
            with pe.Fori(0, NBLK) as i:
                for e in range(EX + 1):
                    if e < EX:
                        up(BLK, e, i * BLK, (i * EX + e) * KH)
                    if e:
                        down(TB, e - 1, (i * EX + (e - 1)) * KH, (i * EX + (e - 1)) * TB + 1)

            exchanges = ((HEADS, 0), (HEADS, 0), (HEADS, 1), (NS, 0))

            def exchange(q):
                k, shift = exchanges[q]
                pe.wait_ge(S["cols_ready"], q + 1)
                nc.tensor.transpose(bank[6][0:k, 0:P], edge_cols[:, 0, 0:k], ident[:, :])
                nc.tensor.transpose(bank[6][0:k, P:2 * P], edge_cols[:, 1, 0:k], ident[:, :]).then_inc(S["cols_T"], 1)
                pe.wait_ge(S["across_ready"], q + 1)
                nc.tensor.transpose(bank[7][:, 0:k], across[0:k, 2, shift:shift + P], ident[0:k, 0:k]).then_inc(S["across_T"], 1)

            pe.wait_ge(S["down_taken"], TB + NBLK * EX * TB)
            exchange(0)
            for e in range(EX + 1):
                if e < EX:
                    up(P, e, NBLK * BLK, (NBLK * EX + e) * KH)
                if e:
                    m = NBLK * EX
                    down(1, e - 1, (m + e - 1) * KH, m * TB + 1 if e == 1 else TB + m * TB + e - 1)
                if e == 2:
                    exchange(1)
            exchange(2)
            exchange(3)
            pe.wait_ge(S["down_taken"], TB + NBLK * EX * TB + EX)
            pe.wait_ge(S["gate_ready"], 1)
            for j in range(GROUPS4 + 1):
                if j < GROUPS4:
                    if j >= 2:
                        pe.wait_ge(S["gate_T_copied"], j - 1)
                    for t in range(4 * j, min(4 * j + 4, NT)):
                        last = nc.tensor.transpose(bank[2 + j % 2][0:EX, (t % 4) * P:(t % 4 + 1) * P], gate[:, :, t], ident[:, :])
                    last.then_inc(S["gate_T"], 1)
                if j == 0:
                    continue
                pe.wait_ge(S["gate_T_copied"], j)
                for t in range(4 * j - 4, min(4 * j, NT)):
                    if t >= 4:
                        pe.wait_ge(S["gb_used"], t - 3)
                    rows = bank[(0, 1, 4, 5)[t % 4]][:, 0:D]
                    nc.tensor.matmul(rows, gT[:, t, :], b2_sb[:, :], start=True, stop=False)
                    pe.wait_ge(S["diag_ready"], t + 1)
                    pe.wait_ge(y_loaded[t % YS], 16 * (t // YS + 1))
                    nc.tensor.matmul(rows, diag[:, t % 4, :], y_in[t % YS][:, EX - 1, :], start=False, stop=True).then_inc(S["gb_mm"], 1)

        @block.vector
        def _(dve):
            steps = Steps(dve, S["dve_step"])
            V = nc.vector
            dve.nop().then_inc(S["agg_free"], AGG)
            dve.nop().then_inc(S["r_used"], 2)
            dve.nop().then_inc(S["gat_free"], SLOTS)
            dve.nop().then_inc(S["xT_done"], T5)

            dve.wait_ge(S["consts"], 1)
            dve.wait_ge(S["ld_src"], 32)
            dve.wait_ge(S["ld_dst"], 32)
            dve.wait_ge(S["ld_wt"], 32)
            steps.mark(V.tensor_copy(payload[:, 1, :], dst1))
            steps.done(V.tensor_single_scalar(tmp1, src1, 7, ALU.logical_shift_right))
            steps.mark(V.tensor_copy(tile1, tmp1))
            steps.done(V.tensor_single_scalar(src1, src1, P - 1, ALU.bitwise_and))
            steps.done(V.tensor_copy(lane1, src1))
            steps.done(V.scalar_tensor_tensor(payload[:, 1, :], payload[:, 1, :], float(P), lane1, ALU.mult, ALU.add))
            with dve.Fori(0, NT // T5) as i:
                steps.enter(i, 2 * T5)
                for u in range(T5):
                    steps.mark(V.tensor_scalar(ind5[:, u, :], tile1, iota_k[:, ds(i * T5 + u, 1)], None, ALU.is_equal))
                steps.wait()
                for u in range(T5):
                    steps.mark(V.tensor_tensor_scan(cum1[:, ds(i * T5 + u, 1), :].rearrange("p a c -> p (a c)"),
                                                    ones[:, 0:1].to_broadcast([P, C1]), ind5[:, u, :], 0.0, ALU.mult, ALU.add))
                steps.wait()
                steps.leave(NT // T5)
            ends = cum1.rearrange("p b (g c) -> p b g c", c=G)[:, :, :, G - 1]
            steps.mark(V.tensor_copy(cnt[0][:, :, 0:1], ends[:, :, 0:1]))
            steps.done(V.tensor_tensor(cnt[0][:, :, 1:NG], ends[:, :, 1:NG], ends[:, :, 0:NG - 1], ALU.subtract))
            dve.nop().then_inc(S["counts_ready"], 1)
            dve.wait_ge(S["counts_mm"], 1)
            flat = [c[:, :, :].rearrange("p b g -> p (b g)") for c in cnt]
            steps.mark(V.tensor_copy(flat[5], bank[1][:, 0:NT * NG]))
            steps.wait()
            steps.done(V.tensor_tensor_scan(flat[1], first_g[:, :, :].rearrange("p b g -> p (b g)"), flat[5],
                                            0.0, ALU.mult, ALU.add))
            total, number, last_, end_, first_ = (bucket[:, i, :] for i in range(5))
            steps.done(V.tensor_scalar(total, cnt[1][:, :, NG - 1], float(P - 1), None, ALU.add))
            steps.done(V.tensor_copy(bucket_i[:, :], total))
            steps.done(V.tensor_single_scalar(bucket_i[:, :], bucket_i[:, :], 7, ALU.logical_shift_right))
            steps.done(V.tensor_copy(number, bucket_i[:, :]))
            steps.done(V.tensor_tensor_scan(end_, ones[:, 0:NT], number, 0.0, ALU.mult, ALU.add))
            dve.nop().then_inc(S["ends_ready"], 1)
            steps.done(V.tensor_tensor(first_, end_, number, ALU.subtract))
            steps.done(V.scalar_tensor_tensor(cnt[1][:, :, :], first_.unsqueeze(2).to_broadcast([P, NT, NG]), float(P),
                                              cnt[1][:, :, :], ALU.mult, ALU.add))
            steps.done(V.tensor_tensor(flat[2], flat[1], flat[5], ALU.subtract))
            steps.done(V.tensor_copy(cnt_i[:, :, :], cnt[2][:, :, :]))
            steps.done(V.tensor_single_scalar(cnt_i[:, :, :], cnt_i[:, :, :], 7, ALU.logical_shift_right))
            steps.done(V.tensor_copy(cnt[3][:, :, :], cnt_i[:, :, :]))
            steps.done(V.tensor_scalar(flat[4], flat[1], float(P - 1), None, ALU.add))
            steps.done(V.tensor_copy(cnt_i[:, :, :], cnt[4][:, :, :]))
            steps.done(V.tensor_single_scalar(cnt_i[:, :, :], cnt_i[:, :, :], 7, ALU.logical_shift_right))
            steps.done(V.tensor_copy(cnt[4][:, :, :], cnt_i[:, :, :]))
            steps.done(V.tensor_tensor(by_g[0][:, :, :].rearrange("p g b -> p b g"), cnt[4][:, :, :], cnt[3][:, :, :], ALU.subtract))
            for g in range(NG):
                steps.mark(V.tensor_tensor_scan(by_g[1][:, g, :], ones[:, 0:NT], by_g[0][:, g, :], 0.0, ALU.mult, ALU.add))
            steps.wait()
            steps.done(V.tensor_tensor(by_g[0][:, :, :], by_g[1][:, :, :], by_g[0][:, :, :], ALU.subtract))
            steps.done(V.tensor_tensor(cnt[4][:, :, :], by_g[0][:, :, :].rearrange("p g b -> p b g"), cnt[3][:, :, :], ALU.subtract))
            steps.done(V.scalar_tensor_tensor(flat[5], flat[4], float(P), flat[2], ALU.mult, ALU.add))
            steps.done(V.tensor_tensor(flat[5], flat[5], bank[0][:, 0:NT * NG], ALU.add))
            steps.done(V.tensor_scalar(flat[5], flat[5], 1.0, None, ALU.subtract))
            steps.done(V.tensor_tensor(cnt[5][:, :, 1:NG], cnt[5][:, :, 1:NG], ends[:, :, 0:NG - 1], ALU.subtract))
            span = by_g[2][:, :, :]
            steps.done(V.tensor_scalar(span, by_g[1][:, :, :], iota_p[:, 0:1], None, ALU.is_le))
            steps.done(V.tensor_scalar(by_g[1][:, :, :], by_g[0][:, :, :], iota_p[:, 0:1], None, ALU.is_le))
            steps.done(V.tensor_tensor(span, by_g[1][:, :, :], span, ALU.subtract))
            steps.done(V.tensor_reduce(global_chunk[:, 0, :], span, AX, ALU.add))
            steps.done(V.tensor_tensor(span, span, cnt[4][:, :, :].rearrange("p b g -> p g b"), ALU.mult))
            steps.done(V.tensor_reduce(global_chunk[:, 1, :], span, AX, ALU.add))
            steps.done(V.tensor_scalar(global_chunk[:, 0, :], global_chunk[:, 0, :], -NO_CHUNK, NO_CHUNK, ALU.mult, ALU.add))
            steps.done(V.tensor_tensor(global_chunk[:, 0, :], global_chunk[:, 0, :], global_chunk[:, 1, :], ALU.subtract))
            steps.done(V.tensor_scalar(global_chunk[:, 2, :], global_chunk[:, 0, :], iota_p[:, 0:1], None, ALU.add))
            dve.wait_ge(S["ends_mm"], 1)
            steps.done(V.tensor_copy(end_col[:, :], bank[2][0:NT, 0:1]))
            V.tensor_scalar(geq, iota_k[0:NT, :], end_col[:, 0:1], None, ALU.is_ge).then_inc(S["geq_ready"], 1)
            dve.wait_ge(S["geq_mm"], 1)
            steps.done(V.tensor_scalar(tile_of_chunk[:, :], bank[3][0:1, 0:K1], float(NT - 1), None, ALU.min))
            steps.done(V.memset(place1, 0.0))
            with dve.Fori(0, NT // T5) as i:
                steps.enter(i, 3 * T5)
                for u in range(T5):
                    b = ds(i * T5 + u, 1)
                    steps.mark(V.tensor_tensor(at5[:, u, :].rearrange("p (g c) -> p g c", c=G),
                                               cum1[:, b, :].rearrange("p a (g c) -> p (a g) c", c=G),
                                               cnt[5][:, b, :].rearrange("p a g -> p (a g)").unsqueeze(2).to_broadcast([P, NG, G]),
                                               ALU.add))
                steps.wait()
                for u in range(T5):
                    steps.mark(V.scalar_tensor_tensor(in5[:, u, :], tile1, iota_k[:, ds(i * T5 + u, 1)], at5[:, u, :],
                                                      ALU.is_equal, ALU.mult))
                steps.wait()
                for u in range(T5):
                    steps.done(V.tensor_tensor(place1, place1, in5[:, u, :], ALU.add))
                steps.leave(NT // T5)
            steps.done(V.tensor_copy(tmp1, place1))
            steps.done(V.tensor_single_scalar(src1, tmp1, P - 1, ALU.bitwise_and))
            steps.mark(V.tensor_copy(lane1, src1))
            steps.done(V.tensor_single_scalar(tmp1, tmp1, 7, ALU.logical_shift_right))
            steps.mark(V.tensor_copy(chunk1, tmp1))
            dve.wait_ge(S["ld_keys"], 32)
            steps.done(V.tensor_single_scalar(key_tile, key2[:, :], 7, ALU.logical_shift_right))
            steps.done(V.tensor_single_scalar(key2[:, :], key2[:, :], P - 1, ALU.bitwise_and))
            dve.nop().then_inc(S["ranks_done"], 1)

            def layer_norm(which):
                with dve.Fori(0, NT // T5) as i:
                    steps.enter(i, 2 * T5 + 1)
                    for u in range(T5):
                        steps.mark(V.bn_stats(stats[:, u, :], xs[:, ds(i * T5 + u, 1), :].rearrange("p a d -> p (a d)")))
                    steps.wait()
                    dve.nop(nofuse=True)
                    for u in range(T5):
                        steps.mark(V.bn_aggr(stats[:, T5 + u, 0:2], stats[:, u, :]))
                    steps.wait()
                    steps.done(V.tensor_copy(mv[:, ds(i * T5, T5), :], stats[:, T5:2 * T5, 0:2]))
                    steps.leave(NT // T5)
                inverse_deviation(rstd, mv[:, :, 1], which)
                apply_turn(0, which, False)
                with dve.Fori(1, NT // T5) as i:
                    apply_turn(i, which, which == "b")
                if which == "b":
                    for u in range(T5):
                        keep_transposed(NT // T5 - 1, u)

            def apply_turn(i, which, keep_before):
                for u in range(T5):
                    t = ds(i * T5 + u, 1)
                    if keep_before:
                        keep_transposed(i - 1, u)
                    dve.wait_ge(S[f"xn_T_{which}"], i * T5 + (u + 1))
                    V.tensor_scalar(xn[:, u, :], xs[:, t, :].rearrange("p a d -> p (a d)"),
                                    mv[:, t, 0:1].rearrange("p a s -> p (a s)"), rstd[:, 3, t],
                                    ALU.subtract, ALU.mult).then_inc(S[f"xn_ready_{which}"], 1)

            def keep_transposed(i, u):
                dve.wait_ge(S["xnT_copied_b"], T5 + i * T5 + (u + 1))
                V.tensor_copy(xT[:, :, ds((i * T5 + u) * P, P)], xnT[:, u, :, :]).then_inc(S["xT_done"], 1)

            def inverse_deviation(r, variance, which):
                steps.done(V.tensor_scalar(r[:, 0, :], variance, LN_EPS, None, ALU.add))
                dve.nop().then_inc(S[f"var_{which}"], 1)
                dve.wait_ge(S[f"std_{which}"], 1)
                steps.done(V.reciprocal(r[:, 2, :], r[:, 1, :]))
                steps.done(V.tensor_tensor(r[:, 3, :], r[:, 2, :], r[:, 2, :], ALU.mult))
                steps.done(V.tensor_tensor(r[:, 3, :], r[:, 3, :], r[:, 0, :], ALU.mult))
                steps.done(V.tensor_scalar(r[:, 3, :], r[:, 3, :], -0.5, 1.5, ALU.mult, ALU.add))
                steps.done(V.tensor_tensor(r[:, 3, :], r[:, 3, :], r[:, 2, :], ALU.mult))

            dve.wait_ge(S["ld_x"], 32)
            dve.wait_ge(S["ld_w"], 16 * (8 + EX + 1))
            layer_norm("a")
            dve.wait_ge(S["xn_ready_a"], NT)
            steps.done(V.tensor_tensor(xs[:, :, :], xs[:, :, :], bias_b[:, :].unsqueeze(1).to_broadcast([P, NT, D]), ALU.add))

            def hots_turn(g, side):
                for half in range(2):
                    dve.wait_ge(S["hots_used"], g * 2 + (half + 1))
                    col = ds(g * G + half * HALF, HALF)
                    bc = lambda v, n: v.unsqueeze(2).to_broadcast([P, HALF, n])
                    steps.mark(V.tensor_tensor(ochunk[:, half, :, :], iota16[:, 0:L].unsqueeze(1).to_broadcast([P, HALF, L]),
                                               bc(chunk1[:, col], L), ALU.is_equal))
                    if half:
                        V.tensor_tensor(olane1[:, half, :, :], iota16[:, 0:P].unsqueeze(1).to_broadcast([P, HALF, P]),
                                        bc(lane1[:, col], P), ALU.is_equal)
                    steps.wait()
                    view = pay_oh[:, half, :, :].rearrange("p c (v l) -> p c v l", v=2)
                    for v in range(2):
                        last = V.tensor_tensor(view[:, :, v, :], ochunk[:, half, :, :], bc(payload[:, v, col], L), ALU.mult)
                    last.then_inc(S["hots_ready"], 1)
                dve.wait_ge(S["moved_mm"], g + 1)
                V.tensor_scalar(ogc[:, side, :], iota_k[0:L, :], global_chunk[0:L, 2, ds(g, 1)], None,
                                ALU.is_equal).then_inc(S["ogc_ready"], 1)

            with dve.Fori(0, NG // 2) as i:
                steps.enter(i, 4)
                for side in range(2):
                    hots_turn(i * 2 + side, side)
                steps.leave(NG // 2)
            dve.wait_ge(S["moved_all"], 1)
            steps.mark(V.tensor_copy(w_s, bank[6][:, 0:K1]))
            steps.done(V.tensor_copy(pack_i, bank[7][:, 0:K1]))
            steps.mark(V.tensor_single_scalar(idx_s, pack_i, 7, ALU.logical_shift_right))
            steps.done(V.tensor_single_scalar(pack_i, pack_i, P - 1, ALU.bitwise_and))
            steps.done(V.tensor_copy(loc_s, pack_i))
            dve.nop().then_inc(S["edges_ready"], 1)

            def dest_hots(turn, u):
                c = ds(turn * U + u, 1)
                V.tensor_scalar(S1[:, u, :], iota_k[:, 0:P], loc_s[:, c], w_s[:, c], ALU.is_equal, ALU.mult).then_inc(S["onehot_ready"], 1)

            def tiles_of(turn):
                return nc.values_load_multi_w_load_instructions(
                    tile_of_chunk[0:1, ds(turn * U, U)], engines=[mybir.EngineType.DVE], min_val=0, max_val=NT - 1,
                    skip_runtime_bounds_check_because="a count of buckets, of which the smaller of it and NT - 1 was taken")[1]

            def sum_chunk(turn, tiles, u, last=False):
                dve.wait_ge(S["slots_free"], U + turn * U + (u + 1))
                dve.wait_ge(S["agg_free"], AGG + turn * U + u)
                acc = xs[:, ds(tiles[u], 1), :].rearrange("p a d -> p (a d)")
                V.tensor_tensor(acc, acc, agg_bank(u), ALU.add).then_inc(S["agg_free"], 1)
                if not last:
                    dest_hots(turn + 1, u)

            for u in range(U):
                dest_hots(0, u)
            tot2, base2 = bucket[:, 0, :], bucket[:, 1, :]
            dve.wait_ge(S["cnt_copied"], NG + 1)
            tiles = tiles_of(0)
            for u in range(U):
                sum_chunk(0, tiles, u)
                if u < NT // T5:
                    some = slice(u * T5, (u + 1) * T5)
                    steps.mark(V.tensor_reduce(tot2[:, some], CT[:, :, some].rearrange("p c t -> p t c"), AX, ALU.add))
                if u == NT // T5 - 1:
                    steps.wait()
                    dve.nop().then_inc(S["tot2_ready"], 1)
            dve.wait_ge(S["base2_mm"], 1)
            steps.done(V.tensor_copy(bucket[:, 2, :], bank[3][:, 0:NT]))
            steps.done(V.tensor_tensor_scan(bucket[:, 3, :], ones[:, 0:NT], bucket[:, 2, :], 0.0, ALU.mult, ALU.add))
            steps.done(V.tensor_tensor(base2, bucket[:, 3, :], bucket[:, 2, :], ALU.subtract))
            steps.done(V.tensor_tensor(base2, base2, bank[2][:, 0:NT], ALU.add))
            steps.done(V.tensor_tensor(bucket[:, 4, :], base2, tot2, ALU.add))
            steps.done(V.tensor_scalar(endpos[:, :], bucket[:, 4, :], 1.0, None, ALU.subtract))
            steps.mark(V.tensor_copy(PT[:, 0, :], base2))
            for turn in range(1, COUNT_TURNS):
                tiles = tiles_of(turn)
                for u in range(U):
                    sum_chunk(turn, tiles, u)
                    for t in range((turn - 1) * U + u, NT, (COUNT_TURNS - 1) * U):
                        steps.mark(V.tensor_tensor_scan(PT[:, 1:C2T + 1, t], ones[:, 0:1].to_broadcast([P, C2T]), CT[:, :, t],
                                                        bucket[:, 1, t:t + 1], ALU.mult, ALU.add))
            steps.wait()

            dve.nop().then_inc(S["places_ready"], 1)

            def rank_turn(i, side):
                k = i * 2 + side
                tiles = tiles_of(k + RANK_0)
                dve.wait_ge(rows_landed[side], i * 16 + 16)
                for u in range(U):
                    sum_chunk(k + RANK_0, tiles, u)
                    for c in range(2 * u, min(2 * u + 2, U2)):
                        last = V.scalar_tensor_tensor(same[:, c, :], rows2[:, side, c, 1, :], keyc2[:, ds(k * U2 + c, 1)], tri16[:, :],
                                                      ALU.is_equal, ALU.mult, accum_out=rank2[:, ds(k * U2 + c, 1)])
                        if c == U2 - 1:
                            last.then_inc(S["ranked"], 1)
                dve.wait_ge(S["r_mm"], k + 1)
                steps.done(V.tensor_tensor(rsel, bank[6 + side][:, 0:U2 * NT].rearrange("p (u t) -> p u t", u=U2),
                                           OH[:, ds(k * U2, U2), :], ALU.mult))
                V.tensor_reduce(pos2[:, ds(k * U2, U2)], rsel, AX, ALU.add).then_inc(S["r_used"], 1)

            with dve.Fori(0, T2 // 2) as i:
                steps.enter(i, 2)
                for side in range(2):
                    rank_turn(i, side)
                steps.leave(T2 // 2)
            dve.wait_ge(S["r_used"], T2 + 2)
            dve.wait_ge(S["ranked"], T2)
            steps.done(V.tensor_tensor(pos2, pos2, rank2[:, :], ALU.add))
            main = slice(0, C2T)
            steps.done(V.tensor_scalar(tmp2, pos2, 1.0 / C2, 0.5 / C2 - 0.5, ALU.mult, ALU.add))
            steps.done(V.tensor_copy(tmp2i, tmp2))
            steps.done(V.tensor_copy(lane2[:, main], tmp2i))
            steps.done(V.scalar_tensor_tensor(col2[:, main], lane2[:, main], -float(C2), pos2, ALU.mult, ALU.add))
            for test, bound, sign in ((ALU.is_lt, 0.0, 1.0), (ALU.is_ge, float(C2), -1.0)):
                steps.done(V.tensor_scalar(tmp2, col2[:, main], bound, None, test))
                steps.mark(V.scalar_tensor_tensor(lane2[:, main], tmp2, -sign, lane2[:, main], ALU.mult, ALU.add))
                steps.done(V.scalar_tensor_tensor(col2[:, main], tmp2, sign * C2, col2[:, main], ALU.mult, ALU.add))
            again = slice(C2T, C2T + LOOPS * U2)
            steps.mark(V.tensor_copy(lane2[:, again], lane2[:, 0:LOOPS * U2]))
            steps.mark(V.tensor_copy(col2[:, again], col2[:, 0:LOOPS * U2]))
            steps.mark(V.memset(src_sorted[:, :], 0))
            tiles = tiles_of(PLACE_TURN)
            for u in range(U):
                sum_chunk(PLACE_TURN, tiles, u)
            steps.wait()
            dve.nop().then_inc(S["lanes_ready"], 1)

            def move_hots(k, q):
                dve.wait_ge(S["perm_used"], k * SUBS + (q + 1))
                for u in range(q * SUB, (q + 1) * SUB):
                    last = V.tensor_scalar(ocol[:, u, :], iota16[:, 0:C2], col2[:, ds(k * U2 + u, 1)], None, ALU.is_equal)
                last.then_inc(S["perm_ready"], 1)

            def move_turn(k, last=False):
                tiles = tiles_of(k + MOVE_0)
                for u in range(U):
                    sum_chunk(k + MOVE_0, tiles, u, last)
                    if u in (0, 2, 4):
                        move_hots(k, u // 2)

            with dve.Fori(0, T2 + LOOPS - 1) as i:
                move_turn(i)
            move_turn(T2 + LOOPS - 1, True)
            dve.wait_ge(S["agg_free"], AGG + K1)
            dve.wait_ge(S["perm_mm"], 1)
            steps.mark(V.tensor_copy(starts[:, :], bank[3][:, 0:C2]))
            steps.done(V.tensor_scalar(src_sorted[:, 0:C2], bank[2][:, 0:C2], MIDDLE, None, ALU.add))
            dve.nop().then_inc(S["perm_taken"], 1)

            layer_norm("b")
            dve.wait_ge(S["proj_taken_b"], NT + 2)
            for a in range(2):
                steps.done(V.tensor_tensor(agg[:, :, :], GT[:, 0:NT, 0:CH], att_b[:, a, :].unsqueeze(1).to_broadcast([P, NT, CH]), ALU.mult))
                steps.done(V.tensor_reduce(GT[:, 0:NT, CH + a * HEADS:CH + (a + 1) * HEADS],
                                           agg[:, :, :].rearrange("p t (h e) -> p t h e", e=EX), AX, ALU.add))
            dve.nop().then_inc(S["table_ready"], 1)

            dve.wait_ge(S["table_sent"], 16)
            with dve.Fori(0, C2G // SLOTS) as i:
                for u in range(SLOTS):
                    dve.wait_ge(gat_in[u], i * 16 + 16)
                    V.tensor_copy(GT[:, ds(i * SLOTS + u, 1), :].rearrange("p a r -> p (a r)"), gat_slot[:, u, :]).then_inc(S["gat_free"], 1)
            dve.wait_ge(S["gat_free"], SLOTS + C2G)
            steps.mark(V.tensor_scalar(keep, starts[:, :], -1.0, 1.0, ALU.mult, ALU.add))
            steps.mark(V.tensor_scalar(drop_f, starts[:, :], -BIG, None, ALU.mult))
            steps.mark(V.tensor_scalar(drop_r[:, 0:C2 - 1], starts[:, 1:C2], -BIG, None, ALU.mult))
            steps.mark(V.memset(drop_r[:, C2 - 1:C2], 0.0))
            steps.done(V.tensor_reduce(flag_any[:, 0:1], starts[:, :], AX, ALU.max))
            steps.mark(V.tensor_scalar(flag_any[:, 1:2], flag_any[:, 0:1], -1.0, 1.0, ALU.mult, ALU.add))
            steps.done(V.tensor_scalar(flag_any[:, 2:3], flag_any[:, 0:1], -BIG, None, ALU.mult))
            steps.done(V.memset(across[:, 2, :], 0.0))

            turns = [0]

            def over_partitions(k, last_cols, flag, op0, op1, nothing, reverse):
                q = turns[0]
                turns[0] += 1
                steps.mark(V.tensor_copy(edge_cols[:, 0, 0:k], last_cols))
                steps.done(V.tensor_copy(edge_cols[:, 1, 0:k], flag_any[:, flag:flag + 1].to_broadcast([P, k])))
                dve.nop().then_inc(S["cols_ready"], 1)
                dve.wait_ge(S["cols_T"], q + 1)
                steps.mark(V.tensor_copy(across[0:k, 0, 0:P], bank[6][0:k, 0:P]))
                steps.mark(V.tensor_copy(across[0:k, 1, 0:P], bank[6][0:k, P:2 * P]))
                edge = P if reverse else 0
                steps.done(V.memset(across[0:k, 2, edge:edge + 1], nothing))
                o = across[0:k, 2, 0:P][:, ::-1] if reverse else across[0:k, 2, 1:P + 1]
                l, f = across[0:k, 0, 0:P], across[0:k, 1, 0:P]
                if reverse:
                    l, f = l[:, ::-1], f[:, ::-1]
                steps.done(V.tensor_tensor_scan(o, f, l, nothing, op0, op1))
                dve.nop().then_inc(S["across_ready"], 1)
                dve.wait_ge(S["across_T"], q + 1)
                steps.done(V.tensor_copy(carry[:, 0, 0:k], bank[7][:, 0:k]))

            steps.done(V.tensor_tensor(s_e, GT[:, 0:C2, CH + HEADS:ROW].rearrange("p c h -> p h c"),
                                       starts[:, :].unsqueeze(1).to_broadcast([P, HEADS, C2]), ALU.mult))

            def spread(initial):
                for h in range(HEADS):
                    steps.mark(V.tensor_tensor_scan(ad_e[:, h, :], keep, s_e[:, h, :], initial(h), ALU.mult, ALU.add))
                steps.wait()

            spread(lambda h: 0.0)
            over_partitions(HEADS, ad_e[:, :, C2 - 1], 1, ALU.mult, ALU.add, 0.0, False)
            spread(lambda h: carry[:, 0, h:h + 1])
            steps.done(V.tensor_tensor(e_e, GT[:, 0:C2, CH:CH + HEADS].rearrange("p c h -> p h c"), ad_e, ALU.add))
            flat_e = e_e.rearrange("p h c -> p (h c)")
            steps.done(V.scalar_tensor_tensor(flat_e, flat_e, 0.2, flat_e, ALU.mult, ALU.max))

            def scan_max(o, flags, initial, reverse):
                for h in range(HEADS):
                    a, b, c = o[:, h, :], flags, e_e[:, h, :]
                    if reverse:
                        a, b, c = a[:, ::-1], b[:, ::-1], c[:, ::-1]
                    steps.mark(V.tensor_tensor_scan(a, b, c, initial(h), ALU.add, ALU.max))
                steps.wait()

            scan_max(f_e, drop_f, lambda h: -BIG, False)
            over_partitions(HEADS, f_e[:, :, C2 - 1], 2, ALU.add, ALU.max, -BIG, False)
            scan_max(f_e, drop_f, lambda h: carry[:, 0, h:h + 1], False)
            scan_max(s_e, drop_r, lambda h: -BIG, True)
            steps.done(V.tensor_scalar(carry[:, 1, 0:HEADS], s_e[:, :, 0], drop_f[:, 0:1], None, ALU.add))
            over_partitions(HEADS, carry[:, 1, 0:HEADS], 2, ALU.add, ALU.max, -BIG, True)
            scan_max(s_e, drop_r, lambda h: carry[:, 0, h:h + 1], True)
            flat_f, flat_s = f_e.rearrange("p h c -> p (h c)"), s_e.rearrange("p h c -> p (h c)")
            steps.done(V.tensor_tensor(flat_f, flat_f, flat_s, ALU.max))
            steps.done(V.tensor_tensor(flat_e, flat_e, flat_f, ALU.subtract))
            dve.nop().then_inc(S["exp_in"], 1)
            dve.wait_ge(S["exp_out"], 1)
            steps.mark(V.tensor_copy(V20[:, 0:HEADS, :], e_e))
            for h in range(HEADS):
                steps.mark(V.tensor_tensor(V20[:, HEADS + h * EX:HEADS + (h + 1) * EX, :],
                                           GT[:, 0:C2, h * EX:(h + 1) * EX].rearrange("p c e -> p e c"),
                                           e_e[:, h:h + 1, :].to_broadcast([P, EX, C2]), ALU.mult))
            steps.wait()

            def scan_sums(initial):
                for s in range(NS):
                    steps.mark(V.tensor_tensor_scan(VS[:, :, s], keep, V20[:, s, :], initial(s), ALU.mult, ALU.add))
                steps.wait()

            scan_sums(lambda s: 0.0)
            over_partitions(NS, VS[:, C2 - 1, :], 1, ALU.mult, ALU.add, 0.0, False)
            scan_sums(lambda s: carry[:, 0, s:s + 1])
            dve.nop().then_inc(S["sums_ready"], 1)
            dve.wait_ge(sums_in, 16 * NT)
            den = node_sums[:, :, 0:HEADS]
            steps.done(V.tensor_scalar(den, den, 1e-16, None, ALU.add))
            steps.done(V.reciprocal(den, den))
            steps.done(V.tensor_tensor(agg[:, :, :].rearrange("p t (h e) -> p t h e", e=EX),
                                       node_sums[:, :, HEADS:NS].rearrange("p t (h e) -> p t h e", e=EX),
                                       den.unsqueeze(3).to_broadcast([P, NT, HEADS, EX]), ALU.mult))

            def row(i):
                return gam_b[:, i, :].unsqueeze(1).to_broadcast([P, NT, CH])

            def node(v):
                return v.unsqueeze(2).to_broadcast([P, NT, CH])

            steps.done(V.tensor_tensor(agg[:, :, :], agg[:, :, :], row(2), ALU.add))
            steps.done(V.tensor_reduce(pair[:, 4, :], agg[:, :, :], AX, ALU.add))
            steps.done(V.tensor_scalar(pair[:, 4, :], pair[:, 4, :], 1.0 / CH, None, ALU.mult))
            steps.done(V.tensor_tensor(agg[:, :, :], agg[:, :, :], node(pair[:, 4, :]), ALU.subtract))
            steps.done(V.tensor_tensor(agg2[:, :, :], agg[:, :, :], agg[:, :, :], ALU.mult))
            steps.done(V.tensor_reduce(pair[:, 5, :], agg2[:, :, :], AX, ALU.add))
            steps.done(V.tensor_scalar(pair[:, 5, :], pair[:, 5, :], 1.0 / CH, None, ALU.mult))
            inverse_deviation(pair, pair[:, 5, :], "c")
            steps.done(V.tensor_tensor(agg[:, :, :], agg[:, :, :], node(pair[:, 3, :]), ALU.mult))
            steps.done(V.tensor_tensor(agg[:, :, :], agg[:, :, :], row(0), ALU.mult))
            steps.done(V.tensor_tensor(agg[:, :, :], agg[:, :, :], row(1), ALU.add))
            steps.done(V.tensor_reduce(sc4[:, :, :].rearrange("p e t -> p t e"),
                                       agg[:, :, :].rearrange("p t (h e) -> p t e h", e=EX), AX, ALU.add))
            flat4 = sc4[:, :, :].rearrange("p e t -> p (e t)")
            steps.done(V.tensor_scalar(flat4, flat4, 1.0 / HEADS, None, ALU.mult))
            steps.done(V.memset(rank4[:, :, :], 0.0))
            for a in range(EX):
                for b in range(a + 1, EX):
                    steps.done(V.tensor_tensor(pair[:, 0, :], sc4[:, a, :], sc4[:, b, :], ALU.is_ge))
                    steps.mark(V.tensor_tensor(rank4[:, b, :], rank4[:, b, :], pair[:, 0, :], ALU.add))
                    steps.mark(V.scalar_tensor_tensor(rank4[:, a, :], rank4[:, a, :], 1.0, pair[:, 0, :], ALU.add, ALU.subtract))
                    steps.wait()
            flat_r = rank4[:, :, :].rearrange("p e t -> p (e t)")
            steps.done(V.tensor_scalar(flat_r, flat_r, 2.0, None, ALU.is_lt))
            steps.done(V.tensor_reduce(pair[:, 1, :], sc4[:, :, :].rearrange("p e t -> p t e"), AX, ALU.max))
            steps.done(V.tensor_tensor(gate[:, :, :], sc4[:, :, :], pair[:, 1, :].unsqueeze(1).to_broadcast([P, EX, NT]), ALU.subtract))
            dve.nop().then_inc(S["wexp_in"], 1)
            dve.wait_ge(S["wexp_out"], 1)
            steps.done(V.tensor_tensor(gate[:, :, :], gate[:, :, :], rank4[:, :, :], ALU.mult))
            steps.done(V.tensor_reduce(pair[:, 2, :], gate[:, :, :].rearrange("p e t -> p t e"), AX, ALU.add))
            steps.done(V.reciprocal(pair[:, 3, :], pair[:, 2, :]))
            steps.done(V.tensor_tensor(gate[:, :, :], gate[:, :, :], pair[:, 3, :].unsqueeze(1).to_broadcast([P, EX, NT]), ALU.mult))
            dve.nop().then_inc(S["gate_ready"], 1)

            for t0 in range(0, NT, 2):
                pair_ = range(t0, min(t0 + 2, NT))
                for t in pair_:
                    dve.wait_ge(y_loaded[t % YS], 16 * (t // YS + 1))
                for e in range(EX - 1):
                    for t in pair_:
                        steps.mark(V.scalar_tensor_tensor(xs[:, t, :], y_in[t % YS][:, e, :], gate[:, e, t:t + 1], xs[:, t, :],
                                                          ALU.mult, ALU.add))
                        if len(pair_) == 2:
                            steps.wait_but_last()
                        else:
                            steps.wait()
                for t in pair_:
                    dve.wait_ge(S["gb_mm"], t + 1)
                    if t == t0 + 1:
                        steps.wait()
                    V.tensor_tensor(xs[:, t, :], xs[:, t, :], bank[(0, 1, 4, 5)[t % 4]][:, 0:D], ALU.add).then_inc(S["gb_used"], 1)
                    if t >= 1:
                        dve.wait_ge(S["gb_used"], t)
                        dve.nop().then_inc(S["out_ready"], 1)
            dve.wait_ge(S["gb_used"], NT)
            dve.nop().then_inc(S["out_ready"], 1)


_NAMES = ["x", "src", "dst", "edge_weight", "L0_gnn_W", "L0_gnn_bias", "L0_ffn_W_gat", "L0_ffn_att_src", "L0_ffn_att_dst",
          "L0_ffn_b_gat", "L0_ffn_ln_gamma", "L0_ffn_ln_beta", "L0_ffn_W1", "L0_ffn_b1", "L0_ffn_W2", "L0_ffn_b2",
          "L0_ffn_edge_index"]


def kernel(**inputs):
    import numpy as _np
    import concourse.bacc as _bacc
    from concourse import mybir as _mybir
    from concourse.bass_utils import run_bass_kernel_spmd as _run

    nc = _bacc.Bacc("TRN2", target_bir_lowering=False, num_devices=1)
    arrays, args = {}, []
    for name in _NAMES:
        a = _np.ascontiguousarray(inputs[name])
        arrays[f"in_{name}"] = a
        args.append(nc.dram_tensor(f"in_{name}", a.shape, _mybir.dt.from_np(a.dtype), kind="ExternalInput").ap())
    shape = inputs["x"].shape
    args.append(nc.dram_tensor("out_rows", shape, _mybir.dt.float32, kind="ExternalOutput").ap())
    gnn_moe_kernel(nc, *args)
    return _run(nc, [arrays], core_ids=[0]).results[0]["out_rows"]
```

```python
import concourse.bass as bass
from concourse import mybir
from contextlib import ExitStack

P = 128


class Steps:

    def __init__(self, engine, sem):
        self.engine, self.sem, self.value, self.offset = engine, sem, 0, 0

    def mark(self, instruction):
        self.value += 1
        instruction.then_inc(self.sem, 1)

    def wait(self):
        self.engine.wait_ge(self.sem, self.value + self.offset)

    def wait_but_last(self):
        self.engine.wait_ge(self.sem, self.value + self.offset - 1)

    def done(self, instruction):
        self.mark(instruction)
        self.wait()

    def enter(self, index, per_turn):
        self.begun, self.per_turn, self.offset = self.value, per_turn, index * per_turn

    def leave(self, turns):
        assert self.value == self.begun + self.per_turn, self.value - self.begun
        self.value, self.offset = self.begun + turns * self.per_turn, 0


def gnn_moe_kernel(nc, x, src, dst, edge_weight, W, bias, W_gat, att_src, att_dst, b_gat,
                   ln_gamma, ln_beta, W1, b1, W2, b2, edge_index, out):
    F32, I32, F16, BF16 = mybir.dt.float32, mybir.dt.int32, mybir.dt.float16, mybir.dt.bfloat16
    ALU, ACT, AX = mybir.AluOpType, mybir.ActivationFunctionType, mybir.AxisListType.X
    ds = bass.ds

    N, D = x.shape
    KD = D // P
    NT = -(-N // P)
    N_LAST = N - (NT - 1) * P
    NP_ = NT * P
    E1 = src.shape[0]
    HALF = 13
    POOL_LANES = 9
    G = 2 * HALF
    NG = -(-E1 // (P * G))
    C1 = NG * G
    E1_LAST = E1 - (P - 1) * C1
    U = 8
    DU = 3
    K1 = -(-((P * C1 + (P - 1) * NT) // P) // U) * U
    L = -(-(P * G + 2 * (P - 1) * NT) // P // 2) * 2
    EX, _, HID = W1.shape
    KH = HID // P
    HEADS = att_src.shape[0]
    CH = HEADS * EX
    ROW = CH + 2 * HEADS
    E2 = edge_index.shape[1]
    C2E = E2 // P
    C2 = NT + C2E
    U2 = 12
    T2 = -(-C2 // U2)
    C2T = T2 * U2
    CG = -(-C2T // NG)
    SUB = 4
    SUBS = U2 // SUB
    LOOPS = -(-NT // U2)
    COUNT_TURNS = 3
    RANK_0 = COUNT_TURNS
    PLACE_TURN = RANK_0 + T2
    MOVE_0 = PLACE_TURN + 1
    MARK_0 = MOVE_0 + T2
    SLOTS = 6
    C2G = -(-C2 // SLOTS) * SLOTS
    NS = CH + HEADS
    T5 = 5
    assert NG % 2 == 0 and T2 % 2 == 0 and C2T % 3 == 0 and CG * NG == C2T and K1 // U == MARK_0 + LOOPS
    assert U2 % SUB == 0 and CG * NT <= 512
    assert NT % T5 == 0 and P * C2E == E2 and HID % P == 0 and L <= P and 0 < E1_LAST <= C1
    LN_EPS = 1e-5
    BIG = 1e30
    MIDDLE = float(NP_ // 2)
    NO_CHUNK = 4096.0
    GROUPS4 = -(-NT // 4)
    BLK = 512
    TB = BLK // P
    NBLK = NT // TB
    assert NT == NBLK * TB + 1 and NP_ // 2 <= 2048

    ctx = ExitStack()
    with ctx:
        def sb(name, shape, dt=F32):
            return ctx.enter_context(nc.sbuf_tensor(name, shape, dt))

        def sem(name):
            return ctx.enter_context(nc.semaphore(name))

        h_dram = nc.dram_tensor("h_rows", [NP_, D], F32, kind="Internal").ap()
        gat_dram = nc.dram_tensor("gat_rows", [NP_, ROW], F32, kind="Internal").ap()
        sums_dram = nc.dram_tensor("gat_sums", [P * C2, ROW], F32, kind="Internal").ap()
        rows_dram = nc.dram_tensor("gat_key_rows", [C2T, 2, P], F16, kind="Internal").ap()
        y_dram = nc.dram_tensor("expert_rows", [NP_, EX, D], F32, kind="Internal").ap()

        xs = sb("xs", [P, NT, D])
        big_t = sb("big_t", [P, KD * NP_])
        big_w = sb("big_w", [P, 2 * EX * KD * HID])
        big_h = sb("big_h", [P, 2 * KH * BLK])
        big_g = sb("big_g", [P, max(C2G * ROW, (C2T + 1) * NT)])
        big_y = sb("big_y", [P, 2 * TB * D])
        REGION = max(4 * K1 + 9 * C1, (4 * HEADS + 3) * C2)
        region = sb("region", [P, REGION])

        def part(place, start, shape, dt=F32):
            n = 1
            for s in shape:
                n *= s
            words = n if dt in (F32, I32) else -(-n // 2)
            assert start + words <= place.shape[1], (place.shape, start, shape)
            v = place[:, start:start + words]
            if dt is not F32:
                v = v.bitcast(dt)
            if len(shape) == 2:
                v = v.rearrange("p (a b) -> p a b", b=shape[1])
            elif len(shape) == 3:
                v = v.rearrange("p (a b c) -> p a b c", b=shape[1], c=shape[2])
            return v, start + words

        xT, _ = part(big_t, 0, [KD, NP_])
        ind5, n_ = part(big_t, 0, [T5, C1])
        at5, n_ = part(big_t, n_, [T5, C1])
        in5, n_ = part(big_t, n_, [T5, C1])
        rows2, n_ = part(big_t, 0, [2, U2, 2 * P], F16)
        rows2 = rows2.rearrange("p s u (v e) -> p s u v e", v=2)
        olT0, n_ = part(big_t, n_, [U2, P])
        rsel, n_ = part(big_t, n_, [U2, NT])
        same, n_ = part(big_t, n_, [U2, P], F16)
        ocol, n_ = part(big_t, 0, [U2, C2], F16)
        olane2, n_ = part(big_t, n_, [U2, P], F16)
        oval2, n_ = part(big_t, n_, [U2, P], F16)
        W1_sb, n_ = part(big_w, 0, [KD, EX, HID])
        W2_sb, _ = part(big_w, n_, [EX, KH, D])
        cum1, _ = part(big_w, 0, [NT, C1], F16)
        OH, n_ = part(big_w, 0, [C2T, NT], BF16)
        CT, n_ = part(big_w, n_, [C2T, NT], BF16)
        TK = C2T // 3
        key_rows, _ = part(big_w, n_, [3, 2 * P], F16)
        key_rows = key_rows.rearrange("p b (v e) -> p b v e", v=2)[0:TK, :, :, :]
        h_ff, _ = part(big_h, 0, [2, KH, BLK])
        olane1, _ = part(big_h, 0, [2, HALF, P])
        GT, _ = part(big_g, 0, [C2G, ROW])
        ochunk, n_ = part(big_g, 0, [2, HALF, L])
        pay_oh, n_ = part(big_g, n_, [2, HALF, 2 * L])
        PT, _ = part(big_g, 0, [C2T + 1, NT])
        y_sb, _ = part(big_y, 0, [2, TB * D])
        y_sb = y_sb.rearrange("p s (t d) -> p s t d", d=D)
        h_out, _ = part(big_y, 0, [T5, D])
        olT = (olT0, part(big_y, 0, [U2, P])[0])

        idx_s, n_ = part(region, 0, [K1], I32)
        w_s, n_ = part(region, n_, [K1])
        loc_s, n_ = part(region, n_, [K1])
        pack_i, n_ = part(region, n_, [K1], I32)
        n_sorting = n_
        lane1, n_ = part(region, n_, [C1])
        chunk1, n_ = part(region, n_, [C1])
        payload, n_ = part(region, n_, [2, C1])
        n_ranked = n_
        dst1, n_ = part(region, n_, [C1], I32)
        tile1, n_ = part(region, n_, [C1])
        n_tiled = n_
        src1, n_ = part(region, n_, [C1], I32)
        place1, n_ = part(region, n_, [C1])
        tmp1, n_ = part(region, n_, [C1], I32)
        lo2, n_ = part(region, n_ranked, [C2T])
        hi2, n_ = part(region, n_, [C2T])
        assert n_ <= n_tiled
        val2, n_ = part(region, n_, [C2T + LOOPS * U2])
        ol1, n_ = part(region, n_, [CG, P], BF16)
        pos2, n_ = part(region, n_sorting, [C2T])
        lane2, n_ = part(region, n_, [C2T + LOOPS * U2])
        col2, n_ = part(region, n_, [C2T + LOOPS * U2])
        tmp2, n_ = part(region, n_, [C2T])
        tmp2i, n_ = part(region, n_, [C2T], I32)
        SCANS = 4 * HEADS
        sums_part, _ = part(region, 0, [SCANS, C2])
        ad_e, n_ = part(region, 0, [HEADS, C2])
        e_e, n_ = part(region, n_, [HEADS, C2])
        f_e, n_ = part(region, n_, [HEADS, C2])
        s_e, n_ = part(region, n_, [HEADS, C2])
        keep, n_ = part(region, n_, [C2])
        drop_f, n_ = part(region, n_, [C2])
        drop_r, n_ = part(region, n_, [C2])

        ident = sb("ident", [P, P])
        tri = sb("tri", [P, P])
        ones = sb("ones", [P, P])
        iota16 = sb("iota16", [P, 512], F16)
        iota_k = sb("iota_k", [P, K1])
        iota_p = sb("iota_p", [P, 1])
        first_g, _ = part(big_h, 0, [NT, NG])
        bias_b = sb("bias_b", [P, D])
        w_sb = sb("w_sb", [P, KD, D])
        wgat_sb = sb("wgat_sb", [P, KD, CH])
        att_b = sb("att_b", [P, 2, CH])
        gam_b = sb("gam_b", [P, 3, CH])
        b1_sb = sb("b1_sb", [P, EX, KH])
        b2_sb = sb("b2_sb", [EX, D])
        mv = sb("mv", [P, NT, 2])
        rstd = sb("rstd", [P, 4, NT])
        eps_c = sb("eps_c", [P, 1])
        xn = sb("xn", [P, T5, D])
        xnT = sb("xnT", [P, T5, KD, P])
        bucket = sb("bucket", [P, 6, NT])
        bucket_i = sb("bucket_i", [P, NT], I32)
        global_chunk = sb("global_chunk", [P, 3, NG])
        ogc = sb("ogc", [L, 2, K1])
        keyc2 = sb("keyc2", [P, C2T])
        rank2 = sb("rank2", [P, C2T])
        stats, _ = part(rank2, 0, [NT, 6])
        tri16 = sb("tri16", [P, P], F16)
        lane_now = sb("lane_now", [P, POOL_LANES])
        group_sb = sb("group_sb", [P, 2, L])
        group_T = sb("group_T", [L, 2, P])
        zero_row = sb("zero_row", [1, K1])
        end_col = sb("end_col", [NT, 1])
        geq = ogc[0:NT, 0, :]
        tile_of_chunk = sb("tile_of_chunk", [1, K1], I32)
        idx_turn = sb("idx_turn", [P, 2, U], I32)
        big_m = sb("big_m", [P, U * (D + P)])
        msgs, n_ = part(big_m, 0, [U, D])
        S1, _ = part(big_m, n_, [U, P])
        cnt = [part(big_m, i * NT * NG, [NT, NG])[0] for i in range(6)]
        cnt_i, _ = part(big_m, 6 * NT * NG, [NT, NG], I32)
        by_g = [part(big_g, i * NT * NG, [NG, NT])[0] for i in range(3)]
        key2 = sb("key2", [P, C2], I32)
        src2 = sb("src2", [P, C2], I32)
        endpos = sb("endpos", [P, NT], I32)
        starts = sb("starts", [P, C2])
        src_sorted = sb("src_sorted", [P, C2G], I32)
        gat_slot = sb("gat_slot", [P, SLOTS, ROW])
        edge_cols = sb("edge_cols", [P, 2, NS])
        across = sb("across", [NS, 3, P + 1])
        carry = sb("carry", [P, 2, NS])
        flag_any = sb("flag_any", [P, 4])
        key_tile, _ = part(starts, 0, [C2], I32)
        node_sums, n_ = part(big_m, 0, [NT, ROW])
        agg, n_ = part(big_m, n_, [NT, CH])
        agg2, n_ = part(big_m, n_, [NT, CH])
        sc4 = sb("sc4", [P, EX, NT])
        gate = sb("gate", [P, EX, NT])
        rank4 = sb("rank4", [P, EX, NT])
        pair = bucket
        gT, n_ = part(big_g, 0, [NT, P])
        gT = gT[0:EX, :, :]
        diag, n_ = part(big_g, n_, [8, P])
        y_in = [part(place, i * EX * D, [EX, D])[0] for place, slots in ((big_h, 4), (big_w, 8), (big_t, 6)) for i in range(slots)]
        YS, Y_FIRST = len(y_in), 4

        bank = [ctx.enter_context(nc.psum_tensor(f"bank{i}", [P, 512], F32)) for i in range(8)]

        AGG = 4

        def agg_bank(u):
            return bank[(0, 1, 4, 5)[u % AGG]][:, 0:D]

        names = """ld_src ld_dst ld_wt ld_x ld_w ld_keys ld_ffw pads_set consts dve_step pool_step
            counts_ready counts_mm ends_ready ends_mm geq_ready geq_mm
            var_a std_a xn_ready_a xn_T_a xnT_copied_a proj_mm_a proj_taken_a
            var_b std_b xn_ready_b xn_T_b xnT_copied_b proj_mm_b proj_taken_b xT_done
            hots_ready hots_used group_copied group_T_mm group_T_copied ogc_ready moved_mm
            edges_ready onehot_ready slots_free act_squares act_relu act_onehot_ready idx_copied agg_free
            in_ready place_added bias_added ranks_done lane_hots_ready keys_ready tile_hots_ready
            squares_ready ol_ready cnt_mm cnt_copied tot2_ready base2_mm places_ready
            keys_T keys_T_copied key_rows_sent olT_squares olT_ready ranked r_mm r_used
            lanes_ready lane_squares lane_hots perm_ready perm_scaled perm_used perm_mm perm_taken
            table_ready table_sent gat_free gat_idx_copied
            up_mm up_free down_mm down_taken y_ready
            cols_ready cols_T across_ready across_T carried exp_in exp_out
            sums_ready sums_sent var_c std_c wexp_in wexp_out
            gate_ready gate_T gate_T_copied diag_ready gb_mm gb_used out_ready out_sent""".split()
        S = {n: sem(n) for n in names}
        h_sent = [sem(f"h_sent{u}") for u in range(T5)]
        gathered = [sem(f"gathered{u}") for u in range(U)]
        gat_in = [sem(f"gat_in{u}") for u in range(SLOTS)]
        y_stored = [sem(f"y_stored{s}") for s in range(2)]
        rows_landed = [sem(f"rows_landed{s}") for s in range(2)]
        y_loaded = [sem(f"y_loaded{s}") for s in range(YS)]
        sums_in = sem("sums_in")

        block = ctx.enter_context(nc.Block())

        @block.sync
        def _(sp):
            sp.wait_ge(S["pads_set"], 1)
            for place, array, landed in ((src1, src, "ld_src"), (dst1, dst, "ld_dst"),
                                         (payload[:, 0, :], edge_weight, "ld_wt")):
                sp.dma_start(place[0:P - 1, :], array[0:(P - 1) * C1].rearrange("(p c) -> p c", c=C1)).then_inc(S[landed], 16)
                sp.dma_start(place[P - 1:P, 0:E1_LAST], array[(P - 1) * C1:E1].rearrange("(p c) -> p c", p=1)).then_inc(S[landed], 16)
            sp.dma_start(xs[:, 0:NT - 1, :], x[0:(NT - 1) * P, :].rearrange("(t p) d -> p t d", p=P)).then_inc(S["ld_x"], 16)
            sp.dma_start(xs[0:N_LAST, NT - 1, :], x[(NT - 1) * P:N, :]).then_inc(S["ld_x"], 16)
            sp.dma_start(w_sb[:, :, :], W.rearrange("(k p) n -> p k n", p=P)).then_inc(S["ld_w"], 16)
            sp.dma_start(wgat_sb[:, :, :], W_gat.rearrange("(k p) n -> p k n", p=P)).then_inc(S["ld_w"], 16)
            sp.dma_start(bias_b[:, :], bias.unsqueeze(0).to_broadcast([P, D])).then_inc(S["ld_w"], 16)
            for i, v in enumerate((att_src, att_dst)):
                sp.dma_start(att_b[:, i, :], v.rearrange("h e -> (h e)").unsqueeze(0).to_broadcast([P, CH])).then_inc(S["ld_w"], 16)
            for i, v in enumerate((ln_gamma, ln_beta, b_gat)):
                sp.dma_start(gam_b[:, i, :], v.unsqueeze(0).to_broadcast([P, CH])).then_inc(S["ld_w"], 16)
            with nc.allow_non_contiguous_dma(reason="2048 bias words, once"):
                for e in range(EX):
                    sp.dma_start(b1_sb[:, e, :], b1[e, :].rearrange("(j p) -> p j", p=P)).then_inc(S["ld_w"], 16)
            sp.dma_start(b2_sb[:, :], b2).then_inc(S["ld_w"], 16)
            sp.dma_start(key2[:, NT:C2], edge_index[1, :].rearrange("(p c) -> p c", c=C2E)).then_inc(S["ld_keys"], 16)
            sp.dma_start(src2[:, NT:C2], edge_index[0, :].rearrange("(p c) -> p c", c=C2E)).then_inc(S["ld_keys"], 16)
            with sp.Fori(0, NT // T5) as i:
                for u in range(T5):
                    sp.wait_ge(S["proj_taken_a"], 2 + i * T5 + (u + 1))
                    sp.dma_start(h_dram[ds((i * T5 + u) * P, P), :], h_out[:, u, :]).then_inc(h_sent[u], 16)
            sp.wait_ge(S["keys_T_copied"], 6)
            sp.dma_start(rows_dram.rearrange("(b c) v e -> c b v e", b=3), key_rows[:, :, :, :]).then_inc(S["key_rows_sent"], 16)
            sp.wait_ge(S["key_rows_sent"], 16)
            sp.wait_ge(S["moved_mm"], 2 + NG)
            def load_rows(k, side):
                sp.dma_start(rows2[:, side, :, :, :], rows_dram[ds(k * U2, U2), :, :].unsqueeze(0).to_broadcast([P, U2, 2, P])
                             ).then_inc(rows_landed[side], 16)

            for side in range(2):
                load_rows(side, side)
            with sp.Fori(1, T2 // 2) as i:
                for side in range(2):
                    sp.wait_ge(S["ranked"], i * 2 + side - 1)
                    sp.wait_ge(S["olT_ready"], i * 2 + side - 1)
                    load_rows(i * 2 + side, side)
            sp.wait_ge(S["perm_taken"], 1)
            for e in range(EX):
                sp.dma_start(W1_sb[:, :, e, :], W1[e, :, :].rearrange("(k p) n -> p k n", p=P)).then_inc(S["ld_ffw"], 16)
                sp.dma_start(W2_sb[:, e, :, :], W2[e, :, :].rearrange("(k p) n -> p k n", p=P)).then_inc(S["ld_ffw"], 16)
            sp.wait_ge(S["table_ready"], 1)
            sp.dma_start(gat_dram.rearrange("(t p) r -> p t r", p=P), GT[:, 0:NT, :]).then_inc(S["table_sent"], 16)

            def store_y(tile0, tiles, e, nth):
                sp.wait_ge(S["y_ready"], nth)
                sp.dma_start(y_dram[ds(tile0 * P, tiles * P), e, :].rearrange("(t p) d -> p t d", p=P),
                             y_sb[:, e % 2, 0:tiles, :]).then_inc(y_stored[e % 2], 16)

            with sp.Fori(0, NBLK) as i:
                for e in range(EX):
                    store_y(i * TB, TB, e, i * EX + (e + 1))
            for e in range(EX):
                store_y(NBLK * TB, 1, e, NBLK * EX + e + 1)
            for s in range(2):
                sp.wait_ge(y_stored[s], 16 * (EX // 2) * (NBLK + 1))
            sp.wait_ge(S["down_mm"], 2 * TB + EX * (NBLK * TB + 1))

            def load_y(t):
                sp.dma_start(y_in[t % YS], y_dram[t * P:(t + 1) * P, :, :]).then_inc(y_loaded[t % YS], 16)

            for t in range(YS):
                if t == Y_FIRST:
                    sp.wait_ge(sums_in, 16 * NT)
                load_y(t)
            for t in range(NT):
                sp.wait_ge(S["out_ready"], t + 1)
                rows = P if t < NT - 1 else N_LAST
                sp.dma_start(out[t * P:t * P + rows, :], xs[0:rows, t, :]).then_inc(S["out_sent"], 16)
                if t + YS < NT:
                    load_y(t + YS)
            sp.wait_ge(S["out_sent"], 16 * NT)

        @block.gpsimd
        def _(pool):
            steps = Steps(pool, S["pool_step"])
            steps.mark(pool.memset(xs[:, NT - 1, :], 0.0))
            for v in (src1, dst1, payload[:, 0, :]):
                steps.mark(pool.memset(v, 0))
            steps.wait()
            pool.nop().then_inc(S["pads_set"], 1)
            steps.mark(pool.memset(ident[:, :], 0.0))
            steps.mark(pool.memset(ones[:, :], 1.0))
            steps.mark(pool.memset(tri[:, :], 1.0))
            steps.mark(pool.memset(first_g[:, :, :], 1.0))
            steps.mark(pool.memset(zero_row[:, :], 0.0))
            steps.mark(pool.memset(eps_c[:, :], LN_EPS))
            for v, pattern, cm in ((iota16[:, :], [[1, 512]], 0), (iota_k[:, :], [[1, K1]], 0), (iota_p[:, :], [[0, 1]], 1)):
                steps.mark(pool.iota(v, pattern=pattern, base=0, channel_multiplier=cm, allow_small_or_imprecise_dtypes=True))
            steps.wait()
            steps.mark(pool.memset(first_g[:, :, 0:1], 0.0))
            steps.mark(pool.affine_select(out=ident[:, :], in_=ident[:, :], compare_op=ALU.not_equal, fill=1.0, base=0,
                                          pattern=[[-1, P]], channel_multiplier=1))
            steps.mark(pool.affine_select(out=tri[:, :], in_=tri[:, :], compare_op=ALU.is_gt, fill=0.0, base=0,
                                          pattern=[[1, P]], channel_multiplier=-1))
            steps.mark(pool.iota(key2[:, 0:NT], pattern=[[P, NT]], base=0, channel_multiplier=1))
            steps.mark(pool.iota(src2[:, 0:NT], pattern=[[P, NT]], base=0, channel_multiplier=1))
            steps.wait()
            steps.done(pool.memset(tri16[:, :], 1.0))
            steps.done(pool.affine_select(out=tri16[:, :], in_=tri16[:, :], compare_op=ALU.is_gt, fill=0.0, base=0,
                                          pattern=[[-1, P]], channel_multiplier=1))
            pool.nop().then_inc(S["consts"], 1)

            pool.wait_ge(S["xn_ready_a"], NT)
            pool.wait_ge(S["ld_w"], 16 * (8 + EX + 1))
            pool.tensor_tensor(xs[:, :, :], xs[:, :, :], bias_b[:, :].unsqueeze(1).to_broadcast([P, NT, D]), ALU.add).then_inc(S["bias_added"], 1)
            steps.done(pool.memset(place1, 0.0))
            pool.nop().then_inc(S["place_added"], T5)
            with pool.Fori(0, NT // T5) as i:
                for u in range(T5):
                    pool.wait_ge(S["in_ready"], 1 + i * T5 + (u + 1))
                    pool.wait_ge(S["place_added"], T5 + i * T5 + u)
                    pool.nop(nofuse=True)
                    pool.tensor_tensor(place1, place1, in5[:, u, :], ALU.add).then_inc(S["place_added"], 1)

            pool.wait_ge(S["ranks_done"], 1)
            with pool.Fori(0, NG) as g:
                pool.wait_ge(S["hots_used"], g * 2 + 1)
                steps.enter(g, 1)
                steps.done(pool.tensor_copy(lane_now[:, :], lane1[:, ds(g * G, POOL_LANES)]))
                steps.leave(NG)
                pool.nop(nofuse=True)
                for c in range(POOL_LANES):
                    last = pool.tensor_scalar(olane1[:, 0, c, :], iota_k[:, 0:P], lane_now[:, c:c + 1], None, ALU.is_equal)
                last.then_inc(S["lane_hots_ready"], 1)

            pool.wait_ge(S["ld_keys"], 32)
            steps.done(pool.memset(val2, 0.0))
            steps.mark(pool.tensor_scalar(val2[:, 0:C2], src2[:, :], MIDDLE, None, ALU.subtract))
            steps.mark(pool.memset(val2[:, C2T:C2T + NT], 1.0))
            steps.wait()

            pool.wait_ge(S["edges_ready"], 1)
            for u in range(T5):
                pool.wait_ge(h_sent[u], 16 * (NT // T5))

            def gather_turn(turn, side, slots, rows, numbers, table, free, copied, landed):
                pool.tensor_copy(idx_turn[:, side, 0:slots], numbers[:, ds(turn * slots, slots)]).then_inc(copied, 1)
                pool.wait_ge(copied, turn + 1)
                for u in range(slots):
                    pool.wait_ge(free, turn * slots + (u + 1))
                    pool.nop(nofuse=True)
                    pool.indirect_dma_start(rows[:, u, :], None, table,
                                            bass.IndirectOffsetOnAxis(ap=idx_turn[:, side, u:u + 1], axis=0)).then_inc(landed[u], 16)

            def gather_all(turns, *how):
                with pool.Fori(0, turns // 2) as i:
                    gather_turn(i * 2, 0, *how)
                    gather_turn(i * 2 + 1, 1, *how)
                for turn in range(turns // 2 * 2, turns):
                    gather_turn(turn, 0, *how)

            gather_all(K1 // U, U, msgs, idx_s, h_dram, S["slots_free"], S["idx_copied"], gathered)

            pool.wait_ge(S["slots_free"], U + K1)
            pool.wait_ge(S["perm_taken"], 1)
            pool.wait_ge(S["table_sent"], 16)
            gather_all(C2G // SLOTS, SLOTS, gat_slot, src_sorted, gat_dram, S["gat_free"], S["gat_idx_copied"], gat_in)

            pool.wait_ge(S["sums_ready"], 1)
            pool.dma_start(sums_dram.rearrange("(p c) r -> p (c r)", p=P), GT[:, 0:C2, :].rearrange("p c r -> p (c r)")).then_inc(S["sums_sent"], 16)
            pool.wait_ge(S["sums_sent"], 16)
            for t in range(NT):
                pool.indirect_dma_start(node_sums[:, t, :], None, sums_dram,
                                        bass.IndirectOffsetOnAxis(ap=endpos[:, t:t + 1], axis=0)).then_inc(sums_in, 16)

        def ln_act(act, which):
            out_rows = (lambda i, u: h_out[:, u, :]) if which == "a" else (lambda i, u: GT[:, ds(i * T5 + u, 1), 0:CH])

            def copy(i, u):
                act.wait_ge(S[f"xn_T_{which}"], T5 + i * T5 + (u + 1))
                act.wait_ge(S[f"proj_mm_{which}"], i * T5 + (u + 1))
                if which == "b":
                    act.wait_ge(S["xT_done"], i * T5 + (u + 1))
                view = bank[u][:, 0:D].rearrange("p (k n) -> p k n", k=KD)
                nc.scalar.activation(xnT[:, u, :, :], view, ACT.Copy).then_inc(S[f"xnT_copied_{which}"], 1)

            def take(i, u, first):
                act.wait_ge(S[f"proj_mm_{which}"], T5 + i * T5 + (u + 1))
                if which == "a" and not first:
                    act.wait_ge(h_sent[u], i * 16)
                width = D if which == "a" else CH
                nc.scalar.activation(out_rows(i, u), bank[5 + u % 3][:, 0:width], ACT.Copy).then_inc(S[f"proj_taken_{which}"], 1)

            def turn(i, first=False):
                for u in range(T5 + 1):
                    if u < T5:
                        copy(i, u)
                    if u:
                        take(i, u - 1, first)

            turn(0, True)
            with act.Fori(1, NT // T5) as i:
                turn(i)

        @block.scalar
        def _(act):
            act.nop().then_inc(S["xnT_copied_a"], T5)
            act.nop().then_inc(S["xnT_copied_b"], T5)
            act.nop().then_inc(S["proj_taken_a"], 2)
            act.nop().then_inc(S["proj_taken_b"], 2)
            act.nop().then_inc(S["group_copied"], 2)
            act.nop().then_inc(S["cnt_copied"], 1)
            act.nop().then_inc(S["perm_scaled"], 1)
            act.nop().then_inc(S["up_free"], KH)
            act.nop().then_inc(S["down_taken"], TB)
            act.wait_ge(S["var_a"], 1)
            nc.scalar.activation(rstd[:, 1, :], rstd[:, 0, :], ACT.Sqrt).then_inc(S["std_a"], 1)
            ln_act(act, "a")
            for n in range(6):
                act.wait_ge(S["keys_T"], n + 1)
                nc.scalar.activation(key_rows[:, n // 2, n % 2, :], bank[n][0:TK, 0:P], ACT.Copy).then_inc(S["keys_T_copied"], 1)
            act.wait_ge(S["keys_ready"], 1)
            act.wait_ge(S["ranks_done"], 1)

            def group_leaves(g, side):
                act.wait_ge(S["hots_used"], g * 2 + 4)
                act.wait_ge(S["group_T_mm"], g + 1)
                nc.scalar.activation(group_sb[:, :, :], bank[3 + side][:, 0:2 * L].rearrange("p (v l) -> p v l", v=2),
                                     ACT.Copy).then_inc(S["group_copied"], 1)

            def counts_leave(g):
                act.wait_ge(S["cnt_mm"], g + 2)
                nc.scalar.activation(CT[:, ds(g * CG, CG), :], bank[0][:, 0:CG * NT].rearrange("p (u t) -> p u t", u=CG),
                                     ACT.Copy).then_inc(S["cnt_copied"], 1)

            def group_T_leaves(g):
                act.wait_ge(S["group_T_mm"], g + 2)
                act.wait_ge(S["moved_mm"], g + 2)
                nc.scalar.activation(group_T[:, :, :], bank[5][0:L, 0:2 * P].rearrange("p (v l) -> p v l", v=2),
                                     ACT.Copy).then_inc(S["group_T_copied"], 1)

            def squares(g):
                for u in range(CG):
                    last = nc.scalar.activation(ol1[:, u, :], iota16[:, 0:P], ACT.Square, scale=-1.0, bias=lo2[:, ds(g * CG + u, 1)])
                last.then_inc(S["squares_ready"], 1)

            def sort_turn(g, side, first=False):
                if not first:
                    group_leaves(g - 1, 1 - side)
                    counts_leave(g - 1)
                squares(g)
                if not first:
                    group_T_leaves(g - 1)
                act.wait_ge(S["squares_ready"], g + 1)
                nc.scalar.activation(ol1, ol1, ACT.Relu, scale=-2.0, bias=ones[:, 0:1]).then_inc(S["ol_ready"], 1)

            sort_turn(0, 0, True)
            sort_turn(1, 1)
            with act.Fori(1, NG // 2) as i:
                for side in range(2):
                    sort_turn(i * 2 + side, side)
            group_leaves(NG - 1, 1)
            counts_leave(NG - 1)
            group_T_leaves(NG - 1)
            act.wait_ge(S["cnt_copied"], NG + 1)
            for t in range(NT):
                last = nc.scalar.activation(PT[:, 1:C2T + 1, t], CT[:, :, t], ACT.Copy, accum_out=bucket[:, 0, t:t + 1])
            last.then_inc(S["tot2_ready"], 1)
            def row_hots(i, side):
                k = i * 2 + side
                act.wait_ge(rows_landed[side], i * 16 + 16)
                act.wait_ge(S["r_mm"], k + 1)
                nc.scalar.activation(olT[side], rows2[:, side, :, 0, :], ACT.Square, scale=-1.0, bias=iota_p[:, 0:1]).then_inc(S["olT_squares"], 1)
                act.wait_ge(S["olT_squares"], k + 1)
                nc.scalar.activation(olT[side], olT[side], ACT.Relu, scale=-2.0, bias=ones[:, 0:1]).then_inc(S["olT_ready"], 1)

            for u in range(T5):
                act.wait_ge(h_sent[u], 16 * (NT // T5))

            def dest_hots(k):
                last_u = range(DU, U)
                act.wait_ge(S["slots_free"], (k + RANK_0) * U + U)
                for u in last_u:
                    last = nc.scalar.activation(S1[:, u, :], iota16[:, 0:P], ACT.Square, scale=-1.0,
                                                bias=loc_s[:, ds((k + RANK_0) * U + u, 1)])
                last.then_inc(S["act_squares"], 1)
                act.wait_ge(S["act_squares"], k + 1)
                nc.scalar.activation(S1[:, DU:U, :], S1[:, DU:U, :], ACT.Relu, scale=-2.0, bias=ones[:, 0:1]).then_inc(S["act_relu"], 1)
                act.wait_ge(S["act_relu"], k + 1)
                for u in last_u:
                    last = nc.scalar.activation(S1[:, u, :], S1[:, u, :], ACT.Copy, scale=w_s[:, ds((k + RANK_0) * U + u, 1)])
                last.then_inc(S["act_onehot_ready"], 1)

            row_hots(0, 0)
            with act.Fori(0, T2 // 2 - 1) as i:
                dest_hots(i * 2)
                row_hots(i, 1)
                dest_hots(i * 2 + 1)
                row_hots(i + 1, 0)
            dest_hots(T2 - 2)
            row_hots(T2 // 2 - 1, 1)
            dest_hots(T2 - 1)
            dest_hots(T2)
            act.wait_ge(S["lanes_ready"], 1)
            with act.Fori(0, T2 + LOOPS) as i:
                act.wait_ge(S["perm_scaled"], i * SUBS + 1)
                for u in range(U2):
                    last = nc.scalar.activation(olane2[:, u, :], iota16[:, 0:P], ACT.Square, scale=-1.0, bias=lane2[:, ds(i * U2 + u, 1)])
                last.then_inc(S["lane_squares"], 1)
                act.wait_ge(S["lane_squares"], i + 1)
                nc.scalar.activation(olane2, olane2, ACT.Relu, scale=-2.0, bias=ones[:, 0:1]).then_inc(S["lane_hots"], 1)
                act.wait_ge(S["lane_hots"], i + 1)
                for q in range(SUBS):
                    act.wait_ge(S["perm_used"], i * SUBS + (q + 1))
                    for u in range(q * SUB, (q + 1) * SUB):
                        last = nc.scalar.activation(oval2[:, u, :], olane2[:, u, :], ACT.Copy, scale=val2[:, ds(i * U2 + u, 1)])
                    last.then_inc(S["perm_scaled"], 1)
            act.wait_ge(S["var_b"], 1)
            nc.scalar.activation(rstd[:, 1, :], rstd[:, 0, :], ACT.Sqrt).then_inc(S["std_b"], 1)
            ln_act(act, "b")

            def hidden(tokens, e, up_before, down_before):
                act.wait_ge(S["down_mm"], 2 * TB + down_before)
                for j in range(KH):
                    act.wait_ge(S["up_mm"], up_before + (j + 1))
                    nc.scalar.activation(h_ff[:, e % 2, j, 0:tokens], bank[j][:, 0:tokens], ACT.Gelu,
                                         bias=b1_sb[:, e, j:j + 1]).then_inc(S["up_free"], 1)

            def rows(tiles, e, down_before, stored_before):
                if stored_before is not None:
                    act.wait_ge(y_stored[e % 2], stored_before)
                for t in range(tiles):
                    act.wait_ge(S["down_mm"], 2 * TB + down_before + (t + 1))
                    nc.scalar.activation(y_sb[:, e % 2, t, :], bank[4 + t][:, 0:D], ACT.Copy).then_inc(S["down_taken"], 1)
                act.wait_ge(S["down_taken"], TB + down_before + tiles)
                act.nop().then_inc(S["y_ready"], 1)

            def block_act(i, first, last=False):
                for e in range(EX + 1):
                    if e < EX:
                        hidden(BLK, e, (i * EX + e) * KH, (i * EX + (e - 1)) * TB)
                    if last and e == 2:
                        act.wait_ge(S["exp_in"], 1)
                        nc.scalar.activation(e_e[:, :, :], e_e[:, :, :], ACT.Exp).then_inc(S["exp_out"], 1)
                    if e:
                        stored = None if first and e - 1 < 2 else (i * (EX // 2) + (e - 1) // 2) * 16
                        rows(TB, e - 1, (i * EX + (e - 1)) * TB, stored)

            act.wait_ge(S["ld_w"], 16 * (8 + EX + 1))
            block_act(0, True)
            with act.Fori(1, NBLK - 1) as i:
                block_act(i, False)
            block_act(NBLK - 1, False, last=True)
            all_before = NBLK * EX * TB
            for e in range(EX + 1):
                if e < EX:
                    hidden(P, e, (NBLK * EX + e) * KH, all_before - TB if e == 0 else all_before + e - 1)
                if e:
                    rows(1, e - 1, all_before + e - 1, (NBLK * (EX // 2) + (e - 1) // 2) * 16)
            act.wait_ge(S["var_c"], 1)
            nc.scalar.activation(pair[:, 1, :], pair[:, 0, :], ACT.Sqrt).then_inc(S["std_c"], 1)
            act.wait_ge(S["wexp_in"], 1)
            nc.scalar.activation(gate[:, :, :], gate[:, :, :], ACT.Exp).then_inc(S["wexp_out"], 1)
            act.wait_ge(S["gate_ready"], 1)
            for j in range(GROUPS4):
                tiles = min(4, NT - j * 4)
                act.wait_ge(S["gate_T"], j + 1)
                nc.scalar.activation(gT[:, 4 * j:4 * j + tiles, :],
                                     bank[2 + j % 2][0:EX, 0:tiles * P].rearrange("p (t n) -> p t n", n=P), ACT.Copy).then_inc(S["gate_T_copied"], 1)
                for t in range(4 * j, 4 * j + tiles):
                    if t >= 4:
                        act.wait_ge(S["gb_mm"], t - 3)
                    for e in range(2):
                        last = nc.scalar.activation(diag[:, t % 4 * 2 + e, :], ident[:, :], ACT.Copy, scale=gate[:, EX - 2 + e, t:t + 1])
                    last.then_inc(S["diag_ready"], 1)

        def ln_pe(pe, which):
            rhs = w_sb if which == "a" else wgat_sb
            width = D if which == "a" else CH

            def transpose(i, u):
                pe.wait_ge(S[f"xn_ready_{which}"], i * T5 + (u + 1))
                pe.wait_ge(S[f"xnT_copied_{which}"], i * T5 + (u + 1))
                for k in range(KD):
                    last = nc.tensor.transpose(bank[u][:, k * P:(k + 1) * P], xn[:, u, k * P:(k + 1) * P], ident[:, :])
                last.then_inc(S[f"xn_T_{which}"], 1)

            def project(i, u):
                pe.wait_ge(S[f"xnT_copied_{which}"], T5 + i * T5 + (u + 1))
                pe.wait_ge(S[f"proj_taken_{which}"], i * T5 + (u + 1))
                for k in range(KD):
                    last = nc.tensor.matmul(bank[5 + u % 3][:, 0:width], xnT[:, u, k, :], rhs[:, k, :],
                                            start=(k == 0), stop=(k == KD - 1))
                last.then_inc(S[f"proj_mm_{which}"], 1)

            with pe.Fori(0, NT // T5) as i:
                for u in range(T5 + 1):
                    if u < T5:
                        transpose(i, u)
                    if u:
                        project(i, u - 1)
            pe.wait_ge(S[f"proj_taken_{which}"], 2 + NT)

        @block.tensor
        def _(pe):
            pe.nop().then_inc(S["xn_T_a"], T5)
            pe.nop().then_inc(S["xn_T_b"], T5)
            pe.nop().then_inc(S["proj_mm_a"], T5)
            pe.nop().then_inc(S["proj_mm_b"], T5)
            pe.nop().then_inc(S["hots_used"], 2)
            pe.nop().then_inc(S["moved_mm"], 2)
            pe.nop().then_inc(S["group_T_mm"], 1)
            pe.nop().then_inc(S["slots_free"], U)
            pe.nop().then_inc(S["cnt_mm"], 1)
            pe.nop().then_inc(S["perm_used"], SUBS)
            pe.nop().then_inc(S["r_mm"], 2)
            pe.nop().then_inc(S["down_mm"], 2 * TB)
            pe.wait_ge(S["consts"], 1)
            pe.wait_ge(S["ld_w"], 16 * (8 + EX + 1))
            ln_pe(pe, "a")
            pe.wait_ge(S["counts_ready"], 1)
            flat = cnt[0][:, :, :].rearrange("p b g -> p (b g)")
            nc.tensor.matmul(bank[0][:, 0:NT * NG], tri[:, :], flat, start=True, stop=True)
            nc.tensor.matmul(bank[1][:, 0:NT * NG], ones[:, :], flat, start=True, stop=True).then_inc(S["counts_mm"], 1)
            pe.wait_ge(S["ends_ready"], 1)
            nc.tensor.matmul(bank[2][0:NT, 0:1], bucket[0:1, 3, :], ones[0:1, 0:1], start=True, stop=True).then_inc(S["ends_mm"], 1)
            pe.wait_ge(S["geq_ready"], 1)
            nc.tensor.matmul(bank[3][0:1, 0:K1], ones[0:NT, 0:1], geq, start=True, stop=True).then_inc(S["geq_mm"], 1)
            pe.wait_ge(S["keys_ready"], 1)
            for n in range(6):
                nc.tensor.transpose(bank[n][0:TK, 0:P], (lo2, keyc2)[n % 2][:, n // 2 * TK:(n // 2 + 1) * TK], ident[:, :]).then_inc(S["keys_T"], 1)
            pe.wait_ge(S["keys_T_copied"], 6)

            def sum_half(g, side, half):
                if half == 0:
                    pe.wait_ge(S["group_copied"], g + 1)
                    pe.wait_ge(S["lane_hots_ready"], g + 1)
                pe.wait_ge(S["hots_ready"], g * 2 + (half + 1))
                for c in range(HALF):
                    last = nc.tensor.matmul(bank[3 + side][:, 0:2 * L], olane1[:, half, c, :], pay_oh[:, half, c, :],
                                            start=(half == 0 and c == 0), stop=(half == 1 and c == HALF - 1))
                last.then_inc(S["hots_used"], 1)

            def transpose_group(g):
                pe.wait_ge(S["group_copied"], g + 3)
                for v in range(2):
                    last = nc.tensor.transpose(bank[5][0:L, v * P:(v + 1) * P], group_sb[:, v, :], ident[:, :])
                last.then_inc(S["group_T_mm"], 1)

            def move_group(g, side, start=False, stop=False):
                pe.wait_ge(S["group_T_copied"], g + 1)
                pe.wait_ge(S["ogc_ready"], g + 1)
                for v in range(2):
                    last = nc.tensor.matmul(bank[6 + v][:, 0:K1], group_T[:, v, :], ogc[:, side, :], start=start, stop=stop)
                last.then_inc(S["moved_mm"], 1)

            def sort_turn(g, side, first=False, second=False):
                sum_half(g, side, 0)
                if not first:
                    transpose_group(g - 1)
                sum_half(g, side, 1)
                if not first:
                    move_group(g - 1, 1 - side, start=second)
                pe.wait_ge(S["tile_hots_ready"], g + 1)
                pe.wait_ge(S["ol_ready"], g + 1)
                pe.wait_ge(S["cnt_copied"], g + 1)
                for u in range(CG):
                    last = nc.tensor.matmul(bank[0][:, u * NT:(u + 1) * NT], ol1[:, u, :],
                                            OH[:, ds(g * CG + u, 1), :].rearrange("p a t -> p (a t)"), start=True, stop=True)
                last.then_inc(S["cnt_mm"], 1)

            sort_turn(0, 0, True)
            sort_turn(1, 1, second=True)
            with pe.Fori(1, NG // 2) as i:
                for side in range(2):
                    sort_turn(i * 2 + side, side)
            transpose_group(NG - 1)
            move_group(NG - 1, 1, stop=True)
            def sum_chunk(turn, u, k=None, by_act=0):
                if k is None:
                    pe.wait_ge(S["onehot_ready"], turn * U + (u + 1 - by_act))
                elif u < DU:
                    pe.wait_ge(S["onehot_ready"], k * DU + (RANK_0 * U + u + 1))
                else:
                    pe.wait_ge(S["act_onehot_ready"], k + 1)
                pe.wait_ge(S["agg_free"], turn * U + (u + 1))
                pe.wait_ge(gathered[u], turn * 16 + 16)
                nc.tensor.matmul(agg_bank(u), S1[:, u, :], msgs[:, u, :], start=True, stop=True).then_inc(S["slots_free"], 1)

            def move(k, q, into):
                pe.wait_ge(S["perm_scaled"], k * SUBS + (q + 2))
                pe.wait_ge(S["perm_ready"], k * SUBS + (q + 1))
                for u in range(q * SUB, (q + 1) * SUB):
                    last = nc.tensor.matmul(into[:, 0:C2], oval2[:, u, :], ocol[:, u, :], start=False, stop=False)
                last.then_inc(S["perm_used"], 1)

            pe.wait_ge(S["cnt_copied"], NG + 1)
            for u in range(U):
                sum_chunk(0, u)
            pe.wait_ge(S["tot2_ready"], 1)
            nc.tensor.matmul(bank[2][:, 0:NT], tri[:, :], bucket[:, 0, :], start=True, stop=True)
            nc.tensor.matmul(bank[3][:, 0:NT], ones[:, :], bucket[:, 0, :], start=True, stop=True).then_inc(S["base2_mm"], 1)
            with pe.Fori(1, COUNT_TURNS) as i:
                for u in range(U):
                    sum_chunk(i, u)
            pe.wait_ge(S["places_ready"], 1)
            def rank_turn(i, side):
                k = i * 2 + side
                for u in range(U):
                    sum_chunk(k + RANK_0, u, k)
                    if u == 0:
                        pe.wait_ge(S["olT_ready"], k + 1)
                        pe.wait_ge(S["r_used"], k + 1)
                        for c in range(U2):
                            last = nc.tensor.matmul(bank[6 + side][:, c * NT:(c + 1) * NT], olT[side][:, c, :],
                                                    PT[:, ds(k * U2 + c, 1), :].rearrange("p a t -> p (a t)"), start=True, stop=True)
                        last.then_inc(S["r_mm"], 1)

            with pe.Fori(0, T2 // 2) as i:
                for side in range(2):
                    rank_turn(i, side)
            for b in range(2):
                nc.tensor.matmul(bank[2 + b][:, 0:C2], zero_row[:, 0:P], zero_row[:, 0:C2], start=True, stop=False)
            for u in range(U):
                sum_chunk(PLACE_TURN, u, T2)

            def move_turn(k, into):
                for u in range(U):
                    sum_chunk(k + MOVE_0, u, by_act=(T2 + 1) * (U - DU))
                    if u in (3, 5, 7):
                        move(k, (u - 3) // 2, into)

            with pe.Fori(0, T2) as i:
                move_turn(i, bank[2])
            with pe.Fori(T2, T2 + LOOPS) as i:
                move_turn(i, bank[3])
            for b in range(2):
                last = nc.tensor.matmul(bank[2 + b][:, 0:C2], zero_row[:, 0:P], zero_row[:, 0:C2], start=False, stop=True)
            last.then_inc(S["perm_mm"], 1)
            pe.wait_ge(S["agg_free"], K1 + AGG)
            pe.wait_ge(S["perm_taken"], 1)
            ln_pe(pe, "b")

            def up(tokens, e, off, up_before):
                for j in range(KH):
                    pe.wait_ge(S["up_free"], up_before + (j + 1))
                    for k in range(KD):
                        last = nc.tensor.matmul(bank[j][:, 0:tokens], W1_sb[:, k, e, j * P:(j + 1) * P],
                                                xT[:, k, ds(off, tokens)], start=(k == 0), stop=(k == KD - 1))
                    last.then_inc(S["up_mm"], 1)

            def down(tiles, e, up_before, taken):
                pe.wait_ge(S["up_free"], up_before + 2 * KH)
                for t in range(tiles):
                    pe.wait_ge(S["down_taken"], taken + t)
                    for j in range(KH):
                        last = nc.tensor.matmul(bank[4 + t][:, 0:D], h_ff[:, e % 2, j, t * P:(t + 1) * P], W2_sb[:, e, j, :],
                                                start=(j == 0), stop=(j == KH - 1))
                    last.then_inc(S["down_mm"], 1)

            pe.wait_ge(S["xT_done"], T5 + NT)
            pe.wait_ge(S["ld_ffw"], 16 * 2 * EX)
            def block_pe(i, between=lambda e: None):
                for e in range(EX + 1):
                    if e < EX:
                        up(BLK, e, i * BLK, (i * EX + e) * KH)
                    between(e)
                    if e:
                        down(TB, e - 1, (i * EX + (e - 1)) * KH, (i * EX + (e - 1)) * TB + 1)

            with pe.Fori(0, NBLK - 1) as i:
                block_pe(i)

            exchanges = ((HEADS, 0), (HEADS, 0), (HEADS, 1), (NS, 0))

            def exchange(q):
                k, shift = exchanges[q]
                pe.wait_ge(S["cols_ready"], q + 1)
                nc.tensor.transpose(bank[6][0:k, 0:P], edge_cols[:, 0, 0:k], ident[:, :])
                nc.tensor.transpose(bank[6][0:k, P:2 * P], edge_cols[:, 1, 0:k], ident[:, :]).then_inc(S["cols_T"], 1)
                pe.wait_ge(S["across_ready"], q + 1)
                nc.tensor.transpose(bank[7][:, 0:k], across[0:k, 2, shift:shift + P], ident[0:k, 0:k]).then_inc(S["across_T"], 1)

            def exchange_between(e):
                if e in (2, 3):
                    pe.wait_ge(S["down_taken"], TB + ((NBLK - 1) * EX + e - 1) * TB)
                    for q in (range(3) if e == 2 else (3,)):
                        exchange(q)
                    pe.wait_ge(S["carried"], 3 if e == 2 else 4)

            block_pe(NBLK - 1, exchange_between)
            for e in range(EX + 1):
                if e < EX:
                    up(P, e, NBLK * BLK, (NBLK * EX + e) * KH)
                if e:
                    m = NBLK * EX
                    down(1, e - 1, (m + e - 1) * KH, m * TB + 1 if e == 1 else TB + m * TB + e - 1)
            pe.wait_ge(S["down_taken"], TB + NBLK * EX * TB + EX)
            pe.wait_ge(S["gate_ready"], 1)
            for j in range(GROUPS4 + 1):
                if j < GROUPS4:
                    if j >= 2:
                        pe.wait_ge(S["gate_T_copied"], j - 1)
                    for t in range(4 * j, min(4 * j + 4, NT)):
                        last = nc.tensor.transpose(bank[2 + j % 2][0:EX, (t % 4) * P:(t % 4 + 1) * P], gate[:, :, t], ident[:, :])
                    last.then_inc(S["gate_T"], 1)
                if j == 0:
                    continue
                pe.wait_ge(S["gate_T_copied"], j)
                for t in range(4 * j - 4, min(4 * j, NT)):
                    if t >= 4:
                        pe.wait_ge(S["gb_used"], t - 3)
                    rows = bank[(0, 1, 4, 5)[t % 4]][:, 0:D]
                    nc.tensor.matmul(rows, gT[:, t, :], b2_sb[:, :], start=True, stop=False)
                    pe.wait_ge(S["diag_ready"], t + 1)
                    pe.wait_ge(y_loaded[t % YS], 16 * (t // YS + 1))
                    for e in range(2):
                        last = nc.tensor.matmul(rows, diag[:, t % 4 * 2 + e, :], y_in[t % YS][:, EX - 2 + e, :], start=False, stop=(e == 1))
                    last.then_inc(S["gb_mm"], 1)

        @block.vector
        def _(dve):
            steps = Steps(dve, S["dve_step"])
            V = nc.vector
            dve.nop().then_inc(S["agg_free"], AGG)
            dve.nop().then_inc(S["r_used"], 2)
            dve.nop().then_inc(S["gat_free"], SLOTS)
            dve.nop().then_inc(S["xT_done"], T5)
            dve.nop().then_inc(S["in_ready"], 1)

            dve.wait_ge(S["consts"], 1)
            dve.wait_ge(S["ld_src"], 32)
            dve.wait_ge(S["ld_dst"], 32)
            dve.wait_ge(S["ld_wt"], 32)
            steps.mark(V.tensor_copy(payload[:, 1, :], dst1))
            steps.done(V.tensor_single_scalar(tmp1, src1, 7, ALU.logical_shift_right))
            steps.mark(V.tensor_copy(tile1, tmp1))
            steps.done(V.tensor_single_scalar(src1, src1, P - 1, ALU.bitwise_and))
            steps.done(V.tensor_copy(lane1, src1))
            steps.done(V.scalar_tensor_tensor(payload[:, 1, :], payload[:, 1, :], float(P), lane1, ALU.mult, ALU.add))
            def statistics(which):
                with dve.Fori(0, NT // T5) as i:
                    steps.enter(i, T5)
                    for u in range(T5):
                        t = ds(i * T5 + u, 1)
                        steps.mark(V.bn_stats(stats[:, t, :].rearrange("p a s -> p (a s)"), xs[:, t, :].rearrange("p a d -> p (a d)")))
                    steps.leave(NT // T5)
                steps.wait()
                for t in range(NT):
                    steps.mark(V.bn_aggr(mv[:, t, :], stats[:, t, :]))
                steps.wait()
                inverse_deviation(rstd, mv[:, :, 1], which)

            def apply_turn(i, which, keep_before):
                for u in range(T5):
                    t = ds(i * T5 + u, 1)
                    if keep_before:
                        keep_transposed(i - 1, u)
                    dve.wait_ge(S[f"xn_T_{which}"], i * T5 + (u + 1))
                    V.tensor_scalar(xn[:, u, :], xs[:, t, :].rearrange("p a d -> p (a d)"),
                                    mv[:, t, 0:1].rearrange("p a s -> p (a s)"), rstd[:, 3, t],
                                    ALU.subtract, ALU.mult).then_inc(S[f"xn_ready_{which}"], 1)

            def keep_transposed(i, u):
                dve.wait_ge(S["xnT_copied_b"], T5 + i * T5 + (u + 1))
                V.tensor_copy(xT[:, :, ds((i * T5 + u) * P, P)], xnT[:, u, :, :]).then_inc(S["xT_done"], 1)

            def inverse_deviation(r, variance, which):
                steps.done(V.tensor_scalar(r[:, 0, :], variance, LN_EPS, None, ALU.add))
                dve.nop().then_inc(S[f"var_{which}"], 1)
                dve.wait_ge(S[f"std_{which}"], 1)
                steps.done(V.reciprocal(r[:, 2, :], r[:, 1, :]))
                steps.done(V.tensor_tensor(r[:, 3, :], r[:, 2, :], r[:, 2, :], ALU.mult))
                steps.done(V.tensor_tensor(r[:, 3, :], r[:, 3, :], r[:, 0, :], ALU.mult))
                steps.done(V.tensor_scalar(r[:, 3, :], r[:, 3, :], -0.5, 1.5, ALU.mult, ALU.add))
                steps.done(V.tensor_tensor(r[:, 3, :], r[:, 3, :], r[:, 2, :], ALU.mult))

            dve.wait_ge(S["ld_keys"], 32)
            steps.done(V.tensor_single_scalar(key_tile, key2[:, :], 7, ALU.logical_shift_right))
            steps.done(V.tensor_single_scalar(key2[:, :], key2[:, :], P - 1, ALU.bitwise_and))
            dve.wait_ge(S["ld_x"], 32)
            statistics("a")
            with dve.Fori(0, NT // T5) as i:
                steps.enter(i, 2 * T5)
                for u in range(T5):
                    steps.mark(V.tensor_scalar(ind5[:, u, :], tile1, iota_k[:, ds(i * T5 + u, 1)], None, ALU.is_equal))
                apply_turn(i, "a", False)
                steps.wait()
                for u in range(T5):
                    steps.mark(V.tensor_tensor_scan(cum1[:, ds(i * T5 + u, 1), :].rearrange("p a c -> p (a c)"),
                                                    ones[:, 0:1].to_broadcast([P, C1]), ind5[:, u, :], 0.0, ALU.mult, ALU.add))
                steps.wait()
                steps.leave(NT // T5)
            ends = cum1.rearrange("p b (g c) -> p b g c", c=G)[:, :, :, G - 1]
            steps.mark(V.tensor_copy(cnt[0][:, :, 0:1], ends[:, :, 0:1]))
            steps.done(V.tensor_tensor(cnt[0][:, :, 1:NG], ends[:, :, 1:NG], ends[:, :, 0:NG - 1], ALU.subtract))
            dve.nop().then_inc(S["counts_ready"], 1)
            dve.wait_ge(S["counts_mm"], 1)
            flat = [c[:, :, :].rearrange("p b g -> p (b g)") for c in cnt]
            steps.mark(V.tensor_copy(flat[5], bank[1][:, 0:NT * NG]))
            steps.wait()
            steps.done(V.tensor_tensor_scan(flat[1], first_g[:, :, :].rearrange("p b g -> p (b g)"), flat[5],
                                            0.0, ALU.mult, ALU.add))
            total, number, last_, end_, first_ = (bucket[:, i, :] for i in range(5))
            steps.done(V.tensor_scalar(total, cnt[1][:, :, NG - 1], float(P - 1), None, ALU.add))
            steps.done(V.tensor_copy(bucket_i[:, :], total))
            steps.done(V.tensor_single_scalar(bucket_i[:, :], bucket_i[:, :], 7, ALU.logical_shift_right))
            steps.done(V.tensor_copy(number, bucket_i[:, :]))
            steps.done(V.tensor_tensor_scan(end_, ones[:, 0:NT], number, 0.0, ALU.mult, ALU.add))
            dve.nop().then_inc(S["ends_ready"], 1)
            steps.done(V.tensor_tensor(first_, end_, number, ALU.subtract))
            steps.done(V.scalar_tensor_tensor(cnt[1][:, :, :], first_.unsqueeze(2).to_broadcast([P, NT, NG]), float(P),
                                              cnt[1][:, :, :], ALU.mult, ALU.add))
            steps.done(V.tensor_tensor(flat[2], flat[1], flat[5], ALU.subtract))
            steps.done(V.tensor_copy(cnt_i[:, :, :], cnt[2][:, :, :]))
            steps.done(V.tensor_single_scalar(cnt_i[:, :, :], cnt_i[:, :, :], 7, ALU.logical_shift_right))
            steps.done(V.tensor_copy(cnt[3][:, :, :], cnt_i[:, :, :]))
            steps.done(V.tensor_scalar(flat[4], flat[1], float(P - 1), None, ALU.add))
            steps.done(V.tensor_copy(cnt_i[:, :, :], cnt[4][:, :, :]))
            steps.done(V.tensor_single_scalar(cnt_i[:, :, :], cnt_i[:, :, :], 7, ALU.logical_shift_right))
            steps.done(V.tensor_copy(cnt[4][:, :, :], cnt_i[:, :, :]))
            steps.done(V.tensor_tensor(by_g[0][:, :, :].rearrange("p g b -> p b g"), cnt[4][:, :, :], cnt[3][:, :, :], ALU.subtract))
            for g in range(NG):
                steps.mark(V.tensor_tensor_scan(by_g[1][:, g, :], ones[:, 0:NT], by_g[0][:, g, :], 0.0, ALU.mult, ALU.add))
            steps.wait()
            steps.done(V.tensor_tensor(by_g[0][:, :, :], by_g[1][:, :, :], by_g[0][:, :, :], ALU.subtract))
            steps.done(V.tensor_tensor(cnt[4][:, :, :], by_g[0][:, :, :].rearrange("p g b -> p b g"), cnt[3][:, :, :], ALU.subtract))
            steps.done(V.scalar_tensor_tensor(flat[5], flat[4], float(P), flat[2], ALU.mult, ALU.add))
            steps.done(V.tensor_tensor(flat[5], flat[5], bank[0][:, 0:NT * NG], ALU.add))
            steps.done(V.tensor_scalar(flat[5], flat[5], 1.0, None, ALU.subtract))
            steps.done(V.tensor_tensor(cnt[5][:, :, 1:NG], cnt[5][:, :, 1:NG], ends[:, :, 0:NG - 1], ALU.subtract))
            span = by_g[2][:, :, :]
            steps.done(V.tensor_scalar(span, by_g[1][:, :, :], iota_p[:, 0:1], None, ALU.is_le))
            steps.done(V.tensor_scalar(by_g[1][:, :, :], by_g[0][:, :, :], iota_p[:, 0:1], None, ALU.is_le))
            steps.done(V.tensor_tensor(span, by_g[1][:, :, :], span, ALU.subtract))
            steps.done(V.tensor_reduce(global_chunk[:, 0, :], span, AX, ALU.add))
            steps.done(V.tensor_tensor(span, span, cnt[4][:, :, :].rearrange("p b g -> p g b"), ALU.mult))
            steps.done(V.tensor_reduce(global_chunk[:, 1, :], span, AX, ALU.add))
            steps.done(V.tensor_scalar(global_chunk[:, 0, :], global_chunk[:, 0, :], -NO_CHUNK, NO_CHUNK, ALU.mult, ALU.add))
            steps.done(V.tensor_tensor(global_chunk[:, 0, :], global_chunk[:, 0, :], global_chunk[:, 1, :], ALU.subtract))
            steps.done(V.tensor_scalar(global_chunk[:, 2, :], global_chunk[:, 0, :], iota_p[:, 0:1], None, ALU.add))
            dve.wait_ge(S["ends_mm"], 1)
            steps.done(V.tensor_copy(end_col[:, :], bank[2][0:NT, 0:1]))
            V.tensor_scalar(geq, iota_k[0:NT, :], end_col[:, 0:1], None, ALU.is_ge).then_inc(S["geq_ready"], 1)
            dve.wait_ge(S["geq_mm"], 1)
            steps.done(V.tensor_scalar(tile_of_chunk[:, :], bank[3][0:1, 0:K1], float(NT - 1), None, ALU.min))
            with dve.Fori(0, NT // T5) as i:
                steps.enter(i, T5)
                dve.wait_ge(S["in_ready"], i * T5 + 1)
                for u in range(T5):
                    b = ds(i * T5 + u, 1)
                    steps.mark(V.tensor_tensor(at5[:, u, :].rearrange("p (g c) -> p g c", c=G),
                                               cum1[:, b, :].rearrange("p a (g c) -> p (a g) c", c=G),
                                               cnt[5][:, b, :].rearrange("p a g -> p (a g)").unsqueeze(2).to_broadcast([P, NG, G]),
                                               ALU.add))
                steps.wait()
                for u in range(T5):
                    dve.wait_ge(S["place_added"], i * T5 + (u + 1))
                    V.scalar_tensor_tensor(in5[:, u, :], tile1, iota_k[:, ds(i * T5 + u, 1)], at5[:, u, :],
                                           ALU.is_equal, ALU.mult).then_inc(S["in_ready"], 1)
                steps.leave(NT // T5)
            dve.wait_ge(S["in_ready"], 1 + NT)
            for v, pad in ((lo2, -1.0), (hi2, -1.0), (keyc2[:, :], 0.0)):
                steps.mark(V.memset(v[:, C2:C2T], pad))
            steps.mark(V.tensor_copy(lo2[:, 0:C2], key2[:, :]))
            steps.done(V.tensor_copy(hi2[:, 0:C2], key_tile))
            steps.done(V.tensor_scalar(keyc2[:, 0:C2], hi2[:, 0:C2], float(P), MIDDLE, ALU.mult, ALU.subtract))
            steps.done(V.tensor_tensor(keyc2[:, 0:C2], keyc2[:, 0:C2], lo2[:, 0:C2], ALU.add))
            dve.nop().then_inc(S["keys_ready"], 1)
            dve.wait_ge(S["place_added"], T5 + NT)
            steps.done(V.tensor_copy(tmp1, place1))
            steps.done(V.tensor_single_scalar(src1, tmp1, P - 1, ALU.bitwise_and))
            steps.mark(V.tensor_copy(lane1, src1))
            steps.done(V.tensor_single_scalar(tmp1, tmp1, 7, ALU.logical_shift_right))
            steps.mark(V.tensor_copy(chunk1, tmp1))
            steps.wait()
            dve.nop().then_inc(S["ranks_done"], 1)

            def hots_turn(g, side):
                for half in range(2):
                    dve.wait_ge(S["hots_used"], g * 2 + (half + 1))
                    col = ds(g * G + half * HALF, HALF)
                    bc = lambda v, n: v.unsqueeze(2).to_broadcast([P, HALF, n])
                    steps.mark(V.tensor_tensor(ochunk[:, half, :, :], iota16[:, 0:L].unsqueeze(1).to_broadcast([P, HALF, L]),
                                               bc(chunk1[:, col], L), ALU.is_equal))
                    made = 0 if half else POOL_LANES
                    n = HALF - made
                    V.tensor_tensor(olane1[:, half, made:HALF, :], iota16[:, 0:P].unsqueeze(1).to_broadcast([P, n, P]),
                                    lane1[:, ds(g * G + half * HALF + made, n)].unsqueeze(2).to_broadcast([P, n, P]), ALU.is_equal)
                    steps.wait()
                    view = pay_oh[:, half, :, :].rearrange("p c (v l) -> p c v l", v=2)
                    for v in range(2):
                        last = V.tensor_tensor(view[:, :, v, :], ochunk[:, half, :, :], bc(payload[:, v, col], L), ALU.mult)
                    last.then_inc(S["hots_ready"], 1)
                dve.wait_ge(S["moved_mm"], g + 1)
                V.tensor_scalar(ogc[:, side, :], iota_k[0:L, :], global_chunk[0:L, 2, ds(g, 1)], None,
                                ALU.is_equal).then_inc(S["ogc_ready"], 1)
                V.tensor_tensor(OH[:, ds(g * CG, CG), :], iota16[:, 0:NT].unsqueeze(1).to_broadcast([P, CG, NT]),
                                hi2[:, ds(g * CG, CG)].unsqueeze(2).to_broadcast([P, CG, NT]), ALU.is_equal).then_inc(S["tile_hots_ready"], 1)

            with dve.Fori(0, NG // 2) as i:
                steps.enter(i, 4)
                for side in range(2):
                    hots_turn(i * 2 + side, side)
                steps.leave(NG // 2)
            dve.wait_ge(S["moved_mm"], 2 + NG)
            steps.mark(V.tensor_copy(w_s, bank[6][:, 0:K1]))
            steps.done(V.tensor_copy(pack_i, bank[7][:, 0:K1]))
            steps.mark(V.tensor_single_scalar(idx_s, pack_i, 7, ALU.logical_shift_right))
            steps.done(V.tensor_single_scalar(pack_i, pack_i, P - 1, ALU.bitwise_and))
            steps.done(V.tensor_copy(loc_s, pack_i))
            dve.nop().then_inc(S["edges_ready"], 1)

            def dest_hots(turn, u):
                c = ds(turn * U + u, 1)
                V.tensor_scalar(S1[:, u, :], iota_k[:, 0:P], loc_s[:, c], w_s[:, c], ALU.is_equal, ALU.mult).then_inc(S["onehot_ready"], 1)

            def tiles_of(turn):
                return nc.values_load_multi_w_load_instructions(
                    tile_of_chunk[0:1, ds(turn * U, U)], engines=[mybir.EngineType.DVE], min_val=0, max_val=NT - 1,
                    skip_runtime_bounds_check_because="a count of buckets, of which the smaller of it and NT - 1 was taken")[1]

            def sum_chunk(turn, tiles, u, made=U):
                dve.wait_ge(S["slots_free"], U + turn * U + (u + 1))
                dve.wait_ge(S["agg_free"], AGG + turn * U + u)
                acc = xs[:, ds(tiles[u], 1), :].rearrange("p a d -> p (a d)")
                V.tensor_tensor(acc, acc, agg_bank(u), ALU.add).then_inc(S["agg_free"], 1)
                if u < made:
                    dest_hots(turn + 1, u)

            for u in range(U):
                dest_hots(0, u)
            tot2, base2 = bucket[:, 0, :], bucket[:, 1, :]
            dve.wait_ge(S["cnt_copied"], NG + 1)
            tiles = tiles_of(0)
            dve.wait_ge(S["bias_added"], 1)
            for u in range(U):
                sum_chunk(0, tiles, u)
            dve.wait_ge(S["base2_mm"], 1)
            steps.done(V.tensor_copy(bucket[:, 2, :], bank[3][:, 0:NT]))
            steps.done(V.tensor_tensor_scan(bucket[:, 3, :], ones[:, 0:NT], bucket[:, 2, :], 0.0, ALU.mult, ALU.add))
            steps.done(V.tensor_tensor(base2, bucket[:, 3, :], bucket[:, 2, :], ALU.subtract))
            steps.done(V.tensor_tensor(base2, base2, bank[2][:, 0:NT], ALU.add))
            steps.done(V.tensor_tensor(bucket[:, 4, :], base2, tot2, ALU.add))
            steps.done(V.tensor_scalar(endpos[:, :], bucket[:, 4, :], 1.0, None, ALU.subtract))
            steps.mark(V.tensor_copy(PT[:, 0, :], base2))
            for turn in range(1, COUNT_TURNS):
                tiles = tiles_of(turn)
                for u in range(U):
                    sum_chunk(turn, tiles, u, DU if turn + 1 == RANK_0 else U)
                    for t in range((turn - 1) * U + u, NT, (COUNT_TURNS - 1) * U):
                        steps.mark(V.tensor_tensor_scan(PT[:, 1:C2T + 1, t], ones[:, 0:1].to_broadcast([P, C2T]), CT[:, :, t],
                                                        bucket[:, 1, t:t + 1], ALU.mult, ALU.add))
            steps.wait()

            dve.nop().then_inc(S["places_ready"], 1)

            def rank_turn(i, side):
                k = i * 2 + side
                tiles = tiles_of(k + RANK_0)
                dve.wait_ge(rows_landed[side], i * 16 + 16)
                for u in range(U):
                    sum_chunk(k + RANK_0, tiles, u, DU)
                    for c in range(2 * u, min(2 * u + 2, U2)):
                        last = V.scalar_tensor_tensor(same[:, c, :], rows2[:, side, c, 1, :], keyc2[:, ds(k * U2 + c, 1)], tri16[:, :],
                                                      ALU.is_equal, ALU.mult, accum_out=rank2[:, ds(k * U2 + c, 1)])
                        if c == U2 - 1:
                            last.then_inc(S["ranked"], 1)
                dve.wait_ge(S["r_mm"], k + 3)
                steps.done(V.tensor_tensor(rsel, bank[6 + side][:, 0:U2 * NT].rearrange("p (u t) -> p u t", u=U2),
                                           OH[:, ds(k * U2, U2), :], ALU.mult))
                V.tensor_reduce(pos2[:, ds(k * U2, U2)], rsel, AX, ALU.add).then_inc(S["r_used"], 1)

            with dve.Fori(0, T2 // 2) as i:
                steps.enter(i, 2)
                for side in range(2):
                    rank_turn(i, side)
                steps.leave(T2 // 2)
            dve.wait_ge(S["r_used"], T2 + 2)
            dve.wait_ge(S["ranked"], T2)
            steps.done(V.tensor_tensor(pos2, pos2, rank2[:, :], ALU.add))
            main = slice(0, C2T)
            steps.done(V.tensor_scalar(tmp2, pos2, 1.0 / C2, 0.5 / C2 - 0.5, ALU.mult, ALU.add))
            steps.done(V.tensor_copy(tmp2i, tmp2))
            steps.done(V.tensor_copy(lane2[:, main], tmp2i))
            steps.done(V.scalar_tensor_tensor(col2[:, main], lane2[:, main], -float(C2), pos2, ALU.mult, ALU.add))
            for test, bound, sign in ((ALU.is_lt, 0.0, 1.0), (ALU.is_ge, float(C2), -1.0)):
                steps.done(V.tensor_scalar(tmp2, col2[:, main], bound, None, test))
                steps.mark(V.scalar_tensor_tensor(lane2[:, main], tmp2, -sign, lane2[:, main], ALU.mult, ALU.add))
                steps.done(V.scalar_tensor_tensor(col2[:, main], tmp2, sign * C2, col2[:, main], ALU.mult, ALU.add))
            again = slice(C2T, C2T + LOOPS * U2)
            steps.mark(V.tensor_copy(lane2[:, again], lane2[:, 0:LOOPS * U2]))
            steps.mark(V.tensor_copy(col2[:, again], col2[:, 0:LOOPS * U2]))
            steps.mark(V.memset(src_sorted[:, :], 0))
            tiles = tiles_of(PLACE_TURN)
            for u in range(U):
                sum_chunk(PLACE_TURN, tiles, u)
            steps.wait()
            dve.nop().then_inc(S["lanes_ready"], 1)

            def move_hots(k, q):
                dve.wait_ge(S["perm_used"], k * SUBS + (q + 1))
                for u in range(q * SUB, (q + 1) * SUB):
                    last = V.tensor_scalar(ocol[:, u, :], iota16[:, 0:C2], col2[:, ds(k * U2 + u, 1)], None, ALU.is_equal)
                last.then_inc(S["perm_ready"], 1)

            def move_turn(k, made=U):
                tiles = tiles_of(k + MOVE_0)
                for u in range(U):
                    sum_chunk(k + MOVE_0, tiles, u, made)
                    if u in (0, 2, 4):
                        move_hots(k, u // 2)

            with dve.Fori(0, T2 + LOOPS - 1) as i:
                move_turn(i)
            move_turn(T2 + LOOPS - 1, 0)
            dve.wait_ge(S["agg_free"], AGG + K1)
            dve.wait_ge(S["perm_mm"], 1)
            steps.mark(V.tensor_copy(starts[:, :], bank[3][:, 0:C2]))
            steps.done(V.tensor_scalar(src_sorted[:, 0:C2], bank[2][:, 0:C2], MIDDLE, None, ALU.add))
            dve.nop().then_inc(S["perm_taken"], 1)

            statistics("b")
            apply_turn(0, "b", False)
            with dve.Fori(1, NT // T5) as i:
                apply_turn(i, "b", True)
            for u in range(T5):
                keep_transposed(NT // T5 - 1, u)
            dve.wait_ge(S["proj_taken_b"], NT + 2)
            for a in range(2):
                steps.done(V.tensor_tensor(agg[:, :, :], GT[:, 0:NT, 0:CH], att_b[:, a, :].unsqueeze(1).to_broadcast([P, NT, CH]), ALU.mult))
                steps.done(V.tensor_reduce(GT[:, 0:NT, CH + a * HEADS:CH + (a + 1) * HEADS],
                                           agg[:, :, :].rearrange("p t (h e) -> p t h e", e=EX), AX, ALU.add))
            dve.nop().then_inc(S["table_ready"], 1)

            dve.wait_ge(S["table_sent"], 16)
            with dve.Fori(0, C2G // SLOTS) as i:
                for u in range(SLOTS):
                    dve.wait_ge(gat_in[u], i * 16 + 16)
                    V.tensor_copy(GT[:, ds(i * SLOTS + u, 1), :].rearrange("p a r -> p (a r)"), gat_slot[:, u, :]).then_inc(S["gat_free"], 1)
            dve.wait_ge(S["gat_free"], SLOTS + C2G)
            steps.mark(V.tensor_scalar(keep, starts[:, :], -1.0, 1.0, ALU.mult, ALU.add))
            steps.mark(V.tensor_scalar(drop_f, starts[:, :], -BIG, None, ALU.mult))
            steps.mark(V.tensor_scalar(drop_r[:, 0:C2 - 1], starts[:, 1:C2], -BIG, None, ALU.mult))
            steps.mark(V.memset(drop_r[:, C2 - 1:C2], 0.0))
            steps.done(V.tensor_reduce(flag_any[:, 0:1], starts[:, :], AX, ALU.max))
            steps.mark(V.tensor_scalar(flag_any[:, 1:2], flag_any[:, 0:1], -1.0, 1.0, ALU.mult, ALU.add))
            steps.done(V.tensor_scalar(flag_any[:, 2:3], flag_any[:, 0:1], -BIG, None, ALU.mult))
            steps.done(V.memset(across[:, 2, :], 0.0))

            turns = [0]

            def over_partitions(k, last_cols, flag, op0, op1, nothing, reverse):
                q = turns[0]
                turns[0] += 1
                steps.mark(V.tensor_copy(edge_cols[:, 0, 0:k], last_cols))
                steps.done(V.tensor_copy(edge_cols[:, 1, 0:k], flag_any[:, flag:flag + 1].to_broadcast([P, k])))
                dve.nop().then_inc(S["cols_ready"], 1)
                dve.wait_ge(S["cols_T"], q + 1)
                steps.mark(V.tensor_copy(across[0:k, 0, 0:P], bank[6][0:k, 0:P]))
                steps.mark(V.tensor_copy(across[0:k, 1, 0:P], bank[6][0:k, P:2 * P]))
                edge = P if reverse else 0
                steps.done(V.memset(across[0:k, 2, edge:edge + 1], nothing))
                o = across[0:k, 2, 0:P][:, ::-1] if reverse else across[0:k, 2, 1:P + 1]
                l, f = across[0:k, 0, 0:P], across[0:k, 1, 0:P]
                if reverse:
                    l, f = l[:, ::-1], f[:, ::-1]
                steps.done(V.tensor_tensor_scan(o, f, l, nothing, op0, op1))
                dve.nop().then_inc(S["across_ready"], 1)
                dve.wait_ge(S["across_T"], q + 1)
                steps.done(V.tensor_copy(carry[:, 0, 0:k], bank[7][:, 0:k]))
                dve.nop().then_inc(S["carried"], 1)

            steps.done(V.tensor_tensor(s_e, GT[:, 0:C2, CH + HEADS:ROW].rearrange("p c h -> p h c"),
                                       starts[:, :].unsqueeze(1).to_broadcast([P, HEADS, C2]), ALU.mult))

            def spread(initial):
                for h in range(HEADS):
                    steps.mark(V.tensor_tensor_scan(ad_e[:, h, :], keep, s_e[:, h, :], initial(h), ALU.mult, ALU.add))
                steps.wait()

            spread(lambda h: 0.0)
            over_partitions(HEADS, ad_e[:, :, C2 - 1], 1, ALU.mult, ALU.add, 0.0, False)
            spread(lambda h: carry[:, 0, h:h + 1])
            steps.done(V.tensor_tensor(e_e, GT[:, 0:C2, CH:CH + HEADS].rearrange("p c h -> p h c"), ad_e, ALU.add))
            flat_e = e_e.rearrange("p h c -> p (h c)")
            steps.done(V.scalar_tensor_tensor(flat_e, flat_e, 0.2, flat_e, ALU.mult, ALU.max))

            def scan_max(o, flags, initial, reverse):
                for h in range(HEADS):
                    a, b, c = o[:, h, :], flags, e_e[:, h, :]
                    if reverse:
                        a, b, c = a[:, ::-1], b[:, ::-1], c[:, ::-1]
                    steps.mark(V.tensor_tensor_scan(a, b, c, initial(h), ALU.add, ALU.max))
                steps.wait()

            scan_max(f_e, drop_f, lambda h: -BIG, False)
            over_partitions(HEADS, f_e[:, :, C2 - 1], 2, ALU.add, ALU.max, -BIG, False)
            scan_max(f_e, drop_f, lambda h: carry[:, 0, h:h + 1], False)
            scan_max(s_e, drop_r, lambda h: -BIG, True)
            steps.done(V.tensor_scalar(carry[:, 1, 0:HEADS], s_e[:, :, 0], drop_f[:, 0:1], None, ALU.add))
            over_partitions(HEADS, carry[:, 1, 0:HEADS], 2, ALU.add, ALU.max, -BIG, True)
            scan_max(s_e, drop_r, lambda h: carry[:, 0, h:h + 1], True)
            flat_f, flat_s = f_e.rearrange("p h c -> p (h c)"), s_e.rearrange("p h c -> p (h c)")
            steps.done(V.tensor_tensor(flat_f, flat_f, flat_s, ALU.max))
            steps.done(V.tensor_tensor(flat_e, flat_e, flat_f, ALU.subtract))
            dve.nop().then_inc(S["exp_in"], 1)
            dve.wait_ge(S["exp_out"], 1)
            for h in range(HEADS):
                rows = GT[:, 0:C2, h * EX:(h + 1) * EX]
                steps.mark(V.tensor_tensor(rows, rows, e_e[:, h, :].unsqueeze(2).to_broadcast([P, C2, EX]), ALU.mult))
            steps.mark(V.tensor_copy(GT[:, 0:C2, CH:NS].rearrange("p c h -> p h c"), e_e))
            steps.wait()
            for first in range(0, NS, SCANS):
                n = min(SCANS, NS - first)
                for j in range(n):
                    steps.mark(V.tensor_tensor_scan(sums_part[:, j, :], keep, GT[:, 0:C2, first + j], 0.0, ALU.mult, ALU.add))
                steps.wait()
                steps.done(V.tensor_copy(carry[:, 1, first:first + n], sums_part[:, 0:n, C2 - 1]))
            over_partitions(NS, carry[:, 1, 0:NS], 1, ALU.mult, ALU.add, 0.0, False)
            for j in range(NS):
                steps.mark(V.tensor_tensor_scan(GT[:, 0:C2, j], keep, GT[:, 0:C2, j], carry[:, 0, j:j + 1], ALU.mult, ALU.add))
            steps.wait()
            dve.nop().then_inc(S["sums_ready"], 1)
            dve.wait_ge(sums_in, 16 * NT)
            den = node_sums[:, :, CH:NS]
            steps.done(V.tensor_scalar(den, den, 1e-16, None, ALU.add))
            steps.done(V.reciprocal(den, den))
            steps.done(V.tensor_tensor(agg[:, :, :].rearrange("p t (h e) -> p t h e", e=EX),
                                       node_sums[:, :, 0:CH].rearrange("p t (h e) -> p t h e", e=EX),
                                       den.unsqueeze(3).to_broadcast([P, NT, HEADS, EX]), ALU.mult))

            def row(i):
                return gam_b[:, i, :].unsqueeze(1).to_broadcast([P, NT, CH])

            def node(v):
                return v.unsqueeze(2).to_broadcast([P, NT, CH])

            steps.done(V.tensor_tensor(agg[:, :, :], agg[:, :, :], row(2), ALU.add))
            steps.done(V.tensor_reduce(pair[:, 4, :], agg[:, :, :], AX, ALU.add))
            steps.done(V.tensor_scalar(pair[:, 4, :], pair[:, 4, :], 1.0 / CH, None, ALU.mult))
            steps.done(V.tensor_tensor(agg[:, :, :], agg[:, :, :], node(pair[:, 4, :]), ALU.subtract))
            steps.done(V.tensor_tensor(agg2[:, :, :], agg[:, :, :], agg[:, :, :], ALU.mult))
            steps.done(V.tensor_reduce(pair[:, 5, :], agg2[:, :, :], AX, ALU.add))
            steps.done(V.tensor_scalar(pair[:, 5, :], pair[:, 5, :], 1.0 / CH, None, ALU.mult))
            inverse_deviation(pair, pair[:, 5, :], "c")
            steps.done(V.tensor_tensor(agg[:, :, :], agg[:, :, :], node(pair[:, 3, :]), ALU.mult))
            steps.done(V.tensor_tensor(agg[:, :, :], agg[:, :, :], row(0), ALU.mult))
            steps.done(V.tensor_tensor(agg[:, :, :], agg[:, :, :], row(1), ALU.add))
            steps.done(V.tensor_reduce(sc4[:, :, :].rearrange("p e t -> p t e"),
                                       agg[:, :, :].rearrange("p t (h e) -> p t e h", e=EX), AX, ALU.add))
            flat4 = sc4[:, :, :].rearrange("p e t -> p (e t)")
            steps.done(V.tensor_scalar(flat4, flat4, 1.0 / HEADS, None, ALU.mult))
            steps.done(V.memset(rank4[:, :, :], 0.0))
            for a in range(EX):
                for b in range(a + 1, EX):
                    steps.done(V.tensor_tensor(pair[:, 0, :], sc4[:, a, :], sc4[:, b, :], ALU.is_ge))
                    steps.mark(V.tensor_tensor(rank4[:, b, :], rank4[:, b, :], pair[:, 0, :], ALU.add))
                    steps.mark(V.scalar_tensor_tensor(rank4[:, a, :], rank4[:, a, :], 1.0, pair[:, 0, :], ALU.add, ALU.subtract))
                    steps.wait()
            flat_r = rank4[:, :, :].rearrange("p e t -> p (e t)")
            steps.done(V.tensor_scalar(flat_r, flat_r, 2.0, None, ALU.is_lt))
            steps.done(V.tensor_reduce(pair[:, 1, :], sc4[:, :, :].rearrange("p e t -> p t e"), AX, ALU.max))
            steps.done(V.tensor_tensor(gate[:, :, :], sc4[:, :, :], pair[:, 1, :].unsqueeze(1).to_broadcast([P, EX, NT]), ALU.subtract))
            dve.nop().then_inc(S["wexp_in"], 1)
            dve.wait_ge(S["wexp_out"], 1)
            steps.done(V.tensor_tensor(gate[:, :, :], gate[:, :, :], rank4[:, :, :], ALU.mult))
            steps.done(V.tensor_reduce(pair[:, 2, :], gate[:, :, :].rearrange("p e t -> p t e"), AX, ALU.add))
            steps.done(V.reciprocal(pair[:, 3, :], pair[:, 2, :]))
            steps.done(V.tensor_tensor(gate[:, :, :], gate[:, :, :], pair[:, 3, :].unsqueeze(1).to_broadcast([P, EX, NT]), ALU.mult))
            dve.nop().then_inc(S["gate_ready"], 1)

            def add_pair(tiles):
                for t in tiles:
                    dve.wait_ge(S["gb_mm"], t + 1)
                    V.tensor_tensor(xs[:, t, :], xs[:, t, :], bank[(0, 1, 4, 5)[t % 4]][:, 0:D], ALU.add).then_inc(S["gb_used"], 1)
                    dve.wait_ge(S["gb_used"], t + 1)
                    dve.nop().then_inc(S["out_ready"], 1)

            pairs = [range(t, min(t + 2, NT)) for t in range(0, NT, 2)]
            for n, tiles in enumerate(pairs):
                for e in range(EX - 2):
                    for t in tiles:
                        dve.wait_ge(y_loaded[t % YS], 16 * (t // YS + 1))
                        steps.mark(V.scalar_tensor_tensor(xs[:, t, :], y_in[t % YS][:, e, :], gate[:, e, t:t + 1], xs[:, t, :],
                                                          ALU.mult, ALU.add))
                        if len(tiles) == 2:
                            steps.wait_but_last()
                        else:
                            steps.wait()
                steps.wait()
                if n:
                    add_pair(pairs[n - 1])
            add_pair(pairs[-1])


_NAMES = ["x", "src", "dst", "edge_weight", "L0_gnn_W", "L0_gnn_bias", "L0_ffn_W_gat", "L0_ffn_att_src", "L0_ffn_att_dst",
          "L0_ffn_b_gat", "L0_ffn_ln_gamma", "L0_ffn_ln_beta", "L0_ffn_W1", "L0_ffn_b1", "L0_ffn_W2", "L0_ffn_b2",
          "L0_ffn_edge_index"]


def kernel(**inputs):
    import numpy as _np
    import concourse.bacc as _bacc
    from concourse import mybir as _mybir
    from concourse.bass_utils import run_bass_kernel_spmd as _run

    nc = _bacc.Bacc("TRN2", target_bir_lowering=False, num_devices=1)
    arrays, args = {}, []
    for name in _NAMES:
        a = _np.ascontiguousarray(inputs[name])
        arrays[f"in_{name}"] = a
        args.append(nc.dram_tensor(f"in_{name}", a.shape, _mybir.dt.from_np(a.dtype), kind="ExternalInput").ap())
    shape = inputs["x"].shape
    args.append(nc.dram_tensor("out_rows", shape, _mybir.dt.float32, kind="ExternalOutput").ap())
    gnn_moe_kernel(nc, *args)
    return _run(nc, [arrays], core_ids=[0]).results[0]["out_rows"]
```
